# Optimizing a Trainium2 kernel written in Bass

```python
import numpy as np
import jax
import jax.numpy as jnp

def _softmax(x, axis=-1):
    return jax.nn.softmax(x, axis=axis)

def _gelu(x):
    return jax.nn.gelu(x, approximate=True)

def _silu(x):
    return jax.nn.silu(x)

def _sigmoid(x):
    return jax.nn.sigmoid(x)

def _layernorm(x, axis=-1, eps=1e-05):
    m = jnp.mean(x, axis=axis, keepdims=True)
    v = jnp.var(x, axis=axis, keepdims=True)
    return (x - m) / jnp.sqrt(v + eps)

def _scatter_add(tgt, idx, src, axis=0):
    return tgt.at[idx].add(src)

def _segment_sum(src, seg, n):
    return jax.ops.segment_sum(src, seg, n)
kernel_name = 'mk_decoder_preln_d1_seqx_r4_5631dc'

def setup_inputs(seed: int=0):
    np.random.seed(seed)
    _w = jnp.asarray

    def _rec_inputs():
        import jax
        import jax.numpy as jnp
        _rk = jax.random.key(seed)
        x = -0.0002928 + 1 * jax.random.normal(jax.random.fold_in(_rk, 1), (2, 1024, 256), jnp.float32)
        _lenS = 1024 - jax.random.randint(jax.random.fold_in(_rk, 7), (2,), 0, max(1, 1024 // 4) + 1, jnp.int32)
        _lenS2 = 77 - jax.random.randint(jax.random.fold_in(_rk, 8), (2,), 0, max(1, 77 // 4) + 1, jnp.int32)
        _ctx_1024P = jax.random.normal(jax.random.fold_in(_rk, 11), (2, 16, 256), jnp.float32)
        _ctx_1024c = jax.random.dirichlet(jax.random.fold_in(_rk, 511), 0.3 * jnp.ones((16,), jnp.float32), (2, 77))
        _ctx_1024t = jnp.einsum('bsk,bkd->bsd', _ctx_1024c, _ctx_1024P)
        _ctx_1024t = _ctx_1024t * jax.lax.rsqrt(jnp.mean(jnp.square(_ctx_1024t)) + 1e-12) * 0.953939
        ctx_1024 = -1.39393e-06 + 0.999914 * (_ctx_1024t + 0.3 * jax.random.normal(jax.random.fold_in(_rk, 611), (2, 77, 256), jnp.float32))
        _validS = jnp.arange(1024)[None, :] < _lenS[:, None]
        _validS2 = jnp.arange(77)[None, :] < _lenS2[:, None]
        _causal = jnp.tril(jnp.ones((1024, 1024), dtype=bool))
        mask_BxSxS2_ik1 = jnp.where(jnp.broadcast_to(_validS2[:, None, :], (2, 1024, 77)), 1, 0).astype(jnp.int32)
        return (x, ctx_1024, mask_BxSxS2_ik1)
    x, ctx_1024, mask_BxSxS2_ik1 = _rec_inputs()

    def _L0_attn_setup():
        import jax, jax.numpy as jnp
        import numpy as np
        B, S, E, H = (8, 256, 256, 16)
        EPS = 0.001
        key = jax.random.key(seed)
        ks = jax.random.split(key, 5)
        x = jax.random.normal(ks[0], (B, S, E), dtype=jnp.float32)
        Wq = jax.random.normal(ks[1], (E, E), dtype=jnp.float32) * 0.02
        Wk = jax.random.normal(ks[2], (E, E), dtype=jnp.float32) * 0.02
        Wv = jax.random.normal(ks[3], (E, E), dtype=jnp.float32) * 0.02
        rel_table = jax.random.normal(ks[4], (2 * S - 1, H), dtype=jnp.float32) * 0.02
        gamma = jnp.ones((E,), dtype=jnp.float32)
        beta = jnp.zeros((E,), dtype=jnp.float32)
        return {'x': x, 'Wq': Wq, 'Wk': Wk, 'Wv': Wv, 'rel_table': rel_table, 'gamma': gamma, 'beta': beta}
    _L0_attn_all = _L0_attn_setup()
    _L0_attn_in = {k: v for k, v in _L0_attn_all.items() if k in ('Wq', 'Wk', 'Wv', 'rel_table', 'gamma', 'beta')}
    del _L0_attn_all

    def _L0_xattn_setup():
        import jax, jax.numpy as jnp
        import numpy as np
        B, S, D, H = (2, 512, 256, 16)
        DK = D // H
        key = jax.random.key(seed)
        ks = jax.random.split(key, 9)
        query = jax.random.normal(ks[0], (B, S, D), dtype=jnp.float32)
        k_in = jax.random.normal(ks[1], (B, S, D), dtype=jnp.float32)
        v_in = jax.random.normal(ks[2], (B, S, D), dtype=jnp.float32)
        mask = jax.random.randint(ks[3], (B, S, S), 0, 2, dtype=jnp.int32)
        sc = 1.0 / np.sqrt(D)
        Wq = jax.random.normal(ks[4], (H, D, DK), dtype=jnp.float32) * sc
        Wk = jax.random.normal(ks[5], (H, D, DK), dtype=jnp.float32) * sc
        Wv = jax.random.normal(ks[6], (H, D, DK), dtype=jnp.float32) * sc
        Wu = jax.random.normal(ks[7], (D, D), dtype=jnp.float32) * sc
        bu = jax.random.normal(ks[8], (D,), dtype=jnp.float32) * 0.01
        return {'query': query, 'key': k_in, 'value': v_in, 'mask': mask, 'Wq': Wq, 'Wk': Wk, 'Wv': Wv, 'Wu': Wu, 'bu': bu}
    _L0_xattn_all = _L0_xattn_setup()
    _L0_xattn_in = {k: v for k, v in _L0_xattn_all.items() if k in ('Wq', 'Wk', 'Wv', 'Wu', 'bu')}
    del _L0_xattn_all

    def _L0_ffn_setup():
        import jax, jax.numpy as jnp
        import numpy as np
        B, S, D, E, H, DO = (4, 512, 256, 8, 1024, 256)
        TOP_K = 2
        LN_EPS = 1e-05
        key = jax.random.key(seed)
        ks = jax.random.split(key, 9)
        s = 0.02
        return {'x': jax.random.normal(ks[0], (B, S, D), dtype=jnp.float32), 'W1': jax.random.normal(ks[1], (E, D, H), dtype=jnp.float32) * s, 'b1': jnp.zeros((E, H), dtype=jnp.float32), 'W2': jax.random.normal(ks[2], (E, H, DO), dtype=jnp.float32) * s, 'b2': jnp.zeros((E, DO), dtype=jnp.float32), 'gate_W': jax.random.normal(ks[3], (D, E), dtype=jnp.float32) * s, 'shared_W': jax.random.normal(ks[4], (D, DO), dtype=jnp.float32) * s, 'shared_b': jnp.zeros((DO,), dtype=jnp.float32), 'gamma': jnp.ones((DO,), dtype=jnp.float32), 'beta': jnp.zeros((DO,), dtype=jnp.float32)}
    _L0_ffn_all = _L0_ffn_setup()
    _L0_ffn_in = {k: v for k, v in _L0_ffn_all.items() if k in ('W1', 'b1', 'W2', 'b2', 'gate_W', 'shared_W', 'shared_b', 'gamma', 'beta')}
    del _L0_ffn_all
    return {'x': x, 'ctx_1024': ctx_1024, 'mask_BxSxS2_ik1': mask_BxSxS2_ik1, 'L0_attn_Wq': _L0_attn_in['Wq'], 'L0_attn_Wk': _L0_attn_in['Wk'], 'L0_attn_Wv': _L0_attn_in['Wv'], 'L0_attn_rel_table': _L0_attn_in['rel_table'], 'L0_attn_gamma': _L0_attn_in['gamma'], 'L0_attn_beta': _L0_attn_in['beta'], 'L0_xattn_Wq': _L0_xattn_in['Wq'], 'L0_xattn_Wk': _L0_xattn_in['Wk'], 'L0_xattn_Wv': _L0_xattn_in['Wv'], 'L0_xattn_Wu': _L0_xattn_in['Wu'], 'L0_xattn_bu': _L0_xattn_in['bu'], 'L0_ffn_W1': _L0_ffn_in['W1'], 'L0_ffn_b1': _L0_ffn_in['b1'], 'L0_ffn_W2': _L0_ffn_in['W2'], 'L0_ffn_b2': _L0_ffn_in['b2'], 'L0_ffn_gate_W': _L0_ffn_in['gate_W'], 'L0_ffn_shared_W': _L0_ffn_in['shared_W'], 'L0_ffn_shared_b': _L0_ffn_in['shared_b'], 'L0_ffn_gamma': _L0_ffn_in['gamma'], 'L0_ffn_beta': _L0_ffn_in['beta']}

def reference(x, ctx_1024, mask_BxSxS2_ik1, L0_attn_Wq, L0_attn_Wk, L0_attn_Wv, L0_attn_rel_table, L0_attn_gamma, L0_attn_beta, L0_xattn_Wq, L0_xattn_Wk, L0_xattn_Wv, L0_xattn_Wu, L0_xattn_bu, L0_ffn_W1, L0_ffn_b1, L0_ffn_W2, L0_ffn_b2, L0_ffn_gate_W, L0_ffn_shared_W, L0_ffn_shared_b, L0_ffn_gamma, L0_ffn_beta):
    import jax
    import jax.numpy as jnp

    def _L0_attn_ref(x, Wq, Wk, Wv, rel_table, gamma, beta):
        import jax, jax.numpy as jnp
        import numpy as np
        B, S, E, H = (8, 256, 256, 16)
        EPS = 0.001
        b, s, e = x.shape
        h = rel_table.shape[1]
        scale = e ** (-0.5)

        def split_heads(t):
            return t.reshape(b, s, h, -1).transpose(0, 2, 1, 3)
        q = split_heads(x @ Wq)
        k = split_heads(x @ Wk)
        v = split_heads(x @ Wv)
        attn = jnp.einsum('bhqd,bhkd->bhqk', q, k) * scale
        attn = jax.nn.softmax(attn, axis=-1)
        r = jnp.arange(s)
        rel_index = jnp.clip(r[None, :] - r[:, None] + (s - 1), 0, 2 * s - 2)
        bias = rel_table[rel_index]
        bias = bias.reshape(-1).reshape(h, s, s)
        attn = attn + bias[None]
        out = jnp.einsum('bhqk,bhkd->bhqd', attn, v)
        out = out.transpose(0, 2, 1, 3).reshape(b, s, e)
        mu = jnp.mean(out, axis=-1, keepdims=True)
        var = jnp.var(out, axis=-1, keepdims=True)
        out = (out - mu) / jnp.sqrt(var + EPS) * gamma + beta
        return out

    def _L0_xattn_ref(query, key, value, mask, Wq, Wk, Wv, Wu, bu):
        import jax, jax.numpy as jnp
        import numpy as np
        B, S, D, H = (2, 512, 256, 16)
        DK = D // H
        scale = DK ** 0.25
        q = jnp.einsum('bsd,hdk->bhsk', query, Wq) / scale
        k = jnp.einsum('bsd,hdk->bhsk', key, Wk) / scale
        v = jnp.einsum('bsd,hdk->bhsk', value, Wv)
        scores = jnp.einsum('bhsk,bhtk->bhst', q, k)
        scores = jnp.where(mask[:, None, :, :] == 0, jnp.float32(-1000000000.0), scores)
        attn = jax.nn.softmax(scores, axis=-1)
        out = jnp.einsum('bhst,bhtk->bhsk', attn, v)
        out = jnp.transpose(out, (0, 2, 1, 3)).reshape(query.shape[0], query.shape[1], D)
        return out @ Wu + bu

    def _L0_ffn_ref(x, W1, b1, W2, b2, gate_W, shared_W, shared_b, gamma, beta):
        import jax, jax.numpy as jnp
        import numpy as np
        B, S, D, E, H, DO = (4, 512, 256, 8, 1024, 256)
        TOP_K = 2
        LN_EPS = 1e-05
        d = x.shape[-1]
        flat = x.reshape(-1, d)
        n_exp = gate_W.shape[-1]
        probs = jax.nn.softmax(flat @ gate_W, axis=-1)
        topk_w, topk_idx = jax.lax.top_k(probs, TOP_K)
        topk_w = topk_w / topk_w.sum(axis=-1, keepdims=True)
        combine = (jax.nn.one_hot(topk_idx, n_exp, dtype=flat.dtype) * topk_w[..., None]).sum(axis=1)
        out = 0.5 * jax.nn.gelu(flat @ shared_W + shared_b, approximate=False)
        for e in range(n_exp):
            h = jax.nn.gelu(flat @ W1[e] + b1[e], approximate=False)
            out = out + combine[:, e:e + 1] * (h @ W2[e] + b2[e])
        mean = out.mean(axis=-1, keepdims=True)
        var = ((out - mean) ** 2).mean(axis=-1, keepdims=True)
        out = (out - mean) * jax.lax.rsqrt(var + LN_EPS) * gamma + beta
        return out.reshape(*x.shape[:-1], out.shape[-1])
    x = x + _L0_attn_ref(_layernorm(x, axis=-1), L0_attn_Wq, L0_attn_Wk, L0_attn_Wv, L0_attn_rel_table, L0_attn_gamma, L0_attn_beta)
    x = x + _L0_xattn_ref(_layernorm(x, axis=-1), ctx_1024, ctx_1024, mask_BxSxS2_ik1, L0_xattn_Wq, L0_xattn_Wk, L0_xattn_Wv, L0_xattn_Wu, L0_xattn_bu)
    x = x + _L0_ffn_ref(_layernorm(x, axis=-1), L0_ffn_W1, L0_ffn_b1, L0_ffn_W2, L0_ffn_b2, L0_ffn_gate_W, L0_ffn_shared_W, L0_ffn_shared_b, L0_ffn_gamma, L0_ffn_beta)
    return x

_drawn_inputs = setup_inputs


def setup_inputs(seed=0):
    import zlib

    import numpy as np

    out = dict(_drawn_inputs(seed))
    spreads = {'L0_attn_gamma': (1.0, 0.2),
     'L0_attn_beta': (0.0, 0.1),
     'L0_ffn_b1': (0.0, 0.1),
     'L0_ffn_b2': (0.0, 0.1),
     'L0_ffn_shared_b': (0.0, 0.1),
     'L0_ffn_gamma': (1.0, 0.2),
     'L0_ffn_beta': (0.0, 0.1)}
    factors = {'L0_attn_Wq': 4.209, 'L0_attn_Wk': 4.115}
    for name, (base, spread) in spreads.items():
        noise = np.random.default_rng([zlib.crc32(name.encode()), seed]).standard_normal(out[name].shape)
        drawn = base * np.exp(spread * noise) if base else spread * noise
        out[name] = jnp.asarray(drawn.astype(out[name].dtype))
    for name, factor in factors.items():
        out[name] = (out[name] * factor).astype(out[name].dtype)
    return out
```

```python
from contextlib import ExitStack

import numpy as np

import concourse.bass as bass
from concourse import mybir

F32 = mybir.dt.float32
BF16 = mybir.dt.bfloat16
I32 = mybir.dt.int32
U32 = mybir.dt.uint32
ALU = mybir.AluOpType
ACT = mybir.ActivationFunctionType
AX = mybir.AxisListType

P = 128
B, S, D, H = 2, 1024, 256, 16
DH = D // H
NT = B * S // P
CP = S // P
KC = D // P
HG = 4
NG = H // HG
NKT = S // P
RELS = 511
TW = 2 * S - 8
TG = 8 * (NKT - 1) + P * 3 + 64 * (HG - 1) + P
T0 = TW - RELS
STK = 6 * DH + 3
NSTK = 13
CTX = 77
BOUND = 64.0
NEG = -float(2 ** 100)
EXPERTS, HID = 8, 1024
SLOT_TILES = 2 * NT + EXPERTS - 1


ARENA = 163 * 256
LATE_DMAS = 4 + 1 + 2 * B + 6 + 7
X_AT, W2_AT, E_AT = 133 * 1024, 64 * 1024, 128 * 1024


def dims(ap, *free):
    return bass.AP(ap.tensor, ap.offset, [list(ap.ap[0])] + [list(f) for f in free])


def decoder_layer(nc, x, ctx_in, mask, wq, wk, wv, rel_rows, attn_g, attn_b, xwq, xwk, xwv, xwu, xbu,
                  w1, b1, w2, b2, gate_w, shared_w, shared_b, ffn_g, ffn_b, consts, out):
    scope = ExitStack()

    def sb(name, shape, dt=F32):
        return scope.enter_context(nc.sbuf_tensor(name, shape, dt))

    def sem(name):
        return scope.enter_context(nc.semaphore(name))

    with scope:
        qs_dram = nc.dram_tensor("q_parts", [B, 3, D, S], BF16).ap()
        ks_dram = nc.dram_tensor("k_parts", [B, 3, D, S], BF16).ap()
        xs_dram = nc.dram_tensor("rows_by_expert", [SLOT_TILES * P, D], F32).ap()
        ys_dram = nc.dram_tensor("results_by_expert", [SLOT_TILES * P, D], F32).ap()
        shift_dram = nc.dram_tensor("shift_parts", [B, 3, H, S], BF16).ap()

        x_sb = sb("x_sb", [P, NT, D])
        xh = sb("xh", [P, NT, D])
        ident = sb("ident", [P, P])
        stats = sb("stats", [P, NT, 6])
        mv = sb("mv", [P, NT, 2])
        rstd = sb("rstd", [P, NT])

        rows_sb = sb("rows_sb", [P, 6, D])
        attn_g_sb, attn_b_sb, xbu_sb, shared_b_sb, ffn_g_sb, ffn_b_sb = (rows_sb[:, i, :] for i in range(6))
        slot = sb("slot", [P, 2, NT], U32)
        weight = sb("weight", [P, 2, NT])
        route_c = sb("route_c", [P, EXPERTS * NT + EXPERTS + EXPERTS * EXPERTS + SLOT_TILES * EXPERTS])
        before = sb("before", [P, P], BF16)
        ones = sb("ones", [P, P], BF16)
        tile_expert = sb("tile_expert", [P, SLOT_TILES], I32)
        ident_bf = sb("ident_bf", [P, P], BF16)
        sizes = sb("sizes", [P, KC, 2, 4])[:, :, :, :]
        size = sb("size", [P, KC, 2])[:, :, :]
        size_prod = sb("size_prod", [P, KC])[:, :]
        head_bound = sb("head_bound", [1, H])[:, :]
        most = sb("most", [1, 2])[:, :]
        flags = sb("flags", [1, 2], I32)[:, :]
        arena = sb("arena", [P, ARENA])

        class Region:

            def __init__(self, at):
                self.at = at // 4

            def take(self, shape, dt=F32):
                n = int(np.prod(shape[1:])) * mybir.dt.size(dt) // 4
                ap = arena[0:shape[0], self.at:self.at + n]
                self.at += n
                assert self.at <= ARENA, self.at
                ap = ap if dt == F32 else ap.bitcast(dt)
                names = "abcde"[:len(shape) - 1]
                sizes = dict(zip(names, shape[1:]))
                return ap.rearrange(f"p ({' '.join(names)}) -> p {' '.join(names)}", **sizes)

        r = Region(0)
        wq_sb, wk_sb, wv_sb = (r.take([P, KC, D]) for _ in range(3))
        table = r.take([P, TW])
        t_grp = r.take([P, TG])
        last_row = r.take([P, 2])
        v_sb = r.take([P, B, NKT, D])
        v_grp = [r.take([P, NKT, HG, 32]) for _ in range(B)]
        v_bias = r.take([P, NKT, HG, B, DH])
        probs = r.take([P, 2, HG, S])
        xt = probs.rearrange("p a h s -> p (a h s)")
        xt_tile = xt[:, 0:KC * B * S].rearrange("p (k n) -> p k n", k=KC)
        xt_nat = xt[:, KC * B * S:2 * KC * B * S].rearrange("p (k n) -> p k n", k=KC)
        q_stk = [r.take([P, HG, S], BF16)[0:STK] for _ in range(B)]
        k_stk = [r.take([P, HG, S], BF16)[0:STK] for _ in range(B)]
        parts = r.take([P, 4, 3, 512], BF16)
        rest = r.take([P, 4, 512])
        rest_end = r.at
        r.at -= 4 * 512
        o_t, bias_t = r.take([P, S]), r.take([P, S])
        rden = r.take([P, CP, HG])
        o_n = r.take([P, CP, HG, DH])
        ATT_END = 4 * max(r.at, rest_end)
        assert ATT_END <= X_AT

        row_max = xt[:, 0:NT * H].rearrange("p (t h) -> p t h", h=H)
        neg_max = rest.rearrange("p a n -> p (a n)")[0:H]
        neg_parts = parts.rearrange("p a c n -> p (a c n)").rearrange("p (c n) -> p c n", c=3)[0:H]

        r = Region(X_AT)
        xwq_sb, xwk_sb, xwv_sb, xwu_sb = (r.take([P, KC, D]) for _ in range(4))
        ctx_sb = r.take([P, B, D])[0:CTX]
        mask_sb = r.take([P, NT, CTX], I32)
        pick = r.take([P, H, CTX + 1], BF16)[0:CTX + 1 + 3 * H]
        head_rows = r.take([P, 8])
        counts = r.take([P, 2])[0:CTX + 1]
        zeros = r.take([P, D])

        r = Region(W2_AT)
        x2_t = r.take([P, KC, B * S])
        probs2 = x2_t.rearrange("p k n -> p (k n)").rearrange("p (a h n) -> p a h n", a=2, h=HG)[0:CTX + 1]
        q2_t = r.take([P, KC, B * S])
        k2_pad = r.take([P, B, H, CTX + 1])
        v2_sb = r.take([P, B, H, 32])[0:CTX + 1]
        ctx_t = r.take([P, B, KC, CTX + 1])
        hide = r.take([P, NT, CTX + 1], BF16)
        hide_max = r.take([P, NT])
        ctx_k = r.take([P, KC, B * CTX])
        k2_size = r.take([P, KC])
        hide_t = r.take([P, B * S], BF16)
        neg_parts2 = Region(4 * r.at).take([P, 3, B * S], BF16)[0:H]
        o2_tr = r.take([P, 2, 512])
        rden2 = r.take([P, 4, HG])
        o2 = r.take([P, 4, D])
        o2_t = r.take([P, KC, 512])
        assert 4 * r.at <= X_AT
        x2_flat = x2_t.rearrange("p k n -> p (k n)")
        hidden_s = x2_flat[:, 0:H * CTX].rearrange("p (h t) -> p h t", h=H)
        row_max2 = x2_flat[:, 1280:1280 + NT * H].rearrange("p (t h) -> p t h", h=H)
        neg_max2 = x2_flat[0:H, 2048:4096]

        w1_sb = Region(0).take([P, EXPERTS, KC, HID])
        w2_sb = Region(W2_AT).take([P, EXPERTS, HID // P, D])
        r = Region(E_AT)
        acc = r.take([P, NT, D])
        sgw_sb = r.take([P, KC, D + EXPERTS])
        x3_at = 4 * r.at
        x3_t = r.take([P, KC, B * S])
        r = Region(x3_at)
        xs_in = r.take([P, 2, D])
        xs_t = r.take([P, 2, KC, P])
        y_sb = r.take([P, 2, D])
        b2_row = r.take([P, 2, D])
        route_at = 4 * r.at
        y_in = r.take([P, 2, 2, D])
        r = Region(route_at)
        logits, hit, cand, pick1, pick2, lg2, pos = (r.take([P, NT, EXPERTS]) for _ in range(7))
        both = r.take([P, NT, EXPERTS], BF16)
        top1, top2, best, over = (r.take([P, NT]) for _ in range(4))
        ended = Region(route_at).take([P, SLOT_TILES, EXPERTS])
        ended_n = r.take([P, SLOT_TILES])
        tiles_of, base, ends = (r.take([P, EXPERTS]) for _ in range(3))
        assert 4 * r.at <= x3_at + 16384
        xh_flat = xh[:, :, :].rearrange("p t f -> p (t f)")
        b1_row = xh_flat[:, 0:2 * HID].rearrange("p (a n) -> p a n", a=2)
        hid = xh_flat[:, 2 * HID:3 * HID]
        hid_t = xh_flat[:, 3 * HID:4 * HID].rearrange("p (k n) -> p k n", k=HID // P)

        ps = scope.enter_context(nc.psum_tensor("ps", [P, 8, 512], F32))

        x_in = [sem(f"x_in{b}") for b in range(B)]
        w_in, table_fill, table_in = sem("w_in"), sem("table_fill"), sem("table_in")
        ln_var, ln_std, dve_link = sem("ln_var"), sem("ln_std"), sem("dve_link")
        xh_ready, xt_ps, xt_ready, nat_ready = sem("xh_ready"), sem("xt_ps"), sem("xt_ready"), sem("nat_ready")
        proj_ps, part0, rest1, part1, part2 = (sem(n) for n in ("proj_ps", "part0", "rest1", "part1", "part2"))
        v_ready = sem("v_ready")
        parts_out = [sem(f"parts_out{i}") for i in range(4)]
        zero_rows, zero_out = sem("zero_rows"), sem("zero_out")
        stk_in = [sem(f"stk_in{b}") for b in range(B)]
        ones_set = sem("ones_set")
        vg_ready = [sem(f"vg_ready{b}") for b in range(B)]
        vb_ready, t_ready = sem("vb_ready"), sem("t_ready")
        s_ready, s_free, p_free = sem("s_ready"), sem("s_free"), sem("p_free")
        bias_ps, bias_out, bias_tr = sem("bias_ps"), sem("bias_out"), sem("bias_tr")
        o_out, o_tr, bias_read, dve_att = sem("o_out"), sem("o_tr"), sem("bias_read"), sem("dve_att")
        att_done = sem("att_done")
        bound_in, bound_ps, flag_set = sem("bound_in"), sem("bound_ps"), sem("flag_set")
        max_in = [sem(f"max_in{b}") for b in range(B)]
        max_ps, max_read, max_done, max_tr, max_split, shift_out, dve_max = (sem(n) for n in (
            "max_ps", "max_read", "max_done", "max_tr", "max_split", "shift_out", "dve_max"))
        max2_ps, max2_read, max2_done, max2_tr, max2_split, shift2_out, dve_max2 = (sem(n) for n in (
            "max2_ps", "max2_read", "max2_done", "max2_tr", "max2_split", "shift2_out", "dve_max2"))
        late_in, zeros_set, xs_zero = sem("late_in"), sem("zeros_set"), sem("xs_zero")
        x_shifted = sem("x_shifted")
        x2_ps, x2_ready, q2_ps, q2_ready = sem("x2_ps"), sem("x2_ready"), sem("q2_ps"), sem("q2_ready")
        ctx_ps, ctx_ready, kv2_ps, kv2_ready = sem("ctx_ps"), sem("ctx_ready"), sem("kv2_ps"), sem("kv2_ready")
        hide_ready, hide_ps, hide_out = sem("hide_ready"), sem("hide_ps"), sem("hide_out")
        s2_ready, s2_free, pv2_done, o2_out = sem("s2_ready"), sem("s2_free"), sem("pv2_done"), sem("o2_out")
        o2_tr_done, o2_div, dve_x = sem("o2_tr_done"), sem("o2_div"), sem("dve_x")
        o2_ps, o2t_ready, u_ps, x2_added = sem("o2_ps"), sem("o2t_ready"), sem("u_ps"), sem("x2_added")
        w1_in, w2_in, sgw_in = sem("w1_in"), sem("w2_in"), sem("sgw_in")
        x3_ps, x3_ready, sg_ps, sg_read, sg_act, halved = (sem(n) for n in (
            "x3_ps", "x3_ready", "sg_ps", "sg_read", "sg_act", "halved"))
        top_ready, pair_ready, both_ready, rank_ps = (sem(n) for n in ("top_ready", "pair_ready", "both_ready", "rank_ps"))
        route_done, scattered = sem("route_done"), sem("scattered")
        xs_landed = [sem(f"xs_landed{i}") for i in range(2)]
        b1_landed = [sem(f"b1_landed{i}") for i in range(2)]
        b2_landed = [sem(f"b2_landed{i}") for i in range(2)]
        xs_ps, xs_ready, h_ps, h_sum, h_act, ht_ps, ht_ready, y_ps, y_ready = (sem(n) for n in (
            "xs_ps", "xs_ready", "h_ps", "h_sum", "h_act", "ht_ps", "ht_ready", "y_ps", "y_ready"))
        y_stored = [sem(f"y_stored{i}") for i in range(2)]
        y_landed = [sem(f"y_landed{i}") for i in range(2)]
        y_used, out_ready, out_done = sem("y_used"), sem("out_ready"), sem("out_done")

        proj = ([("k", 0, n) for n in range(4)] + [("q", 0, n) for n in range(4)]
                + [("v", b, n) for b in range(B) for n in range(4)]
                + [("k", 1, n) for n in range(4)] + [("q", 1, n) for n in range(4)])
        qk_at = [c for c, (kind, _, _) in enumerate(proj) if kind != "v"]
        v_at = [c for c, (kind, _, _) in enumerate(proj) if kind == "v"]
        PB = 6

        block = scope.enter_context(nc.Block())

        def needed(on, eng, which):
            eng.wait_ge(flag_set, which + 1)
            flag = on.alloc_register(f"flag_{which}_{on.engine.name}")
            on.reg_load(flag, flags[0:1, which:which + 1])
            return eng.If_ne(flag, 0)

        @block.sync
        def _(sp):
            for b in range(B):
                rows = x[b].rearrange("(a c o) f -> o a c f", c=CP, o=2)
                for o in range(2):
                    sp.dma_start(x_sb[64 * (1 - o):64 * (2 - o), CP * b:CP * (b + 1), :], rows[o]).then_inc(x_in[b], 16)
            sp.dma_start(ident[:, :], consts["ident"]).then_inc(w_in, 16)
            for dst, src in ((wk_sb, wk), (wq_sb, wq), (wv_sb, wv)):
                sp.dma_start(dst[:, :, :], src.rearrange("(k p) n -> p k n", p=P)).then_inc(w_in, 16)
            for r in range(8):
                sp.dma_start(last_row[16 * r:16 * r + 16, 0:1], rel_rows[:, 0:1],
                             allow_slow_non_contiguous=True).then_inc(w_in, 16)
            sp.wait_ge(table_fill, 1)
            for r in range(8):
                sp.dma_start(table[16 * r:16 * r + 16, T0 + r:TW], rel_rows[:, 0:RELS - r]).then_inc(table_in, 16)
            for dst, src in ((xwq_sb, xwq), (xwk_sb, xwk), (xwv_sb, xwv), (xwu_sb, xwu)):
                sp.dma_start(dst, src.rearrange("(k p) n -> p k n", p=P)).then_inc(late_in, 16)
            sp.dma_start(ctx_sb, ctx_in.rearrange("b t d -> t b d")).then_inc(late_in, 16)
            for b in range(B):
                rows = mask[b].rearrange("(a c o) t -> o a c t", c=CP, o=2)
                for o in range(2):
                    sp.dma_start(mask_sb[64 * (1 - o):64 * (2 - o), CP * b:CP * (b + 1), :], rows[o]).then_inc(late_in, 16)
            for i, row in enumerate((attn_g, attn_b, xbu, shared_b, ffn_g, ffn_b)):
                sp.dma_start(rows_sb[:, i, :], row.partition_broadcast(P)).then_inc(late_in, 16)
            for dst, name in ((pick, "pick"), (head_rows, "head_rows"), (counts, "counts"), (ident_bf[:, :], "ident_bf"),
                              (before[:, :], "before"), (ones[:, :], "ones"), (route_c[:, :], "route_c")):
                sp.dma_start(dst, consts[name]).then_inc(late_in, 16)
            sp.wait_ge(zeros_set, 1)
            for half in range(3):
                rows = xs_dram[13 * P * half:13 * P * (half + 1), :].rearrange("(t p) f -> p t f", p=P)
                sp.dma_start(rows, zeros.unsqueeze(1).to_broadcast([P, 13, D])).then_inc(xs_zero, 16)
            sp.wait_ge(zero_rows, 1)
            for b in range(B):
                sp.dma_start(shift_dram[b].rearrange("c h s -> (c h) s"),
                             rest[0:48, 0, :].bitcast(BF16)).then_inc(zero_out, 16)
            for q, c in enumerate(qk_at):
                kind, m, n = proj[c]
                dst = (qs_dram if kind == "q" else ks_dram)[n // 2, :, P * m:P * (m + 1), 512 * (n % 2):512 * (n % 2 + 1)]
                sp.wait_ge(part2, q + 1)
                sp.dma_start(dst.rearrange("c p n -> p c n"), parts[:, q % 4, :, :]).then_inc(parts_out[q % 4], 16)
            for i in range(4):
                sp.wait_ge(parts_out[i], 16 * (len(qk_at) // 4))
            sp.wait_ge(zero_out, 32)
            sp.wait_ge(ones_set, 1)

            def load_parts(g, b, landed):
                for blk in range(6):
                    for stk, src, part in ((k_stk[b], ks_dram, (0, 1, 2, 0, 1, 0)[blk]),
                                           (q_stk[b], qs_dram, (0, 0, 0, 1, 1, 2)[blk])):
                        rows = src[b, part, bass.ds(64 * g, 64), :].rearrange("(h d) s -> d h s", h=HG)
                        sp.dma_start(stk[16 * blk:16 * blk + 16, :, :], rows).then_inc(landed, 16)

            with needed(nc.sync, sp, 0):
                with sp.Fori(0, NG) as g:
                    sp.wait_ge(max_read, B * HG * CP * g + 2)
                    for b in range(B):
                        load_parts(g, b, max_in[b])
                sp.wait_ge(max_read, B * HG * CP * NG + 2)
                sp.wait_ge(max_split, 1)
                for b in range(B):
                    sp.dma_start(shift_dram[b].rearrange("c h s -> h c s"), neg_parts[:, :, S * b:S * (b + 1)])\
                        .then_inc(shift_out, 16)
                sp.wait_ge(shift_out, 16 * B)

            def load_group(g, b):
                load_parts(g, b, stk_in[b])
                sp.dma_start(q_stk[b][96:99, :, :], shift_dram[b, :, bass.ds(HG * g, HG), :]).then_inc(stk_in[b], 16)

            for b in range(B):
                load_group(0, b)
            with sp.Fori(1, NG) as g:
                for b in range(B):
                    sp.wait_ge(s_free, B * NKT * HG * g + (NKT * HG * (b + 1 - B) + 2))
                    load_group(g, b)

            sp.wait_ge(att_done, NG)
            for e in range(EXPERTS):
                sp.dma_start(w1_sb[:, e], w1[e].rearrange("(k p) n -> p k n", p=P)).then_inc(w1_in, 16)
            with needed(nc.sync, sp, 1):
                sp.wait_ge(max2_split, 1)
                for c in range(3):
                    at = CTX + 1 + H * c
                    sp.dma_start(hide_t[at:at + H, :], neg_parts2[:, c, :]).then_inc(shift2_out, 16)
            sp.wait_ge(x2_added, NT // 4)
            sp.dma_start(sgw_sb[:, :, 0:D], shared_w.rearrange("(k p) n -> p k n", p=P)).then_inc(sgw_in, 16)
            sp.dma_start(sgw_sb[:, :, D:D + EXPERTS], gate_w.rearrange("(k p) n -> p k n", p=P)).then_inc(sgw_in, 16)
            for e in range(EXPERTS):
                sp.dma_start(w2_sb[:, e], w2[e].rearrange("(k p) n -> p k n", p=P)).then_inc(w2_in, 16)

            def expert(j):
                return nc.sync.value_load(tile_expert[0:1, bass.ds(j, 1)], min_val=0, max_val=EXPERTS - 1)

            def load_rows(j, buf):
                sp.dma_start(xs_in[:, buf, :], xs_dram[bass.ds(j * P, P), :]).then_inc(xs_landed[buf], 16)

            def load_b1(j, buf):
                sp.dma_start(b1_row[:, buf, :], b1[bass.ds(expert(j), 1), :].partition_broadcast(P)).then_inc(b1_landed[buf], 16)

            def load_b2(j, buf):
                sp.dma_start(b2_row[:, buf, :], b2[bass.ds(expert(j), 1), :].partition_broadcast(P)).then_inc(b2_landed[buf], 16)

            def step(j, buf, rows=True, b2_too=True):
                if rows:
                    sp.wait_ge(xs_ps, j + 1)
                    load_rows(j + 2, buf)
                    sp.wait_ge(h_sum, j + 1)
                    load_b1(j + 2, buf)
                sp.wait_ge(y_ready, j)
                sp.dma_start(ys_dram[bass.ds((j - 1) * P, P), :], y_sb[:, 1 - buf, :]).then_inc(y_stored[1 - buf], 16)
                if b2_too:
                    load_b2(j + 1, 1 - buf)

            sp.wait_ge(scattered, 16 * 2 * NT)
            sp.wait_ge(route_done, 1)
            for j in range(2):
                load_rows(j, j)
                load_b1(j, j)
                load_b2(j, j)
            sp.wait_ge(xs_ps, 1)
            load_rows(2, 0)
            sp.wait_ge(h_sum, 1)
            load_b1(2, 0)
            with sp.Fori(0, (SLOT_TILES - 3) // 2) as i:
                for o in range(2):
                    step(2 * i + (o + 1), 1 - o)
            for j in range(SLOT_TILES - 2, SLOT_TILES + 1):
                step(j, j % 2, False, j + 1 < SLOT_TILES)
            out_rows = out.rearrange("b (a c o) f -> b o a c f", c=CP, o=2)
            for b in range(B):
                sp.wait_ge(out_ready, b + 1)
                for o in range(2):
                    sp.dma_start(out_rows[b, o], x_sb[64 * (1 - o):64 * (2 - o), CP * b:CP * (b + 1), :]).then_inc(out_done, 16)
            sp.wait_ge(out_done, 16 * 2 * B)

        @block.gpsimd
        def _(pool):
            nc.gpsimd.memset(zeros, 0.0).then_inc(zeros_set, 1)
            for b in range(B):
                nc.gpsimd.memset(v_grp[b][:, :, :, DH:DH + 1], 1.0)
                nc.gpsimd.memset(v_grp[b][:, :, :, DH + 1:32], 0.0)
            pool.wait_ge(late_in, 16 * LATE_DMAS)
            pool.wait_ge(xh_ready, NT)
            nc.gpsimd.tensor_tensor(x_sb[:, :, :], x_sb[:, :, :], attn_b_sb.unsqueeze(1).to_broadcast([P, NT, D]),
                                    ALU.add).then_inc(x_shifted, 1)

            def group_values(g, b):
                src = v_sb[:, b, :, bass.ds(64 * g, 64)].rearrange("p t (h d) -> p t h d", h=HG)
                nc.gpsimd.tensor_copy(v_grp[b][:, :, :, 0:DH], src).then_inc(vg_ready[b], 1)
                nc.gpsimd.tensor_copy(v_bias[:, :, :, b, :], src).then_inc(vb_ready, 1)

            def group_table(g):
                nc.gpsimd.tensor_copy(t_grp[:, :], table[:, bass.ds(512 + 64 * HG * g, TG)]).then_inc(t_ready, 1)

            pool.wait_ge(v_ready, len(v_at))
            pool.wait_ge(table_in, 16 * 8)
            group_table(0)
            for b in range(B):
                group_values(0, b)
            with pool.Fori(1, NG) as g:
                pool.wait_ge(bias_ps, g)
                group_table(g)
                for b in range(B):
                    pool.wait_ge(p_free, B * NKT * g + (NKT * (b + 1 - B) + 2))
                    group_values(g, b)

            pool.wait_ge(xh_ready, 3 * NT)
            nc.gpsimd.tensor_tensor(x_sb[:, :, :], x_sb[:, :, :], xbu_sb.unsqueeze(1).to_broadcast([P, NT, D]),
                                    ALU.add).then_inc(x_shifted, 1)
            pool.wait_ge(xs_zero, 16 * 3)
            pool.wait_ge(route_done, 1)
            for t in range(NT):
                for k in range(2):
                    nc.gpsimd.indirect_dma_start(
                        out=xs_dram, out_offset=bass.IndirectOffsetOnAxis(ap=slot[:, k, t:t + 1], axis=0),
                        in_=xh[:, t, :], in_offset=None).then_inc(scattered, 16)
            pool.wait_ge(sg_act, NT // 4)
            nc.gpsimd.tensor_scalar(acc, acc, 0.5, None, ALU.mult).then_inc(halved, 1)
            nc.gpsimd.tensor_tensor(x_sb[:, :, :], x_sb[:, :, :], ffn_b_sb.unsqueeze(1).to_broadcast([P, NT, D]),
                                    ALU.add).then_inc(x_shifted, 1)
            for i in range(2):
                pool.wait_ge(y_stored[i], 16 * ((SLOT_TILES + 1 - i) // 2))
            for t in range(NT):
                if t >= 2:
                    pool.wait_ge(y_used, t - 1)
                for k in range(2):
                    nc.gpsimd.indirect_dma_start(
                        out=y_in[:, t % 2, k, :], out_offset=None, in_=ys_dram,
                        in_offset=bass.IndirectOffsetOnAxis(ap=slot[:, k, t:t + 1], axis=0)).then_inc(y_landed[t % 2], 16)

        @block.scalar
        def _(act):
            n_sqrt = [0]

            def sqrt_of_var(b):
                n_sqrt[0] += 1
                act.wait_ge(ln_var, n_sqrt[0])
                r = rstd[:, CP * b:CP * (b + 1)]
                nc.scalar.activation(r, r, ACT.Sqrt).then_inc(ln_std, 1)

            for b in range(B):
                sqrt_of_var(b)
            for b in range(B):
                act.wait_ge(xt_ready, CP // 2 * (b + 1))
                for k in range(KC):
                    for o in range(2):
                        src = xt_tile[:, k, S * b + 64 * (1 - o):S * b + 64 * (1 - o) + 1]
                        dst = xt_nat[:, k, S * b + o:S * b + o + 1]
                        nc.scalar.copy(dims(dst, [2, CP], [16, 64]), dims(src, [P, CP], [1, 64])).then_inc(nat_ready, 1)

            def first_part(q):
                act.wait_ge(proj_ps, qk_at[q] + 1)
                if q >= 4:
                    act.wait_ge(parts_out[q % 4], 16 * (q // 4))
                nc.scalar.copy(parts[:, q % 4, 0, :], ps[:, qk_at[q] % PB, :]).then_inc(part0, 1)

            def second_part(q):
                act.wait_ge(rest1, q + 1)
                nc.scalar.copy(parts[:, q % 4, 1, :], rest[:, q % 4, :]).then_inc(part1, 1)

            for c, (kind, m, n) in enumerate(proj):
                if kind == "v":
                    act.wait_ge(proj_ps, c + 1)
                    nc.scalar.copy(v_sb[:, m, 2 * n:2 * n + 2, :],
                                   ps[:, c % PB, :].rearrange("p (t f) -> p t f", t=2)).then_inc(v_ready, 1)
                else:
                    q = qk_at.index(c)
                    first_part(q)
                    if q >= 1:
                        second_part(q - 1)
            second_part(len(qk_at) - 1)

            act.sem_inc(s_free, 2)
            with act.Fori(0, NG) as g:
                for st in range(B * NKT):
                    for h in range(HG):
                        u = HG * st + h
                        if h == 0:
                            act.wait_ge(p_free, B * NKT * g + (st + 1))
                        act.wait_ge(s_ready, B * NKT * HG * g + (u + 1))
                        nc.scalar.activation(probs[:, st % 2, h, :],
                                             ps[:, 2 * (u % 2):2 * (u % 2) + 2, :].rearrange("p a n -> p (a n)"),
                                             ACT.Exp, scale=float(D) ** -0.5).then_inc(s_free, 1)

            for b in range(B):
                sqrt_of_var(b)
            for b in range(B):
                sqrt_of_var(b)
            for c in range(KC * 4):
                act.wait_ge(q2_ps, c + 1)
                nc.scalar.copy(q2_t[:, c % KC, 512 * (c // KC):512 * (c // KC + 1)], ps[:, c % 4, :]).then_inc(q2_ready, 1)
            act.sem_inc(s2_free, 2)
            with act.Fori(0, 2) as i:
                for b in range(B):
                    for hg in range(NG):
                        for pr in range(2):
                            u = 8 * b + 2 * hg + pr
                            act.wait_ge(s2_ready, 16 * i + (u + 1))
                            if pr == 0:
                                act.wait_ge(pv2_done, 8 * i + (4 * b + hg + 1))
                            nc.scalar.activation(probs2[:, hg % 2, 2 * pr:2 * pr + 2, :], ps[0:CTX + 1, 2 * (u % 2):2 * (u % 2) + 2, :],
                                                 ACT.Exp, scale=float(DH) ** -0.5).then_inc(s2_free, 1)
                    act.wait_ge(o2_ps, 2 * i + (b + 1))
                    nc.scalar.copy(o2_t, ps[:, 6:8, :]).then_inc(o2t_ready, 1)
            for b in range(B):
                sqrt_of_var(b)
            for q in range(NT // 4):
                act.wait_ge(sg_read, 4 * q + 4)
                nc.scalar.activation(acc[:, 4 * q:4 * q + 4, :], acc[:, 4 * q:4 * q + 4, :], ACT.Gelu).then_inc(sg_act, 1)
            act.wait_ge(top_ready, 1)
            nc.scalar.activation(over, over, ACT.Exp).then_inc(pair_ready, 1)
            def turned_rows(j, buf, n):
                act.wait_ge(xs_ps, n)
                nc.scalar.copy(xs_t[:, buf, :, :], ps[:, 7, 0:KC * P].rearrange("p (k n) -> p k n", k=KC)).then_inc(xs_ready, 1)

            def activate(n):
                act.wait_ge(h_sum, n)
                nc.scalar.activation(hid, hid, ACT.Gelu).then_inc(h_act, 1)

            turned_rows(0, 0, 1)
            turned_rows(1, 1, 2)
            activate(1)
            with act.Fori(0, (SLOT_TILES - 3) // 2) as i:
                for o in range(2):
                    turned_rows(2 * i + (o + 2), o, 2 * i + (o + 3))
                    activate(2 * i + (o + 2))
            for j in range(SLOT_TILES - 2, SLOT_TILES):
                if j + 1 < SLOT_TILES:
                    turned_rows(j + 1, (j + 1) % 2, j + 2)
                activate(j + 1)
            for b in range(B):
                sqrt_of_var(b)

        @block.vector
        def _(dve):
            links = [0]

            def link(ins):
                links[0] += 1
                ins.then_inc(dve_link, 1)
                dve.wait_ge(dve_link, links[0])

            n_ln = [0]

            def normalise(src, dst, b, eps):
                for t in range(CP * b, CP * (b + 1)):
                    last = nc.vector.bn_stats(stats[:, t, :], src[:, t, :])
                link(last)
                for t in range(CP * b, CP * (b + 1)):
                    last = nc.vector.bn_aggr(mv[:, t, :], stats[:, t, :])
                link(last)
                r = rstd[:, CP * b:CP * (b + 1)]
                nc.vector.tensor_scalar(r, mv[:, CP * b:CP * (b + 1), 1], eps, None, ALU.add).then_inc(ln_var, 1)
                n_ln[0] += 1
                dve.wait_ge(ln_std, n_ln[0])
                link(nc.vector.reciprocal(r, r))
                for t in range(CP * b, CP * (b + 1)):
                    last = nc.vector.tensor_scalar(dst[:, t, :], src[:, t, :], mv[:, t, 0:1], rstd[:, t:t + 1],
                                                   ALU.subtract, ALU.mult)
                    last.then_inc(xh_ready, 1)

            nc.vector.memset(rest[0:48, 0, :], 0.0).then_inc(zero_rows, 1)
            for b in range(B):
                dve.wait_ge(x_in[b], 32)
                normalise(x_sb, xh, b, 1e-5)
            dve.wait_ge(w_in, 16 * 12)
            nc.vector.tensor_copy(table[:, 0:T0 + 8], last_row[:, 0:1].to_broadcast([P, T0 + 8])).then_inc(table_fill, 1)
            for pair in range(NT // 2):
                dve.wait_ge(xt_ps, pair + 1)
                nc.vector.tensor_copy(xt_tile[:, :, 2 * P * pair:2 * P * (pair + 1)],
                                      ps[:, 6 + pair % 2, :].rearrange("p (k n) -> p k n", k=KC)).then_inc(xt_ready, 1)
            nc.vector.memset(k_stk[0][96:99, :, :], 1.0)
            nc.vector.memset(k_stk[1][96:99, :, :], 1.0).then_inc(ones_set, 1)
            dve.wait_ge(zero_out, 32)

            def first_rest(q):
                dve.wait_ge(part0, q + 1)
                nc.vector.tensor_tensor(rest[:, q % 4, :], ps[:, qk_at[q] % PB, :], parts[:, q % 4, 0, :],
                                        ALU.subtract).then_inc(rest1, 1)

            def third_part(q):
                dve.wait_ge(part1, q + 1)
                nc.vector.tensor_tensor(parts[:, q % 4, 2, :], rest[:, q % 4, :], parts[:, q % 4, 1, :],
                                        ALU.subtract).then_inc(part2, 1)

            def largest(q):
                kind, m, n = proj[qk_at[q]]
                nc.vector.tensor_reduce(sizes[:, m, "qk".index(kind), n:n + 1], parts[:, q % 4, 0, :], AX.X, ALU.max, apply_absolute_value=True)

            for q in range(len(qk_at)):
                first_rest(q)
                largest(q)
                if q >= 1:
                    third_part(q - 1)
            third_part(len(qk_at) - 1)

            def bound(scale, which, linked):
                nc.vector.tensor_tensor(size_prod, size[:, :, 0], size[:, :, 1], ALU.mult).then_inc(bound_in, 1)
                dve.wait_ge(bound_ps, which + 1)
                linked(nc.vector.tensor_copy(head_bound, ps[0:1, 7, 0:H]))
                linked(nc.vector.tensor_reduce(most[:, 0:1], head_bound, AX.X, ALU.max))
                nc.vector.tensor_scalar(flags[:, which:which + 1], most[:, 0:1], BOUND / scale, None, ALU.is_gt)\
                    .then_inc(flag_set, 1)

            dve.wait_ge(part2, len(qk_at))
            link(nc.vector.tensor_reduce(size, sizes, AX.X, ALU.max))
            bound(float(D) ** -0.5, 0, link)

            def link_on(s):
                n = [0]

                def linked(ins):
                    n[0] += 1
                    ins.then_inc(s, 1)
                    dve.wait_ge(s, n[0])
                return linked

            def negated_parts(rows, into, linked, done):
                linked(nc.vector.tensor_scalar(rows, ps[0:H, 4:8, :].rearrange("p a n -> p (a n)"), -1.0, None, ALU.mult))
                linked(nc.vector.tensor_copy(into[:, 0, :], rows))
                linked(nc.vector.tensor_tensor(rows, rows, into[:, 0, :], ALU.subtract))
                linked(nc.vector.tensor_copy(into[:, 1, :], rows))
                nc.vector.tensor_tensor(into[:, 2, :], rows, into[:, 1, :], ALU.subtract).then_inc(done, 1)

            with needed(nc.vector, dve, 0):
                dve.sem_inc(max_read, 2)
                with dve.Fori(0, NG) as g:
                    for b in range(B):
                        for h in range(HG):
                            for t in range(CP):
                                u = CP * (HG * b + h) + t
                                dve.wait_ge(max_ps, B * HG * CP * g + (u + 1))
                                nc.vector.tensor_reduce(row_max[:, CP * b + t, bass.ds(HG * g + h, 1)],
                                                        ps[:, 2 * (u % 2):2 * (u % 2) + 2, :].rearrange("p a n -> p (a n)"),
                                                        AX.X, ALU.max).then_inc(max_read, 1)
                dve.wait_ge(max_tr, 1)
                for i in range(4):
                    dve.wait_ge(parts_out[i], 16 * (len(qk_at) // 4))
                negated_parts(neg_max, neg_parts, link_on(dve_max), max_split)

            dve.sem_inc(dve_att, 1)
            dve.sem_inc(o_out, 1)
            K = 4
            with dve.Fori(0, NG) as g:
                def link_att(ins, n):
                    ins.then_inc(dve_att, 1)
                    dve.wait_ge(dve_att, K * g + (n + 1))

                def heads_of(b):
                    return xh[:, CP * b:CP * (b + 1), bass.ds(64 * g, 64)].rearrange("p t (h d) -> p t h d", h=HG)

                turned = ps[:, 6:8, :].rearrange("p a (c h e) -> p (a c) h e", c=4, h=HG)

                def leave_psum(b):
                    dve.wait_ge(p_free, B * NKT * g + (NKT * (b + 1) + 2))
                    nc.vector.tensor_copy(o_t[:, :], ps[:, 4:6, :].rearrange("p a n -> p (a n)")).then_inc(o_out, 1)

                def divide(b):
                    dve.wait_ge(o_tr, 2 * g + (b + 1))
                    link_att(nc.vector.reciprocal(rden[:, :, :], turned[:, :, :, DH]), 2 * b + 1)
                    ins = nc.vector.tensor_tensor(o_n[:, :, :, :], turned[:, :, :, 0:DH],
                                                  rden[:, :, :].unsqueeze(3).to_broadcast([P, CP, HG, DH]), ALU.mult)
                    link_att(ins, 2 * b + 2)
                    return nc.vector.tensor_tensor(heads_of(b), heads_of(b), o_n[:, :, :, :], ALU.add)

                dve.wait_ge(bias_ps, g + 1)
                nc.vector.tensor_copy(bias_t[:, 0:512], ps[:, 6, :])
                nc.vector.tensor_copy(bias_t[:, 512:1024], ps[:, 7, 0:1].to_broadcast([P, 512])).then_inc(bias_out, 1)
                leave_psum(0)
                dve.wait_ge(bias_tr, g + 1)
                pair = ps[:, 6:8, :].rearrange("p a (c h b d) -> p (a c) h b d", c=4, h=HG, b=B)
                for b in range(B):
                    last = nc.vector.tensor_copy(heads_of(b), pair[:, :, :, b, :])
                last.then_inc(bias_read, 1)
                divide(0)
                leave_psum(1)
                divide(1).then_inc(att_done, 1)

            dve.wait_ge(dve_att, 4 * NG + 1)
            dve.wait_ge(att_done, NG)
            for b in range(B):
                normalise(xh, xh, b, 1e-3)
            dve.wait_ge(xh_ready, 2 * NT)
            dve.wait_ge(x_shifted, 1)
            link(nc.vector.tensor_tensor(xh[:, :, :], xh[:, :, :], attn_g_sb.unsqueeze(1).to_broadcast([P, NT, D]), ALU.mult))
            link(nc.vector.tensor_tensor(x_sb[:, :, :], x_sb[:, :, :], xh[:, :, :], ALU.add))
            dve.wait_ge(ctx_ps, 1)
            link(nc.vector.tensor_copy(ctx_t[:, :, :, 0:CTX], ps[:, 0, 0:B * KC * (CTX + 1)].rearrange(
                "p (b k t) -> p b k t", b=B, k=KC)[:, :, :, 0:CTX]))
            nc.vector.tensor_reduce(ctx_t[:, :, :, CTX:CTX + 1], ctx_t[:, :, :, 0:CTX], AX.X, ALU.add).then_inc(ctx_ready, 1)
            nc.vector.memset(k2_pad, 0.0)
            nc.vector.memset(hide_t[64:P, :], 0.0)
            link(nc.vector.memset(v2_sb, 0.0))
            nc.vector.tensor_copy(v2_sb[:, :, :, DH], counts[:, 0:1].unsqueeze(2).to_broadcast([CTX + 1, B, H]))
            dve.wait_ge(late_in, 16 * LATE_DMAS)
            link(nc.vector.tensor_scalar(hide[:, :, 0:CTX], mask_sb, 0.0, NEG, ALU.is_equal, ALU.mult))
            link(nc.vector.tensor_reduce(hide_max, hide[:, :, 0:CTX], AX.X, ALU.max))
            nc.vector.tensor_scalar(hide[:, :, CTX], hide_max, -1.0, NEG, ALU.mult, ALU.add).then_inc(hide_ready, 1)
            dve.wait_ge(kv2_ps, 1)
            nc.vector.tensor_copy(ctx_k, ps[:, 1:1 + KC, 0:B * CTX])
            for m in range(KC):
                for j in range(H // KC):
                    last = nc.vector.tensor_scalar(k2_pad[:, :, H // KC * m + j, 0:CTX],
                                                   ps[:, 1 + m, 0:B * CTX].rearrange("p (b t) -> p b t", b=B),
                                                   head_rows[:, j:j + 1], None, ALU.mult)
            last = nc.vector.tensor_copy(v2_sb[:, :, :, 0:DH], ps[0:CTX + 1, 3, :].rearrange("p (b h d) -> p b h d", b=B, h=H))
            last.then_inc(kv2_ready, 1)
            for i in range(2):
                dve.wait_ge(hide_ps, i + 1)
                last = nc.vector.tensor_copy(hide_t[0:CTX + 1, S * i:S * (i + 1)], ps[0:CTX + 1, 4 + i, :].bitcast(BF16))
            last.then_inc(hide_out, 1)
            for b in range(B):
                normalise(x_sb, xh, b, 1e-5)
            for pair in range(NT // 2):
                dve.wait_ge(x2_ps, pair + 1)
                nc.vector.tensor_copy(x2_t[:, :, 2 * P * pair:2 * P * (pair + 1)],
                                      ps[:, 6 + pair % 2, :].rearrange("p (k n) -> p k n", k=KC)).then_inc(x2_ready, 1)
            dve.wait_ge(q2_ready, KC * 4)
            nc.vector.tensor_reduce(size[:, :, 0:1], q2_t, AX.X, ALU.max, apply_absolute_value=True)
            link(nc.vector.tensor_reduce(k2_size, ctx_k, AX.X, ALU.max, apply_absolute_value=True))
            link(nc.vector.tensor_copy(size[:, :, 1], k2_size))
            bound(float(DH) ** -0.5, 1, link)
            with needed(nc.vector, dve, 1):
                linked = link_on(dve_max2)
                for t in range(NT):
                    dve.wait_ge(max2_ps, t + 1)
                    ins = nc.vector.tensor_tensor(hidden_s.rearrange("p (g h) t -> p g h t", g=NG),
                                                  ps[:, 0:NG, 0:HG * CTX].rearrange("p g (h t) -> p g h t", h=HG),
                                                  hide[:, t, 0:CTX].unsqueeze(1).unsqueeze(1).to_broadcast([P, NG, HG, CTX]), ALU.add)
                    linked(ins)
                    dve.sem_inc(max2_read, 1)
                    linked(nc.vector.tensor_reduce(row_max2[:, t, :], hidden_s, AX.X, ALU.max))
                nc.vector.tensor_scalar(row_max2, row_max2, -float(2 ** 90), None, ALU.max).then_inc(max2_done, 1)
                dve.wait_ge(max2_tr, 1)
                negated_parts(neg_max2, neg_parts2, linked, max2_split)
            dve.wait_ge(x_shifted, 2)
            dve.sem_inc(dve_x, 1)
            dve.sem_inc(o2_out, 2)
            with dve.Fori(0, 2) as i:
                for b in range(B):
                    for hg in range(NG):
                        n = 4 * b + hg
                        dve.wait_ge(pv2_done, 8 * i + (n + 3))
                        nc.vector.tensor_copy(o2_tr[:, hg % 2, :], ps[:, 4 + hg % 2, :]).then_inc(o2_out, 1)
                        dve.wait_ge(o2_tr_done, 8 * i + (n + 1))
                        turned2 = ps[:, 6, :].rearrange("p (t h e) -> p t h e", t=4, h=HG)
                        nc.vector.reciprocal(rden2, turned2[:, :, :, DH]).then_inc(dve_x, 1)
                        dve.wait_ge(dve_x, 8 * i + (n + 2))
                        nc.vector.tensor_tensor(o2[:, :, 64 * hg:64 * (hg + 1)].rearrange("p t (h d) -> p t h d", h=HG),
                                                turned2[:, :, :, 0:DH],
                                                rden2.unsqueeze(3).to_broadcast([P, 4, HG, DH]), ALU.mult).then_inc(o2_div, 1)
                    dve.wait_ge(u_ps, 2 * i + (b + 1))
                    xs = x_sb[:, bass.ds(4 * i + CP * b, 4), :]
                    nc.vector.tensor_tensor(xs, ps[:, 4:6, :].rearrange("p a (t f) -> p (a t) f", t=2), xs,
                                            ALU.add).then_inc(x2_added, 1)
            dve.wait_ge(x2_added, NT // 4)
            for b in range(B):
                normalise(x_sb, xh, b, 1e-5)
            for pair in range(NT // 2):
                dve.wait_ge(x3_ps, pair + 1)
                nc.vector.tensor_copy(x3_t[:, :, 2 * P * pair:2 * P * (pair + 1)],
                                      ps[:, 6 + pair % 2, :].rearrange("p (k n) -> p k n", k=KC)).then_inc(x3_ready, 1)
            for t in range(NT):
                dve.wait_ge(sg_ps, t + 1)
                nc.vector.tensor_copy(logits[:, t, :], ps[:, t % 4, D:D + EXPERTS])
                nc.vector.tensor_tensor(acc[:, t, :], ps[:, t % 4, 0:D], shared_b_sb, ALU.add).then_inc(sg_read, 1)
            e_names = [P, NT, EXPERTS]
            thresholds = route_c[:, 0:EXPERTS * NT].rearrange("p (e j) -> p e j", e=EXPERTS)
            rev = route_c[:, EXPERTS * NT:EXPERTS * NT + EXPERTS]
            tri = route_c[:, EXPERTS * NT + EXPERTS:EXPERTS * (NT + 1 + EXPERTS)].rearrange("p (e f) -> p e f", e=EXPERTS)
            tiles_c = route_c[:, EXPERTS * (NT + 1 + EXPERTS):].rearrange("p (j e) -> p j e", e=EXPERTS)

            def first_largest(values, top, picked):
                link(nc.vector.tensor_reduce(top, values, AX.X, ALU.max))
                link(nc.vector.tensor_tensor(hit, values, top.unsqueeze(2).to_broadcast(e_names), ALU.is_equal))
                link(nc.vector.tensor_tensor(cand, hit, rev.unsqueeze(1).to_broadcast(e_names), ALU.mult))
                link(nc.vector.tensor_reduce(best, cand, AX.X, ALU.max))
                link(nc.vector.tensor_tensor(picked, cand, best.unsqueeze(2).to_broadcast(e_names), ALU.is_equal))

            dve.wait_ge(sg_read, NT)
            first_largest(logits, top1, pick1)
            link(nc.vector.scalar_tensor_tensor(out=lg2, in0=pick1, scalar=NEG, in1=logits, op0=ALU.mult, op1=ALU.add))
            first_largest(lg2, top2, pick2)
            nc.vector.tensor_tensor(over, top2, top1, ALU.subtract).then_inc(top_ready, 1)
            nc.vector.tensor_tensor(both, pick1, pick2, ALU.add).then_inc(both_ready, 1)
            dve.wait_ge(rank_ps, 1)
            link(nc.vector.tensor_tensor(hit.rearrange("p t e -> p e t"), thresholds,
                                         ps[:, 5, 0:EXPERTS].unsqueeze(2).to_broadcast([P, EXPERTS, NT]), ALU.is_lt))
            link(nc.vector.tensor_reduce(tiles_of, hit.rearrange("p t e -> p e t"), AX.X, ALU.add))
            link(nc.vector.tensor_tensor(cand[:, 0:EXPERTS, :], tri, tiles_of.unsqueeze(1).to_broadcast([P, EXPERTS, EXPERTS]),
                                         ALU.mult))
            link(nc.vector.tensor_reduce(base, cand[:, 0:EXPERTS, :], AX.X, ALU.add))
            nc.vector.tensor_tensor(ends, base, tiles_of, ALU.add)
            link(nc.vector.scalar_tensor_tensor(out=pos, in0=base.unsqueeze(1).to_broadcast(e_names), scalar=float(P),
                                                in1=ps[:, 4, 0:P].rearrange("p (t e) -> p t e", e=EXPERTS),
                                                op0=ALU.mult, op1=ALU.add))
            for k, picked in enumerate((pick1, pick2)):
                link(nc.vector.tensor_tensor(hit, picked, pos, ALU.mult))
                link(nc.vector.tensor_reduce(best, hit, AX.X, ALU.add))
                link(nc.vector.tensor_copy(slot[:, k, :], best))
            link(nc.vector.tensor_tensor(ended, ends.unsqueeze(1).to_broadcast([P, SLOT_TILES, EXPERTS]), tiles_c, ALU.is_le))
            link(nc.vector.tensor_reduce(ended_n, ended, AX.X, ALU.add))
            nc.vector.tensor_scalar(tile_expert[:, :], ended_n, EXPERTS - 1.0, None, ALU.min).then_inc(route_done, 1)
            dve.wait_ge(pair_ready, 1)
            link(nc.vector.tensor_scalar(top1, over, 1.0, None, ALU.add))
            link(nc.vector.reciprocal(weight[:, 0, :], top1))
            link(nc.vector.tensor_tensor(weight[:, 1, :], over, weight[:, 0, :], ALU.mult))

            def sum_hidden(buf, n, nb):
                dve.wait_ge(h_ps, n)
                dve.wait_ge(b1_landed[buf], nb)
                nc.vector.tensor_tensor(hid, ps[:, 0:2, :].rearrange("p a n -> p (a n)"), b1_row[:, buf, :],
                                        ALU.add).then_inc(h_sum, 1)

            def turned_hidden(n):
                dve.wait_ge(ht_ps, n)
                nc.vector.tensor_copy(hid_t, ps[:, 4:6, :].rearrange("p a (k n) -> p (a k) n", n=P)).then_inc(ht_ready, 1)

            def result(buf, n, landed, stored=None):
                dve.wait_ge(y_ps, n)
                dve.wait_ge(b2_landed[buf], landed)
                if stored is not None:
                    dve.wait_ge(y_stored[buf], stored)
                nc.vector.tensor_tensor(y_sb[:, buf, :], ps[:, 6, 0:D], b2_row[:, buf, :], ALU.add).then_inc(y_ready, 1)

            sum_hidden(0, 1, 16)
            turned_hidden(1)
            sum_hidden(1, 2, 16)
            result(0, 1, 16)
            turned_hidden(2)
            sum_hidden(0, 3, 32)
            result(1, 2, 16)
            with dve.Fori(1, (SLOT_TILES - 1) // 2 - 1) as i:
                for o in range(2):
                    turned_hidden(2 * i + (o + 1))
                    sum_hidden(1 - o, 2 * i + (o + 2), 16 * i + 16 * (1 + o))
                    result(o, 2 * i + (o + 1), 16 * i + 16, 16 * i)
            for j in range(SLOT_TILES - 2, SLOT_TILES + 1):
                turned_hidden(j)
                if j < SLOT_TILES:
                    sum_hidden(j % 2, j + 1, 16 * (j // 2 + 1))
                result((j - 1) % 2, j, 16 * ((j - 1) // 2 + 1), 16 * ((j - 1) // 2))
            dve.wait_ge(halved, 1)
            for t in range(NT):
                dve.wait_ge(y_landed[t % 2], 32 * (t // 2 + 1))
                link(nc.vector.scalar_tensor_tensor(out=acc[:, t, :], in0=y_in[:, t % 2, 0, :], scalar=weight[:, 0, t:t + 1],
                                                    in1=acc[:, t, :], op0=ALU.mult, op1=ALU.add))
                ins = nc.vector.scalar_tensor_tensor(out=acc[:, t, :], in0=y_in[:, t % 2, 1, :], scalar=weight[:, 1, t:t + 1],
                                                     in1=acc[:, t, :], op0=ALU.mult, op1=ALU.add)
                ins.then_inc(y_used, 1)
            dve.wait_ge(y_used, NT)
            dve.wait_ge(x_shifted, 3)
            for b in range(B):
                normalise(acc, acc, b, 1e-5)
                dve.wait_ge(xh_ready, NT * 4 + CP * (b + 1))
                rows = slice(CP * b, CP * (b + 1))
                link(nc.vector.tensor_tensor(acc[:, rows, :], acc[:, rows, :], ffn_g_sb.unsqueeze(1).to_broadcast([P, CP, D]), ALU.mult))
                nc.vector.tensor_tensor(x_sb[:, rows, :], x_sb[:, rows, :], acc[:, rows, :], ALU.add).then_inc(out_ready, 1)

        @block.tensor
        def _(pe):
            pe.wait_ge(w_in, 16 * 12)
            for pair in range(NT // 2):
                pe.wait_ge(xh_ready, 2 * pair + 2)
                if pair >= 2:
                    pe.wait_ge(xt_ready, pair - 1)
                for k in range(KC):
                    for j in range(2):
                        last = nc.tensor.transpose(ps[:, 6 + pair % 2, 256 * k + P * j:256 * k + P * (j + 1)],
                                                   xh[:, 2 * pair + j, P * k:P * (k + 1)], ident[:, :])
                last.then_inc(xt_ps, 1)

            for c, (kind, m, n) in enumerate(proj):
                if c >= PB:
                    if proj[c - PB][0] == "v":
                        pe.wait_ge(v_ready, v_at.index(c - PB) + 1)
                    else:
                        pe.wait_ge(rest1, qk_at.index(c - PB) + 1)
                if c == 0:
                    pe.wait_ge(nat_ready, 4 * B)
                bank = ps[:, c % PB, :]
                if kind == "v":
                    for j in range(2):
                        t = S * m + P * (2 * n + j)
                        for k in range(KC):
                            last = nc.tensor.matmul(bank[:, D * j:D * (j + 1)], xt_nat[:, k, t:t + P], wv_sb[:, k, :],
                                                    start=(k == 0), stop=(k == KC - 1))
                else:
                    w, src = (wq_sb, xt_tile) if kind == "q" else (wk_sb, xt_nat)
                    for k in range(KC):
                        last = nc.tensor.matmul(bank, w[:, k, P * m:P * (m + 1)], src[:, k, 512 * n:512 * (n + 1)],
                                                start=(k == 0), stop=(k == KC - 1))
                last.then_inc(proj_ps, 1)
            pe.wait_ge(table_in, 16 * 8)
            pe.wait_ge(rest1, len(qk_at))
            pe.wait_ge(v_ready, len(v_at))

            def head_bounds(which):
                pe.wait_ge(bound_in, which + 1)
                for m in range(KC):
                    last = nc.tensor.matmul(ps[0:1, 7, 8 * m:8 * m + 8], size_prod[:, m:m + 1], head_rows,
                                            start=True, stop=True)
                last.then_inc(bound_ps, 1)

            def turn_maxima(maxima, into):
                for t in range(NT):
                    last = nc.tensor.transpose(ps[0:H, 4 + t // 4, P * (t % 4):P * (t % 4 + 1)], maxima[:, t, :], ident[:, :])
                last.then_inc(into, 1)

            pe.wait_ge(late_in, 16 * LATE_DMAS)
            head_bounds(0)
            with needed(nc.tensor, pe, 0):
                with pe.Fori(0, NG) as g:
                    for b in range(B):
                        pe.wait_ge(max_in[b], 16 * (NSTK - 1) * g + 16 * (NSTK - 1))
                        for h in range(HG):
                            for t in range(CP):
                                u = CP * (HG * b + h) + t
                                pe.wait_ge(max_read, B * HG * CP * g + (u + 1))
                                for half in range(2):
                                    last = nc.tensor.matmul(ps[:, 2 * (u % 2) + half, :], q_stk[b][0:96, h, P * t:P * (t + 1)],
                                                            k_stk[b][0:96, h, 512 * half:512 * (half + 1)], start=True, stop=True)
                                last.then_inc(max_ps, 1)
                pe.wait_ge(max_read, B * HG * CP * NG + 2)
                turn_maxima(row_max, max_tr)

            pe.sem_inc(p_free, 2)
            with pe.Fori(0, NG) as g:
                def scores(st, pair):
                    b, kt = divmod(st, NKT)
                    if kt == 0 and pair == 0:
                        pe.wait_ge(stk_in[b], 16 * NSTK * g + 16 * NSTK)
                    for h in range(2 * pair, 2 * pair + 2):
                        u = HG * st + h
                        pe.wait_ge(s_free, B * NKT * HG * g + (u + 1))
                        for half in range(2):
                            last = nc.tensor.matmul(ps[:, 2 * (u % 2) + half, :], k_stk[b][:, h, P * kt:P * (kt + 1)],
                                                    q_stk[b][:, h, 512 * half:512 * (half + 1)], start=True, stop=True)
                        last.then_inc(s_ready, 1)

                def bias(jt):
                    if jt == 0:
                        pe.wait_ge(dve_att, 4 * g + 1)
                        pe.wait_ge(vb_ready, 2 * g + 2)
                        pe.wait_ge(t_ready, g + 1)
                    for half in range(2):
                        for h in range(HG):
                            if half == 1:
                                last = nc.tensor.matmul(ps[32 * h:32 * h + 32, 7, 0:2],
                                                 v_bias[:, jt, h, :, :].rearrange("p b d -> p (b d)"), table[:, 0:2],
                                                 start=(jt == 0), stop=(jt == NKT - 1), tile_position=(0, 32 * h))
                                continue
                            start = 440 + 64 * h - 8 * jt
                            row = dims(t_grp[:, start:start + 1], [-P, 4], [1, P])
                            last = nc.tensor.matmul(ps[32 * h:32 * h + 32, 6 + half, :],
                                                    v_bias[:, jt, h, :, :].rearrange("p b d -> p (b d)"), row,
                                                    start=(jt == 0), stop=(jt == NKT - 1), tile_position=(0, 32 * h))
                    if jt == NKT - 1:
                        last.then_inc(bias_ps, 1)

                def values(st, half):
                    b, kt = divmod(st, NKT)
                    if kt == 0 and half == 0:
                        pe.wait_ge(vg_ready[b], g + 1)
                        pe.wait_ge(o_out, 2 * g + (b + 1))
                    if half == 0:
                        pe.wait_ge(s_free, B * NKT * HG * g + (HG * (st + 1) + 2))
                    for h in range(HG):
                        last = nc.tensor.matmul(ps[32 * h:32 * h + 32, 4 + half, :], v_grp[b][:, kt, h, :],
                                                probs[:, st % 2, h, 512 * half:512 * (half + 1)],
                                                start=(kt == 0), stop=(kt == NKT - 1), tile_position=(0, 32 * h))
                    if half == 1:
                        last.then_inc(p_free, 1)

                def turn(src):
                    for c in range(CP):
                        last = nc.tensor.transpose(ps[:, 6 + c // 4, P * (c % 4):P * (c % 4 + 1)],
                                                   src[:, P * c:P * (c + 1)], ident[:, :])
                    return last

                for st in range(B * NKT):
                    for half in range(2):
                        scores(st, half)
                        if st >= 1:
                            values(st - 1, half)
                    if st < NKT:
                        bias(st)
                    if st == NKT + 1:
                        pe.wait_ge(bias_out, g + 1)
                        turn(bias_t).then_inc(bias_tr, 1)
                    if st == NKT + 2:
                        pe.wait_ge(bias_read, g + 1)
                        pe.wait_ge(o_out, 2 * g + 2)
                        turn(o_t).then_inc(o_tr, 1)
                for half in range(2):
                    values(B * NKT - 1, half)
                pe.wait_ge(dve_att, 4 * g + 3)
                pe.wait_ge(o_out, 2 * g + 3)
                turn(o_t).then_inc(o_tr, 1)

            pe.wait_ge(late_in, 16 * LATE_DMAS)
            pe.wait_ge(att_done, NG)
            for b in range(B):
                for k in range(KC):
                    at = (CTX + 1) * (KC * b + k)
                    last = nc.tensor.transpose(ps[:, 0, at:at + CTX], ctx_sb[:, b, P * k:P * (k + 1)], ident[0:CTX, 0:CTX])
            last.then_inc(ctx_ps, 1)
            pe.wait_ge(ctx_ready, 1)
            for m in range(KC):
                for k in range(KC):
                    nc.tensor.matmul(ps[:, 1 + m, 0:B * CTX], xwk_sb[:, k, P * m:P * (m + 1)], ctx_t[:, :, k, 0:CTX],
                                     start=(k == 0), stop=(k == KC - 1))
            for b in range(B):
                for k in range(KC):
                    last = nc.tensor.matmul(ps[0:CTX + 1, 3, D * b:D * (b + 1)], ctx_t[:, b, k, :], xwv_sb[:, k, :],
                                            start=(k == 0), stop=(k == KC - 1))
            last.then_inc(kv2_ps, 1)
            pe.wait_ge(hide_ready, 1)
            for t in range(NT):
                bank = ps[0:CTX + 1, 4 + t // CP, :].bitcast(BF16)
                last = nc.tensor.transpose(bank[:, P * (t % CP):P * (t % CP + 1)], hide[:, t, :], ident_bf[:, :])
                if t % CP == CP - 1:
                    last.then_inc(hide_ps, 1)

            def turn_rows(src, done_ps, done_copy, first):
                for pair in range(NT // 2):
                    pe.wait_ge(xh_ready, first + 2 * pair + 2)
                    if pair >= 2:
                        pe.wait_ge(done_copy, pair - 1)
                    for k in range(KC):
                        for j in range(2):
                            last = nc.tensor.transpose(ps[:, 6 + pair % 2, 256 * k + P * j:256 * k + P * (j + 1)],
                                                       src[:, 2 * pair + j, P * k:P * (k + 1)], ident[:, :])
                    last.then_inc(done_ps, 1)

            turn_rows(xh, x2_ps, x2_ready, 2 * NT)
            pe.wait_ge(kv2_ready, 1)
            pe.wait_ge(hide_out, 1)
            for c in range(KC * 4):
                n, m = divmod(c, KC)
                pe.wait_ge(x2_ready, 2 * n + 2)
                if c >= 4:
                    pe.wait_ge(q2_ready, c - 3)
                for k in range(KC):
                    last = nc.tensor.matmul(ps[:, c % 4, :], xwq_sb[:, k, P * m:P * (m + 1)], x2_t[:, k, 512 * n:512 * (n + 1)],
                                            start=(k == 0), stop=(k == KC - 1))
                last.then_inc(q2_ps, 1)
            pe.wait_ge(q2_ready, KC * 4)
            pe.wait_ge(x2_ready, NT // 2)
            head_bounds(1)
            with needed(nc.tensor, pe, 1):
                for t in range(NT):
                    if t >= 1:
                        pe.wait_ge(max2_read, t)
                    for hg in range(NG):
                        last = nc.tensor.matmul(ps[:, hg, 0:HG * CTX], q2_t[:, hg // 2, P * t:P * (t + 1)],
                                                k2_pad[:, t // CP, HG * hg:HG * (hg + 1), 0:CTX], start=True, stop=True)
                    last.then_inc(max2_ps, 1)
                pe.wait_ge(max2_done, 1)
                turn_maxima(row_max2, max2_tr)
                pe.wait_ge(shift2_out, 48)
            pe.sem_inc(pv2_done, 2)
            with pe.Fori(0, 2) as i:
                def scores2(b, hg):
                    for pr in range(2):
                        u = 8 * b + 2 * hg + pr
                        pe.wait_ge(s2_free, 16 * i + (u + 1))
                        for hh in range(2):
                            h = HG * hg + 2 * pr + hh
                            bank = ps[0:CTX + 1, 2 * (u % 2) + hh, :]
                            nc.tensor.matmul(bank, k2_pad[:, b, h, :], q2_t[:, h // 8, bass.ds(512 * i + S * b, 512)],
                                             start=True, stop=False)
                            last = nc.tensor.matmul(bank, pick[:, h, :], hide_t[0:CTX + 1 + 3 * H, bass.ds(512 * i + S * b, 512)],
                                                    start=False, stop=True)
                        last.then_inc(s2_ready, 1)

                def values2(b, hg):
                    n = 4 * b + hg
                    pe.wait_ge(o2_out, 8 * i + (n + 1))
                    pe.wait_ge(s2_free, 16 * i + (8 * b + 2 * hg + 4))
                    for h in range(HG):
                        last = nc.tensor.matmul(ps[32 * h:32 * h + 32, 4 + hg % 2, :], v2_sb[:, b, HG * hg + h, :],
                                                probs2[:, hg % 2, h, :], start=True, stop=True, tile_position=(0, 32 * h))
                    last.then_inc(pv2_done, 1)

                def turn2(b, hg):
                    n = 4 * b + hg
                    pe.wait_ge(o2_out, 8 * i + (n + 3))
                    if n > 0:
                        pe.wait_ge(o2_div, 8 * i + n)
                    for t in range(4):
                        last = nc.tensor.transpose(ps[:, 6, P * t:P * (t + 1)], o2_tr[:, hg % 2, P * t:P * (t + 1)], ident[:, :])
                    last.then_inc(o2_tr_done, 1)

                for b in range(B):
                    for hg in range(NG):
                        scores2(b, hg)
                        if hg >= 1:
                            values2(b, hg - 1)
                            turn2(b, hg - 1)
                    values2(b, NG - 1)
                    turn2(b, NG - 1)
                    pe.wait_ge(o2_div, 8 * i + 4 * (b + 1))
                    for k in range(KC):
                        for t in range(4):
                            last = nc.tensor.transpose(ps[:, 6 + k, P * t:P * (t + 1)], o2[:, t, P * k:P * (k + 1)], ident[:, :])
                    last.then_inc(o2_ps, 1)
                    pe.wait_ge(o2t_ready, 2 * i + (b + 1))
                    for t in range(4):
                        for k in range(KC):
                            last = nc.tensor.matmul(ps[:, 4 + t // 2, D * (t % 2):D * (t % 2 + 1)], o2_t[:, k, P * t:P * (t + 1)],
                                                    xwu_sb[:, k, :], start=(k == 0), stop=(k == KC - 1))
                    last.then_inc(u_ps, 1)
                    pe.wait_ge(x2_added, 2 * i + (b + 1))
            turn_rows(xh, x3_ps, x3_ready, 3 * NT)
            pe.wait_ge(sgw_in, 32)
            for t in range(NT):
                pe.wait_ge(x3_ready, t // 2 + 1)
                if t >= 4:
                    pe.wait_ge(sg_read, t - 3)
                for k in range(KC):
                    last = nc.tensor.matmul(ps[:, t % 4, 0:D + EXPERTS], x3_t[:, k, P * t:P * (t + 1)], sgw_sb[:, k, :],
                                            start=(k == 0), stop=(k == KC - 1))
                last.then_inc(sg_ps, 1)
            pe.wait_ge(both_ready, 1)
            flat = both.rearrange("p t e -> p (t e)")
            nc.tensor.matmul(ps[:, 4, 0:P], before[:, :], flat, start=True, stop=False)
            for t in range(1, NT):
                nc.tensor.matmul(ps[:, 4, EXPERTS * t:P], ones[:, :], flat[:, 0:P - EXPERTS * t], start=False, stop=(t == NT - 1))
            for t in range(NT):
                last = nc.tensor.matmul(ps[:, 5, 0:EXPERTS], ones[:, :], both[:, t, :], start=(t == 0), stop=(t == NT - 1))
            last.then_inc(rank_ps, 1)

            def turn_tile(buf, n, ready=None):
                pe.wait_ge(xs_landed[buf], n)
                if ready is not None:
                    pe.wait_ge(xs_ready, ready)
                for k in range(KC):
                    last = nc.tensor.transpose(ps[:, 7, P * k:P * (k + 1)], xs_in[:, buf, P * k:P * (k + 1)], ident[:, :])
                last.then_inc(xs_ps, 1)

            def layer1(j, buf, ready, summed=None):
                e = nc.tensor.value_load(tile_expert[0:1, bass.ds(j, 1)], min_val=0, max_val=EXPERTS - 1)
                pe.wait_ge(xs_ready, ready)
                if summed is not None:
                    pe.wait_ge(h_sum, summed)
                for half in range(2):
                    for k in range(KC):
                        last = nc.tensor.matmul(ps[:, half, :], xs_t[:, buf, k, :],
                                                w1_sb[:, bass.ds(e, 1), k, 512 * half:512 * (half + 1)].squeeze(1),
                                                start=(k == 0), stop=(k == KC - 1))
                last.then_inc(h_ps, 1)

            def turn_hidden(n):
                pe.wait_ge(h_act, n)
                for k in range(HID // P):
                    last = nc.tensor.transpose(ps[:, 4 + k // 4, P * (k % 4):P * (k % 4 + 1)], hid[:, P * k:P * (k + 1)], ident[:, :])
                last.then_inc(ht_ps, 1)

            def layer2(j, n, taken=None):
                e = nc.tensor.value_load(tile_expert[0:1, bass.ds(j, 1)], min_val=0, max_val=EXPERTS - 1)
                pe.wait_ge(ht_ready, n)
                if taken is not None:
                    pe.wait_ge(y_ready, taken)
                for k in range(HID // P):
                    last = nc.tensor.matmul(ps[:, 6, 0:D], hid_t[:, k, :], w2_sb[:, bass.ds(e, 1), k, :].squeeze(1),
                                            start=(k == 0), stop=(k == HID // P - 1))
                last.then_inc(y_ps, 1)

            pe.wait_ge(w1_in, 16 * EXPERTS)
            pe.wait_ge(w2_in, 16 * EXPERTS)
            turn_tile(0, 16)
            layer1(0, 0, 1)
            turn_tile(1, 16, 1)
            turn_hidden(1)
            layer1(1, 1, 2, 1)
            turn_tile(0, 32, 2)
            layer2(0, 1)
            with pe.Fori(0, (SLOT_TILES - 3) // 2) as i:
                for o in range(2):
                    turn_hidden(2 * i + (o + 2))
                    layer1(2 * i + (o + 2), o, 2 * i + (o + 3), 2 * i + (o + 2))
                    turn_tile(1 - o, 16 * i + (32 + 16 * o), 2 * i + (3 + o))
                    layer2(2 * i + (o + 1), 2 * i + (o + 2), 2 * i + (o + 1))
            turn_hidden(SLOT_TILES - 1)
            layer1(SLOT_TILES - 1, 0, SLOT_TILES, SLOT_TILES - 1)
            layer2(SLOT_TILES - 2, SLOT_TILES - 1, SLOT_TILES - 2)
            turn_hidden(SLOT_TILES)
            layer2(SLOT_TILES - 1, SLOT_TILES, SLOT_TILES - 1)


_INS = ["x", "ctx_1024", "mask_BxSxS2_ik1", "L0_attn_Wq", "L0_attn_Wk", "L0_attn_Wv", "L0_attn_rel_table",
        "L0_attn_gamma", "L0_attn_beta", "L0_xattn_Wq", "L0_xattn_Wk", "L0_xattn_Wv", "L0_xattn_Wu", "L0_xattn_bu",
        "L0_ffn_W1", "L0_ffn_b1", "L0_ffn_W2", "L0_ffn_b2", "L0_ffn_gate_W", "L0_ffn_shared_W", "L0_ffn_shared_b",
        "L0_ffn_gamma", "L0_ffn_beta"]


def constants():
    bf16 = mybir.dt.np(BF16)
    p = np.arange(P)
    e = np.arange(EXPERTS)
    c = {"ident": np.eye(P, dtype=np.float32), "ident_bf": np.eye(P).astype(bf16)}
    pick = np.zeros((CTX + 1 + 3 * H, H, CTX + 1))
    pick[:CTX + 1] = np.eye(CTX + 1)[:, None, :]
    for n in range(3):
        for h in range(H):
            pick[CTX + 1 + H * n + h, h, :CTX] = 1
    c["pick"] = pick.astype(bf16)
    c["head_rows"] = (p[:, None] // DH == np.arange(8)[None, :]).astype(np.float32)
    c["counts"] = np.r_[np.ones(CTX), CTX].astype(np.float32)[:, None].repeat(2, 1)
    c["before"] = (p[:, None] < p[None, :]).astype(bf16)
    c["ones"] = np.ones((P, P)).astype(bf16)
    thresholds = np.tile(P * np.arange(NT), (EXPERTS, 1))
    tiles = np.tile(np.arange(SLOT_TILES)[:, None], (1, EXPERTS))
    row = np.concatenate([thresholds.ravel(), EXPERTS - e, (e[None, :] < e[:, None]).ravel(), tiles.ravel()])
    c["route_c"] = np.tile(row.astype(np.float32), (P, 1))
    return c


def kernel(**inputs):
    import concourse.bacc as bacc
    from concourse.bass_utils import run_bass_kernel_spmd

    nc = bacc.Bacc("TRN2", target_bir_lowering=False, num_devices=1)
    arrays, args = {}, []

    def give(name, a):
        a = np.ascontiguousarray(a)
        arrays[name] = a
        return nc.dram_tensor(name, a.shape, mybir.dt.from_np(a.dtype), kind="ExternalInput").ap()

    for name in _INS:
        a = np.asarray(inputs[name])
        if name == "L0_attn_rel_table":
            a = a[::-1].T
        if name in ("L0_xattn_Wq", "L0_xattn_Wk", "L0_xattn_Wv"):
            a = a.transpose(1, 0, 2).reshape(D, D)
        args.append(give("in_" + name, a))
    consts = {k: give("const_" + k, v) for k, v in constants().items()}
    out = nc.dram_tensor("out_0_dram", (B, S, D), F32, kind="ExternalOutput").ap()
    decoder_layer(nc, *args, consts, out)
    r = run_bass_kernel_spmd(nc, [arrays], core_ids=[0])
    return r.results[0]["out_0_dram"]
```

```python
from contextlib import ExitStack

import numpy as np

import concourse.bass as bass
from concourse import mybir

F32 = mybir.dt.float32
BF16 = mybir.dt.bfloat16
I32 = mybir.dt.int32
U32 = mybir.dt.uint32
ALU = mybir.AluOpType
ACT = mybir.ActivationFunctionType
AX = mybir.AxisListType

P = 128
B, S, D, H = 2, 1024, 256, 16
DH = D // H
NT = B * S // P
CP = S // P
KC = D // P
HG = 4
NG = H // HG
NKT = S // P
RELS = 511
TW = 2 * S - 8
TG = 8 * (NKT - 1) + P * 3 + 64 * (HG - 1) + P
T0 = TW - RELS
STK = 6 * DH + 3
NSTK = 13
CTX = 77
BOUND = 64.0
NEG = -float(2 ** 100)
EXPERTS, HID = 8, 1024
SLOT_TILES = 2 * NT + EXPERTS - 1


REGION_TILES = 2 * 1024 // P
ROW_TILES = EXPERTS * REGION_TILES + SLOT_TILES - 2 * NT
NEWTON = 3
PAIR_LINKS = 6 + 2 * (3 + 3 * NEWTON)
VARYING = (0, 0, 2, 4)
CHUNK = 4
ARENA = 651 * 64
LATE_DMAS = 4 + 1 + 2 * B + 6 + 7
W2_AT, SGW_AT, X_AT, ACC_AT = (n * 256 for n in (256, 520, 529, 587))


def dims(ap, *free):
    return bass.AP(ap.tensor, ap.offset, [list(ap.ap[0])] + [list(f) for f in free])


def decoder_layer(nc, x, ctx_in, mask, wq, wk, wv, rel_rows, attn_g, attn_b, xwq, xwk, xwv, xwu, xbu,
                  w1, b1, w2, b2, gate_w, shared_w, shared_b, ffn_g, ffn_b, consts, out):
    scope = ExitStack()

    def sb(name, shape, dt=F32):
        return scope.enter_context(nc.sbuf_tensor(name, shape, dt))

    def sem(name):
        return scope.enter_context(nc.semaphore(name))

    with scope:
        qs_dram = nc.dram_tensor("q_parts", [B, 3, D, S], BF16).ap()
        ks_dram = nc.dram_tensor("k_parts", [B, 3, D, S], BF16).ap()
        xs_dram = nc.dram_tensor("rows_by_expert", [ROW_TILES * P, D], F32).ap()
        ys_dram = nc.dram_tensor("results_by_expert", [SLOT_TILES * P, D], F32).ap()
        shift_dram = nc.dram_tensor("shift_parts", [B, 3, H, S], BF16).ap()

        x_sb = sb("x_sb", [P, NT, D])
        xh = sb("xh", [P, NT, D])
        ident = sb("ident", [P, P])
        stats = sb("stats", [P, NT, 6])
        mv = sb("mv", [P, NT, 2])
        rstd = sb("rstd", [P, NT])
        root_s, root_t = sb("root_s", [P, CP]), sb("root_t", [P, CP])

        rows_sb = sb("rows_sb", [P, 6, D])
        attn_g_sb, attn_b_sb, xbu_sb, shared_b_sb, ffn_g_sb, ffn_b_sb = (rows_sb[:, i, :] for i in range(6))
        slot = sb("slot", [P, 2, NT], U32)
        slot_y = sb("slot_y", [P, 2, NT], U32)
        weight = sb("weight", [P, 2, NT])
        route_c = sb("route_c", [P, EXPERTS * (NT + 1 + EXPERTS + 1 + SLOT_TILES)])
        before = sb("before", [P, P], BF16)
        ones = sb("ones", [P, P], BF16)
        tile_expert = sb("tile_expert", [P, SLOT_TILES], I32)
        tile_row = sb("tile_row", [P, SLOT_TILES], I32)
        seen = sb("seen", [P, EXPERTS])
        seen_bf = sb("seen_bf", [P, EXPERTS], BF16)
        over = sb("over", [P, NT])
        ident_bf = sb("ident_bf", [P, P], BF16)
        sizes = sb("sizes", [P, KC, 2, 4])[:, :, :, :]
        size = sb("size", [P, KC, 2])[:, :, :]
        size_prod = sb("size_prod", [P, KC])[:, :]
        head_bound = sb("head_bound", [1, H])[:, :]
        most = sb("most", [1, 2])[:, :]
        flags = sb("flags", [1, 1 + B], I32)[:, :]
        small = [P, CHUNK, EXPERTS]
        picks = sb("picks", [P, 2, NT, EXPERTS])
        place_f = sb("place_f", [P, 2, NT])
        delta = sb("delta", [P, EXPERTS])[:, :]
        both = sb("both", small, BF16)[:, :, :]
        top1, top2, best = (sb(n, [P, CHUNK])[:, :] for n in ("top1", "top2", "best"))
        both_n = sb("both_n", [P, EXPERTS])[:, :]
        tiles_of, base, ends = (sb(n, [P, EXPERTS])[:, :] for n in ("tiles_of", "base", "ends"))
        over_one = sb("over_one", [P, NT])
        head_rows = sb("head_rows", [P, 8])[:, :]
        counts = sb("counts", [CTX + 1, 2])[:, :]
        hide_max = sb("hide_max", [P, NT])
        k2_size = sb("k2_size", [P, KC])
        pair_stats, pair_mv, pair_r = sb("pair_stats", [P, 2, 6]), sb("pair_mv", [P, 2, 2]), sb("pair_r", [P, 2])
        arena = sb("arena", [P, ARENA])
        ended = arena[:, SGW_AT // 4:SGW_AT // 4 + SLOT_TILES * EXPERTS].rearrange("p (j e) -> p j e", e=EXPERTS)
        moved = arena[:, SGW_AT // 4:SGW_AT // 4 + 2 * NT * EXPERTS].rearrange("p (t e) -> p t e", e=EXPERTS)
        move = arena[:, SGW_AT // 4 + 2 * NT * EXPERTS:SGW_AT // 4 + 2 * NT * (EXPERTS + 1)]
        ended_x = arena[:, X_AT // 4:X_AT // 4 + SLOT_TILES * EXPERTS].rearrange("p (j e) -> p j e", e=EXPERTS)
        full = arena[:, X_AT // 4 + 512:X_AT // 4 + 512 + EXPERTS * NT].rearrange("p (e j) -> p e j", e=EXPERTS)
        ended_n, ended_w, rowf = (arena[:, X_AT // 4 + 768 + 64 * n:X_AT // 4 + 768 + 64 * n + SLOT_TILES] for n in range(3))

        class Region:

            def __init__(self, at):
                self.at = at // 4

            def take(self, shape, dt=F32):
                n = int(np.prod(shape[1:])) * mybir.dt.size(dt) // 4
                ap = arena[0:shape[0], self.at:self.at + n]
                self.at += n
                assert self.at <= ARENA, self.at
                ap = ap if dt == F32 else ap.bitcast(dt)
                names = "abcde"[:len(shape) - 1]
                sizes = dict(zip(names, shape[1:]))
                return ap.rearrange(f"p ({' '.join(names)}) -> p {' '.join(names)}", **sizes)

        r = Region(0)
        wq_sb, wk_sb, wv_sb = (r.take([P, KC, D]) for _ in range(3))
        table = r.take([P, TW])
        t_grp = r.take([P, TG])
        table_end = 4 * r.at
        last_row = r.take([P, 2])
        v_sb = r.take([P, B, NKT, D])
        v_grp = [r.take([P, NKT, HG, 32]) for _ in range(B)]
        v_bias = r.take([P, NKT, HG, B, DH])
        q_stk = [None, r.take([P, HG, S], BF16)[0:STK]]
        rest = r.take([P, 4, 512])
        rest_end = r.at
        r.at -= 4 * 512
        o_t, bias_t = r.take([P, S]), r.take([P, 512 + P])
        rden = r.take([P, CP, HG])
        o_n = r.take([P, CP, HG, DH])
        assert 4 * max(r.at, rest_end) <= W2_AT
        r = Region(W2_AT)
        probs = r.take([P, 2, HG, S])
        xt = probs.rearrange("p a h s -> p (a h s)")
        xt_tile = xt[:, 0:KC * B * S].rearrange("p (k n) -> p k n", k=KC)
        xt_nat = xt[:, KC * B * S:2 * KC * B * S].rearrange("p (k n) -> p k n", k=KC)
        k_stk = [None, r.take([P, HG, S], BF16)[0:STK]]
        q_stk[0], k_stk[0] = (r.take([P, HG, S], BF16)[0:STK] for _ in range(2))
        parts_at = 4 * r.at
        parts = r.take([P, 4, 3, 512], BF16)
        assert 4 * r.at <= X_AT

        row_max = xt[:, 0:NT * H].rearrange("p (t h) -> p t h", h=H)
        neg_max = rest.rearrange("p a n -> p (a n)")[0:H]
        neg_parts = parts.rearrange("p a c n -> p (a c n)").rearrange("p (c n) -> p c n", c=3)[0:H]

        r = Region(X_AT)
        xwq_sb, xwu_sb = (r.take([P, KC, D]) for _ in range(2))
        pick = r.take([P, H, CTX + 1], BF16)[0:CTX + 1 + 3 * H]
        hide_t = r.take([P, B * S], BF16)
        v2_sb = r.take([P, B, H, 32])[0:CTX + 1]
        assert 4 * r.at <= ACC_AT
        r = Region(ACC_AT)
        xwk_sb, xwv_sb = (r.take([P, KC, D]) for _ in range(2))
        ctx_sb = r.take([P, B, D])[0:CTX]
        mask_sb = r.take([P, NT, CTX], I32)
        zeros = r.take([P, D])
        ctx_t = r.take([P, B, KC, CTX + 1])
        hide = r.take([P, NT, CTX + 1], BF16)
        assert 4 * ACC_AT // 4 + 12 * 1024 <= 4 * r.at <= ACC_AT + 16384
        k2_pad = Region(parts_at).take([P, B, H, CTX + 1])

        r = Region(W2_AT)
        probs2 = r.take([P, 2, HG, 512])[0:CTX + 1]
        q2_t = [None, r.take([P, KC, S])]
        o2_tr = r.take([P, 2, 512])
        o2 = r.take([P, CHUNK, D])
        o2_t = r.take([P, KC, 512])
        rden2 = r.take([P, CHUNK, HG])
        r = Region(parts_at - 16384)
        x3_t = r.take([P, KC, 512])
        logits, hit, cand, lg2, pos = (r.take([P, CHUNK, EXPERTS]) for _ in range(5))
        r = Region(0)
        q2_t[0] = r.take([P, KC, S])
        x2_t = r.take([P, KC, 512])
        pair_rows = r.take([P, 2, D])
        assert 4 * r.at <= table_end
        r = Region(W2_AT)
        hidden_s = r.take([P, H, CTX])
        row_max2 = r.take([P, CP, H])
        neg_max2 = r.take([P, S])[0:H]
        neg_parts2 = r.take([P, 3, S], BF16)[0:H]
        assert 4 * r.at <= W2_AT + 16384

        w1_sb = Region(0).take([P, EXPERTS, KC, HID])
        w2_sb = Region(W2_AT).take([P, EXPERTS, HID // P, D])
        acc = Region(ACC_AT).take([P, NT, D])
        sgw_sb = Region(SGW_AT).take([P, KC, D + EXPERTS])
        r = Region(X_AT)
        xs_in = r.take([P, 2, D])
        xs_t = r.take([P, 2, KC, P])
        y_sb = r.take([P, 2, D])
        b2_row = r.take([P, 2, D])
        y_in = r.take([P, 2, 2, D])
        assert 4 * r.at <= ACC_AT
        xh_flat = xh[:, :, :].rearrange("p t f -> p (t f)")
        b1_row = xh_flat[:, 0:2 * HID].rearrange("p (a n) -> p a n", a=2)
        hid = xh_flat[:, 2 * HID:3 * HID]
        hid_t = xh_flat[:, 3 * HID:4 * HID].rearrange("p (k n) -> p k n", k=HID // P)

        ps = scope.enter_context(nc.psum_tensor("ps", [P, 8, 512], F32))

        x_in = [sem(f"x_in{b}") for b in range(B)]
        w_in, table_fill, table_in = sem("w_in"), sem("table_fill"), sem("table_in")
        ln_var, ln_std, dve_link = sem("ln_var"), sem("ln_std"), sem("dve_link")
        xh_ready, xt_ps, xt_ready, nat_ready = sem("xh_ready"), sem("xt_ps"), sem("xt_ready"), sem("nat_ready")
        proj_ps, part0, rest1, part1, part2 = (sem(n) for n in ("proj_ps", "part0", "rest1", "part1", "part2"))
        v_ready = sem("v_ready")
        parts_out = [sem(f"parts_out{i}") for i in range(4)]
        zero_rows, zero_out = sem("zero_rows"), sem("zero_out")
        stk_in = [sem(f"stk_in{b}") for b in range(B)]
        ones_set = sem("ones_set")
        vg_ready, vb_ready, t_ready = sem("vg_ready"), sem("vb_ready"), sem("t_ready")
        s_ready, s_free, p_free = sem("s_ready"), sem("s_free"), sem("p_free")
        bias_ps, bias_out, bias_tr = sem("bias_ps"), sem("bias_out"), sem("bias_tr")
        o_out, o_tr, bias_read, dve_att = sem("o_out"), sem("o_tr"), sem("bias_read"), sem("dve_att")
        att_done = sem("att_done")
        bound_in, bound_ps, flag_set = sem("bound_in"), sem("bound_ps"), sem("flag_set")
        max_in = [sem(f"max_in{b}") for b in range(B)]
        max_ps, max_read, max_done, max_tr, max_split, shift_out, dve_max = (sem(n) for n in (
            "max_ps", "max_read", "max_done", "max_tr", "max_split", "shift_out", "dve_max"))
        max2_ps, max2_read, max2_done, max2_tr, max2_split, shift2_out, dve_max2 = ([sem(f"{n}{b}") for b in range(B)] for n in (
            "max2_ps", "max2_read", "max2_done", "max2_tr", "max2_split", "shift2_out", "dve_max2"))
        late_in, zeros_set, xs_zero = sem("late_in"), sem("zeros_set"), sem("xs_zero")
        x_shifted = sem("x_shifted")
        x2_ps, x2_ready, q2_ps, q2_ready = sem("x2_ps"), sem("x2_ready"), sem("q2_ps"), sem("q2_ready")
        ctx_ps, ctx_ready, kv2_ps, kv2_ready = sem("ctx_ps"), sem("ctx_ready"), sem("kv2_ps"), sem("kv2_ready")
        hide_ready, hide_ps, hide_out = sem("hide_ready"), sem("hide_ps"), sem("hide_out")
        s2_ready, s2_free, pv2_done, o2_out = sem("s2_ready"), sem("s2_free"), sem("pv2_done"), sem("o2_out")
        o2_tr_done, o2_div, dve_pair, work_zero, pool_link = sem("o2_tr_done"), sem("o2_div"), sem("dve_pair"), sem("work_zero"), sem("pool_link")
        gate_ps, gate_read, seen_ready, slot_ready, count_ps, sh_added, moved_ready = (sem(n) for n in (
            "gate_ps", "gate_read", "seen_ready", "slot_ready", "count_ps", "sh_added", "moved_ready"))
        o2_ps, o2t_ready, u_ps, x2_added = sem("o2_ps"), sem("o2t_ready"), sem("u_ps"), sem("x2_added")
        w1_in, w2_in, sgw_in = sem("w1_in"), sem("w2_in"), sem("sgw_in")
        x3_ps, x3_ready, sg_ps, sg_read, sg_act, halved = (sem(n) for n in (
            "x3_ps", "x3_ready", "sg_ps", "sg_read", "sg_act", "halved"))
        pair_ready, both_ready, rank_ps, rank_read = (sem(n) for n in ("pair_ready", "both_ready", "rank_ps", "rank_read"))
        route_done, scattered = sem("route_done"), sem("scattered")
        xs_landed = [sem(f"xs_landed{i}") for i in range(2)]
        b1_landed = [sem(f"b1_landed{i}") for i in range(2)]
        b2_landed = [sem(f"b2_landed{i}") for i in range(2)]
        xs_ps, xs_ready, h_ps, h_sum, h_act, ht_ps, ht_ready, y_ps, y_ready = (sem(n) for n in (
            "xs_ps", "xs_ready", "h_ps", "h_sum", "h_act", "ht_ps", "ht_ready", "y_ps", "y_ready"))
        y_stored = [sem(f"y_stored{i}") for i in range(2)]
        y_landed = [sem(f"y_landed{i}") for i in range(2)]
        y_used, out_ready, out_done = sem("y_used"), sem("out_ready"), sem("out_done")

        proj = ([("k", 0, n) for n in range(4)] + [("q", 0, n) for n in range(4)]
                + [("v", b, n) for b in range(B) for n in range(4)]
                + [("k", 1, n) for n in range(4)] + [("q", 1, n) for n in range(4)])
        qk_at = [c for c, (kind, _, _) in enumerate(proj) if kind != "v"]
        v_at = [c for c, (kind, _, _) in enumerate(proj) if kind == "v"]
        PB = 6

        block = scope.enter_context(nc.Block())

        def needed(on, eng, which):
            eng.wait_ge(flag_set, which + 1)
            flag = on.alloc_register(f"flag_{which}_{on.engine.name}")
            on.reg_load(flag, flags[0:1, which:which + 1])
            return eng.If_ne(flag, 0)

        @block.sync
        def _(sp):
            for b in range(B):
                rows = x[b].rearrange("(a c o) f -> o a c f", c=CP, o=2)
                for o in range(2):
                    sp.dma_start(x_sb[64 * (1 - o):64 * (2 - o), CP * b:CP * (b + 1), :], rows[o]).then_inc(x_in[b], 16)
            sp.dma_start(ident[:, :], consts["ident"]).then_inc(w_in, 16)
            for dst, src in ((wk_sb, wk), (wq_sb, wq), (wv_sb, wv)):
                sp.dma_start(dst[:, :, :], src.rearrange("(k p) n -> p k n", p=P)).then_inc(w_in, 16)
            for r in range(8):
                sp.dma_start(last_row[16 * r:16 * r + 16, 0:1], rel_rows[:, 0:1],
                             allow_slow_non_contiguous=True).then_inc(w_in, 16)
            sp.wait_ge(table_fill, 1)
            for r in range(8):
                sp.dma_start(table[16 * r:16 * r + 16, T0 + r:TW], rel_rows[:, 0:RELS - r]).then_inc(table_in, 16)
            for dst, src in ((xwq_sb, xwq), (xwk_sb, xwk), (xwv_sb, xwv), (xwu_sb, xwu)):
                sp.dma_start(dst, src.rearrange("(k p) n -> p k n", p=P)).then_inc(late_in, 16)
            sp.dma_start(ctx_sb, ctx_in.rearrange("b t d -> t b d")).then_inc(late_in, 16)
            for b in range(B):
                rows = mask[b].rearrange("(a c o) t -> o a c t", c=CP, o=2)
                for o in range(2):
                    sp.dma_start(mask_sb[64 * (1 - o):64 * (2 - o), CP * b:CP * (b + 1), :], rows[o]).then_inc(late_in, 16)
            for i, row in enumerate((attn_g, attn_b, xbu, shared_b, ffn_g, ffn_b)):
                sp.dma_start(rows_sb[:, i, :], row.partition_broadcast(P)).then_inc(late_in, 16)
            for dst, name in ((pick, "pick"), (head_rows, "head_rows"), (counts, "counts"), (ident_bf[:, :], "ident_bf"),
                              (before[:, :], "before"), (ones[:, :], "ones"), (route_c[:, :], "route_c")):
                sp.dma_start(dst, consts[name]).then_inc(late_in, 16)
            sp.wait_ge(zero_rows, 1)
            for b in range(B):
                sp.dma_start(shift_dram[b].rearrange("c h s -> (c h) s"),
                             rest[0:48, 0, :].bitcast(BF16)).then_inc(zero_out, 16)
            for q, c in enumerate(qk_at):
                kind, m, n = proj[c]
                dst = (qs_dram if kind == "q" else ks_dram)[n // 2, :, P * m:P * (m + 1), 512 * (n % 2):512 * (n % 2 + 1)]
                sp.wait_ge(part2, q + 1)
                sp.dma_start(dst.rearrange("c p n -> p c n"), parts[:, q % 4, :, :]).then_inc(parts_out[q % 4], 16)
            for i in range(4):
                sp.wait_ge(parts_out[i], 16 * (len(qk_at) // 4))
            sp.wait_ge(zero_out, 32)
            sp.wait_ge(ones_set, 1)

            def load_parts(g, b, landed, buf):
                for blk in range(6):
                    for stk, src, part in ((k_stk[buf], ks_dram, (0, 1, 2, 0, 1, 0)[blk]),
                                           (q_stk[buf], qs_dram, (0, 0, 0, 1, 1, 2)[blk])):
                        rows = src[b, part, bass.ds(64 * g, 64), :].rearrange("(h d) s -> d h s", h=HG)
                        sp.dma_start(stk[16 * blk:16 * blk + 16, :, :], rows).then_inc(landed, 16)

            with needed(nc.sync, sp, 0):
                with sp.Fori(0, NG) as g:
                    sp.wait_ge(max_read, B * HG * CP * g + 2)
                    for b in range(B):
                        load_parts(g, b, max_in[b], b)
                sp.wait_ge(max_read, B * HG * CP * NG + 2)
                sp.wait_ge(max_split, 1)
                for b in range(B):
                    sp.dma_start(shift_dram[b].rearrange("c h s -> h c s"), neg_parts[:, :, S * b:S * (b + 1)])\
                        .then_inc(shift_out, 16)
                sp.wait_ge(shift_out, 16 * B)

            def load_group(b, g, buf):
                load_parts(g, b, stk_in[buf], buf)
                sp.dma_start(q_stk[buf][96:99, :, :], shift_dram[b, :, bass.ds(HG * g, HG), :]).then_inc(stk_in[buf], 16)

            sp.wait_ge(zeros_set, 1)
            for g in range(NG):
                if g >= 2:
                    sp.wait_ge(s_free, NKT * HG * (g - 1) + 2)
                load_group(0, g, g % 2)
                if g >= 1:
                    for part in range(3 * g - 3, 3 * g):
                        n = ROW_TILES // 9
                        rows = xs_dram[n * P * part:n * P * (part + 1), :].rearrange("(t p) f -> p t f", p=P)
                        sp.dma_start(rows, zeros.unsqueeze(1).to_broadcast([P, n, D])).then_inc(xs_zero, 16)
            with sp.Fori(0, NG // 2) as i:
                for o in range(2):
                    g = sp.snap(2 * i + o, min_val=0, max_val=NG - 1)
                    sp.wait_ge(s_free, 2 * NKT * HG * i + (NKT * HG * (NG + o - 1) + 2))
                    load_group(1, g, o)

            def load_w1(e):
                sp.dma_start(w1_sb[:, e], w1[e].rearrange("(k p) n -> p k n", p=P)).then_inc(w1_in, 16)

            sp.wait_ge(att_done, B * NG)
            sp.dma_start(sgw_sb[:, :, 0:D], shared_w.rearrange("(k p) n -> p k n", p=P)).then_inc(sgw_in, 16)
            sp.dma_start(sgw_sb[:, :, D:D + EXPERTS], gate_w.rearrange("(k p) n -> p k n", p=P)).then_inc(sgw_in, 16)
            for e in range(2, EXPERTS):
                load_w1(e)
            for b in range(B):
                with needed(nc.sync, sp, 1 + b):
                    sp.wait_ge(max2_split[b], 1)
                    for c in range(3):
                        at = CTX + 1 + H * c
                        sp.dma_start(hide_t[at:at + H, S * b:S * (b + 1)], neg_parts2[:, c, :]).then_inc(shift2_out[b], 16)
            sp.wait_ge(s2_free, 16)
            for e in range(2):
                load_w1(e)
            sp.wait_ge(x2_added, NT // 2)
            for e in range(EXPERTS):
                if e == 5:
                    sp.wait_ge(sg_ps, NT // 2)
                    sp.wait_ge(slot_ready, NT // CHUNK)
                sp.dma_start(w2_sb[:, e], w2[e].rearrange("(k p) n -> p k n", p=P)).then_inc(w2_in, 16)

            def expert(j):
                return nc.sync.value_load(tile_expert[0:1, bass.ds(j, 1)], min_val=0, max_val=EXPERTS - 1)

            def slots_of(j):
                return bass.ds(nc.sync.value_load(tile_row[0:1, bass.ds(j, 1)], min_val=0, max_val=ROW_TILES - 1) * P, P)

            def load_rows(slots, buf):
                sp.dma_start(xs_in[:, buf, :], xs_dram[slots, :]).then_inc(xs_landed[buf], 16)

            def load_b1(e, buf):
                sp.dma_start(b1_row[:, buf, :], b1[bass.ds(e, 1), :].partition_broadcast(P)).then_inc(b1_landed[buf], 16)

            def load_b2(e, buf):
                sp.dma_start(b2_row[:, buf, :], b2[bass.ds(e, 1), :].partition_broadcast(P)).then_inc(b2_landed[buf], 16)

            def step(j, buf, rows=True, b2_too=True):
                if rows:
                    slots, e = slots_of(j + 2), expert(j + 2)
                    sp.wait_ge(xs_ps, j + 1)
                    load_rows(slots, buf)
                    sp.wait_ge(h_sum, j + 1)
                    load_b1(e, buf)
                if b2_too:
                    e = expert(j + 1)
                sp.wait_ge(y_ready, j)
                sp.dma_start(ys_dram[bass.ds((j - 1) * P, P), :], y_sb[:, 1 - buf, :]).then_inc(y_stored[1 - buf], 16)
                if b2_too:
                    load_b2(e, 1 - buf)

            sp.wait_ge(scattered, 16 * 2 * NT)
            sp.wait_ge(route_done, 1)
            for j in range(2):
                load_rows(slots_of(j), j)
                load_b1(expert(j), j)
                load_b2(expert(j), j)
            sp.wait_ge(xs_ps, 1)
            load_rows(slots_of(2), 0)
            sp.wait_ge(h_sum, 1)
            load_b1(expert(2), 0)
            with sp.Fori(0, (SLOT_TILES - 3) // 2) as i:
                for o in range(2):
                    step(2 * i + (o + 1), 1 - o)
            for j in range(SLOT_TILES - 2, SLOT_TILES + 1):
                step(j, j % 2, False, j + 1 < SLOT_TILES)
            out_rows = out.rearrange("b (a c o) f -> b o a c f", c=CP, o=2)
            for b in range(B):
                sp.wait_ge(out_ready, b + 1)
                for o in range(2):
                    sp.dma_start(out_rows[b, o], x_sb[64 * (1 - o):64 * (2 - o), CP * b:CP * (b + 1), :]).then_inc(out_done, 16)
            sp.wait_ge(out_done, 16 * 2 * B)

        @block.gpsimd
        def _(pool):
            nc.gpsimd.memset(zeros, 0.0).then_inc(zeros_set, 1)
            nc.gpsimd.memset(seen[:, :], 0.0)
            nc.gpsimd.memset(seen_bf[:, :], 0.0).then_inc(seen_ready, 1)
            for buf in range(2):
                nc.gpsimd.memset(v_grp[buf][:, :, :, DH:DH + 1], 1.0)
                nc.gpsimd.memset(v_grp[buf][:, :, :, DH + 1:32], 0.0).then_inc(pool_link, 1)
            pool.wait_ge(pool_link, 2)
            nc.gpsimd.memset(hide_t[64:P, :], 0.0).then_inc(pool_link, 1)
            pool.wait_ge(pool_link, 3)
            nc.gpsimd.memset(v2_sb, 0.0)
            pool.wait_ge(late_in, 16 * LATE_DMAS)
            pool.wait_ge(xh_ready, NT)
            nc.gpsimd.tensor_tensor(x_sb[:, :, :], x_sb[:, :, :], attn_b_sb.unsqueeze(1).to_broadcast([P, NT, D]),
                                    ALU.add).then_inc(x_shifted, 1)

            def values_of(b, g):
                return v_sb[:, b, :, 64 * g:64 * (g + 1)].rearrange("p t (h d) -> p t h d", h=HG)

            pool.wait_ge(v_ready, len(v_at))
            pool.wait_ge(table_in, 16 * 8)
            for b in range(B):
                for g in range(NG):
                    n = NG * b + g
                    if n >= 2:
                        pool.wait_ge(p_free, NKT * (n - 1) + 2)
                    nc.gpsimd.tensor_copy(v_grp[n % 2][:, :, :, 0:DH], values_of(b, g)).then_inc(vg_ready, 1)
                    if b == 0:
                        if g >= 1:
                            pool.wait_ge(bias_ps, g)
                        if g >= 2:
                            nc.gpsimd.tensor_copy(t_grp[:, :], table[:, 512 + 64 * HG * g:512 + 64 * HG * g + TG])
                        for c in range(B):
                            last = nc.gpsimd.tensor_copy(v_bias[:, :, :, c, :], values_of(c, g))
                        last.then_inc(vb_ready, 1)
                    if n == 0:
                        for i in range(2):
                            pool.wait_ge(stk_in[i], 16 * NSTK)
                        nc.gpsimd.memset(k2_pad, 0.0).then_inc(work_zero, 1)

            def shift_batch(b, row):
                rows = x_sb[:, CP * b:CP * (b + 1), :]
                return nc.gpsimd.tensor_tensor(rows, rows, row.unsqueeze(1).to_broadcast([P, CP, D]), ALU.add)

            for b in range(B):
                pool.wait_ge(xh_ready, NT + CP * (b + 1))
                shift_batch(b, xbu_sb).then_inc(x_shifted, 1)
            pool.wait_ge(xs_zero, 16 * 9)
            for ch in range(NT // CHUNK):
                pool.wait_ge(slot_ready, ch + 1)
                for t in range(CHUNK * ch, CHUNK * (ch + 1)):
                    for k in range(2):
                        nc.gpsimd.indirect_dma_start(
                            out=xs_dram, out_offset=bass.IndirectOffsetOnAxis(ap=slot[:, k, t:t + 1], axis=0),
                            in_=xh[:, t, :], in_offset=None).then_inc(scattered, 16)
                pool.wait_ge(sg_read, 2 * (ch + 1))
                rows = acc[:, CHUNK * ch:CHUNK * (ch + 1), :]
                nc.gpsimd.tensor_tensor(rows, rows, shared_b_sb.unsqueeze(1).to_broadcast([P, CHUNK, D]), ALU.add)\
                    .then_inc(sh_added, 1)
            pool.wait_ge(sg_act, NT // 4)
            nc.gpsimd.tensor_scalar(acc, acc, 0.5, None, ALU.mult).then_inc(halved, 1)
            nc.gpsimd.tensor_tensor(x_sb[:, :, :], x_sb[:, :, :], ffn_b_sb.unsqueeze(1).to_broadcast([P, NT, D]),
                                    ALU.add).then_inc(x_shifted, 1)
            pool.wait_ge(moved_ready, 1)
            for i in range(2):
                pool.wait_ge(y_stored[i], 16 * ((SLOT_TILES + 1 - i) // 2))
            for t in range(NT):
                if t >= 2:
                    pool.wait_ge(y_used, t - 1)
                for k in range(2):
                    nc.gpsimd.indirect_dma_start(
                        out=y_in[:, t % 2, k, :], out_offset=None, in_=ys_dram,
                        in_offset=bass.IndirectOffsetOnAxis(ap=slot_y[:, k, t:t + 1], axis=0)).then_inc(y_landed[t % 2], 16)

        @block.scalar
        def _(act):
            n_sqrt = [0]

            def sqrt_of_var(b):
                n_sqrt[0] += 1
                act.wait_ge(ln_var, n_sqrt[0])
                r = rstd[:, CP * b:CP * (b + 1)]
                nc.scalar.activation(r, r, ACT.Sqrt).then_inc(ln_std, 1)

            for b in range(B):
                sqrt_of_var(b)
            for b in range(B):
                act.wait_ge(xt_ready, CP // 2 * (b + 1))
                for k in range(KC):
                    for o in range(2):
                        src = xt_tile[:, k, S * b + 64 * (1 - o):S * b + 64 * (1 - o) + 1]
                        dst = xt_nat[:, k, S * b + o:S * b + o + 1]
                        nc.scalar.copy(dims(dst, [2, CP], [16, 64]), dims(src, [P, CP], [1, 64])).then_inc(nat_ready, 1)

            def first_part(q):
                act.wait_ge(proj_ps, qk_at[q] + 1)
                if q >= 4:
                    act.wait_ge(parts_out[q % 4], 16 * (q // 4))
                nc.scalar.copy(parts[:, q % 4, 0, :], ps[:, qk_at[q] % PB, :]).then_inc(part0, 1)

            def second_part(q):
                act.wait_ge(rest1, q + 1)
                nc.scalar.copy(parts[:, q % 4, 1, :], rest[:, q % 4, :]).then_inc(part1, 1)

            for c, (kind, m, n) in enumerate(proj):
                if kind == "v":
                    act.wait_ge(proj_ps, c + 1)
                    nc.scalar.copy(v_sb[:, m, 2 * n:2 * n + 2, :],
                                   ps[:, c % PB, :].rearrange("p (t f) -> p t f", t=2)).then_inc(v_ready, 1)
                else:
                    q = qk_at.index(c)
                    first_part(q)
                    if q >= 1:
                        second_part(q - 1)
            second_part(len(qk_at) - 1)

            act.sem_inc(s_free, 2)
            with act.Fori(0, B * NG) as g:
                for st in range(NKT):
                    for h in range(HG):
                        u = HG * st + h
                        if h == 0:
                            act.wait_ge(p_free, NKT * g + (st + 1))
                        act.wait_ge(s_ready, NKT * HG * g + (u + 1))
                        nc.scalar.activation(probs[:, st % 2, h, :],
                                             ps[:, 2 * (u % 2):2 * (u % 2) + 2, :].rearrange("p a n -> p (a n)"),
                                             ACT.Exp, scale=float(D) ** -0.5).then_inc(s_free, 1)

            def turned_outputs(ch):
                for k in range(KC):
                    act.wait_ge(o2_ps, KC * ch + k + 1)
                    nc.scalar.copy(o2_t[:, k, :], ps[:, 6 + k, :]).then_inc(o2t_ready, 1)

            def turned_rows3(ch):
                for p in range(2):
                    act.wait_ge(x3_ps, 2 * ch + p + 1)
                    nc.scalar.copy(x3_t[:, :, 256 * p:256 * (p + 1)],
                                   ps[:, 6 + p, :].rearrange("p (k n) -> p k n", k=KC)).then_inc(x3_ready, 1)

            def shared_results(ch):
                if ch == 0:
                    act.wait_ge(xs_zero, 16 * 9)
                for p in range(2):
                    act.wait_ge(sg_ps, 2 * ch + p + 1)
                    t = CHUNK * ch + 2 * p
                    nc.scalar.copy(acc[:, t:t + 2, :], ps[:, 7 - p, :].rearrange("p (t f) -> p t f", t=2)).then_inc(sg_read, 1)

            for ch in range(NT // CHUNK):
                b, i = divmod(ch, 2)
                if i == 0:
                    with needed(nc.scalar, act, 1 + b):
                        act.wait_ge(shift2_out[b], 48)
                for hg in range(NG):
                    for pr in range(2):
                        u = 8 * ch + 2 * hg + pr
                        act.wait_ge(s2_ready, u + 1)
                        if pr == 0 and NG * ch + hg >= 2:
                            act.wait_ge(pv2_done, NG * ch + hg - 1)
                        nc.scalar.activation(probs2[:, hg % 2, 2 * pr:2 * pr + 2, :], ps[0:CTX + 1, 2 * (u % 2):2 * (u % 2) + 2, :],
                                             ACT.Exp, scale=float(DH) ** -0.5).then_inc(s2_free, 1)
                        if ch >= 1 and (hg, pr) == (0, 0):
                            turned_outputs(ch - 1)
                        if ch >= 1 and (hg, pr) == (3, 0):
                            turned_rows3(ch - 1)
                if ch >= 1:
                    shared_results(ch - 1)
                if b == 0:
                    for m in range(KC):
                        act.wait_ge(q2_ps, NG + KC * i + m + 1)
                        nc.scalar.copy(q2_t[1][:, m, 512 * i:512 * (i + 1)], ps[:, 6 + m, :]).then_inc(q2_ready, 1)
            turned_outputs(3)
            turned_rows3(3)
            shared_results(3)
            act.wait_ge(both_ready, NT // CHUNK)
            nc.scalar.activation(over[:, :], over[:, :], ACT.Exp).then_inc(pair_ready, 1)
            for q in range(NT // 4):
                act.wait_ge(sh_added, q + 1)
                nc.scalar.activation(acc[:, 4 * q:4 * q + 4, :], acc[:, 4 * q:4 * q + 4, :], ACT.Gelu).then_inc(sg_act, 1)
            def turned_rows(j, buf, n):
                act.wait_ge(xs_ps, n)
                nc.scalar.copy(xs_t[:, buf, :, :], ps[:, 7, 0:KC * P].rearrange("p (k n) -> p k n", k=KC)).then_inc(xs_ready, 1)

            def activate(n):
                act.wait_ge(h_sum, n)
                nc.scalar.activation(hid, hid, ACT.Gelu).then_inc(h_act, 1)

            turned_rows(0, 0, 1)
            turned_rows(1, 1, 2)
            activate(1)
            with act.Fori(0, (SLOT_TILES - 3) // 2) as i:
                for o in range(2):
                    turned_rows(2 * i + (o + 2), o, 2 * i + (o + 3))
                    activate(2 * i + (o + 2))
            for j in range(SLOT_TILES - 2, SLOT_TILES):
                if j + 1 < SLOT_TILES:
                    turned_rows(j + 1, (j + 1) % 2, j + 2)
                activate(j + 1)
            for b in range(B):
                sqrt_of_var(b)

        @block.vector
        def _(dve):
            links = [0]

            def link(ins):
                links[0] += 1
                ins.then_inc(dve_link, 1)
                dve.wait_ge(dve_link, links[0])

            n_ln = [0]

            def inverse_root(r, v, eps, n, link):
                s, t = root_s[:, 0:n], root_t[:, 0:n]
                link(nc.vector.tensor_scalar(s, v, eps, None, ALU.add))
                link(nc.vector.tensor_scalar(t.bitcast(I32), s.bitcast(I32), 1, None, ALU.logical_shift_right))
                link(nc.vector.tensor_scalar(r.bitcast(I32), t.bitcast(I32), -1.0, float(0x5F3759DF), ALU.mult, ALU.add))
                for _ in range(NEWTON):
                    link(nc.vector.scalar_tensor_tensor(out=t, in0=r, scalar=-0.5, in1=s, op0=ALU.mult, op1=ALU.mult))
                    link(nc.vector.tensor_tensor(t, t, r, ALU.mult))
                    link(nc.vector.scalar_tensor_tensor(out=r, in0=t, scalar=1.5, in1=r, op0=ALU.add, op1=ALU.mult))

            def normalise(src, dst, b, eps):
                for t in range(CP * b, CP * (b + 1)):
                    last = nc.vector.bn_stats(stats[:, t, :], src[:, t, :])
                link(last)
                for t in range(CP * b, CP * (b + 1)):
                    last = nc.vector.bn_aggr(mv[:, t, :], stats[:, t, :])
                link(last)
                r = rstd[:, CP * b:CP * (b + 1)]
                nc.vector.tensor_scalar(r, mv[:, CP * b:CP * (b + 1), 1], eps, None, ALU.add).then_inc(ln_var, 1)
                n_ln[0] += 1
                dve.wait_ge(ln_std, n_ln[0])
                link(nc.vector.reciprocal(r, r))
                for t in range(CP * b, CP * (b + 1)):
                    last = nc.vector.tensor_scalar(dst[:, t, :], src[:, t, :], mv[:, t, 0:1], rstd[:, t:t + 1],
                                                   ALU.subtract, ALU.mult)
                    last.then_inc(xh_ready, 1)

            nc.vector.memset(rest[0:48, 0, :], 0.0).then_inc(zero_rows, 1)
            for b in range(B):
                dve.wait_ge(x_in[b], 32)
                normalise(x_sb, xh, b, 1e-5)
            dve.wait_ge(w_in, 16 * 12)
            nc.vector.tensor_copy(table[:, 0:T0 + 8], last_row[:, 0:1].to_broadcast([P, T0 + 8])).then_inc(table_fill, 1)
            for pair in range(NT // 2):
                dve.wait_ge(xt_ps, pair + 1)
                nc.vector.tensor_copy(xt_tile[:, :, 2 * P * pair:2 * P * (pair + 1)],
                                      ps[:, 6 + pair % 2, :].rearrange("p (k n) -> p k n", k=KC)).then_inc(xt_ready, 1)
            nc.vector.memset(k_stk[0][96:99, :, :], 1.0)
            nc.vector.memset(k_stk[1][96:99, :, :], 1.0).then_inc(ones_set, 1)
            dve.wait_ge(zero_out, 32)

            def first_rest(q):
                dve.wait_ge(part0, q + 1)
                nc.vector.tensor_tensor(rest[:, q % 4, :], ps[:, qk_at[q] % PB, :], parts[:, q % 4, 0, :],
                                        ALU.subtract).then_inc(rest1, 1)

            def third_part(q):
                dve.wait_ge(part1, q + 1)
                nc.vector.tensor_tensor(parts[:, q % 4, 2, :], rest[:, q % 4, :], parts[:, q % 4, 1, :],
                                        ALU.subtract).then_inc(part2, 1)

            def largest(q):
                kind, m, n = proj[qk_at[q]]
                nc.vector.tensor_reduce(sizes[:, m, "qk".index(kind), n:n + 1], parts[:, q % 4, 0, :], AX.X, ALU.max, apply_absolute_value=True)

            for q in range(len(qk_at)):
                first_rest(q)
                largest(q)
                if q >= 1:
                    third_part(q - 1)
            third_part(len(qk_at) - 1)

            def bound(scale, which, linked):
                nc.vector.tensor_tensor(size_prod, size[:, :, 0], size[:, :, 1], ALU.mult).then_inc(bound_in, 1)
                dve.wait_ge(bound_ps, which + 1)
                linked(nc.vector.tensor_copy(head_bound, ps[0:1, 7, 0:H]))
                linked(nc.vector.tensor_reduce(most[:, 0:1], head_bound, AX.X, ALU.max))
                nc.vector.tensor_scalar(flags[:, which:which + 1], most[:, 0:1], BOUND / scale, None, ALU.is_gt)\
                    .then_inc(flag_set, 1)

            dve.wait_ge(part2, len(qk_at))
            link(nc.vector.tensor_reduce(size, sizes, AX.X, ALU.max))
            bound(float(D) ** -0.5, 0, link)

            def link_on(s):
                n = [0]

                def linked(ins):
                    n[0] += 1
                    ins.then_inc(s, 1)
                    dve.wait_ge(s, n[0])
                return linked

            def negated_parts(rows, banks, into, linked, done):
                linked(nc.vector.tensor_scalar(rows, ps[0:H, 4:4 + banks, :].rearrange("p a n -> p (a n)"), -1.0, None, ALU.mult))
                linked(nc.vector.tensor_copy(into[:, 0, :], rows))
                linked(nc.vector.tensor_tensor(rows, rows, into[:, 0, :], ALU.subtract))
                linked(nc.vector.tensor_copy(into[:, 1, :], rows))
                nc.vector.tensor_tensor(into[:, 2, :], rows, into[:, 1, :], ALU.subtract).then_inc(done, 1)

            with needed(nc.vector, dve, 0):
                dve.sem_inc(max_read, 2)
                with dve.Fori(0, NG) as g:
                    for b in range(B):
                        for h in range(HG):
                            for t in range(CP):
                                u = CP * (HG * b + h) + t
                                dve.wait_ge(max_ps, B * HG * CP * g + (u + 1))
                                nc.vector.tensor_reduce(row_max[:, CP * b + t, bass.ds(HG * g + h, 1)],
                                                        ps[:, 2 * (u % 2):2 * (u % 2) + 2, :].rearrange("p a n -> p (a n)"),
                                                        AX.X, ALU.max).then_inc(max_read, 1)
                dve.wait_ge(max_tr, 1)
                for i in range(4):
                    dve.wait_ge(parts_out[i], 16 * (len(qk_at) // 4))
                negated_parts(neg_max, 4, neg_parts, link_on(dve_max), max_split)

            dve.sem_inc(dve_att, 1)
            dve.sem_inc(o_out, 1)

            def heads_of(b, g):
                return xh[:, CP * b:CP * (b + 1), bass.ds(64 * g, 64)].rearrange("p t (h d) -> p t h d", h=HG)

            turned = ps[:, 6:8, :].rearrange("p a (c h e) -> p (a c) h e", c=4, h=HG)

            def group_outputs(b, g):
                n = NG * b + g
                dve.wait_ge(p_free, NKT * n + (NKT + 2))
                nc.vector.tensor_copy(o_t[:, :], ps[:, 4:6, :].rearrange("p a n -> p (a n)")).then_inc(o_out, 1)
                dve.wait_ge(o_tr, n + 1)
                nc.vector.reciprocal(rden[:, :, :], turned[:, :, :, DH]).then_inc(dve_att, 1)
                dve.wait_ge(dve_att, 2 * n + 2)
                nc.vector.tensor_tensor(o_n[:, :, :, :], turned[:, :, :, 0:DH],
                                        rden[:, :, :].unsqueeze(3).to_broadcast([P, CP, HG, DH]), ALU.mult).then_inc(dve_att, 1)
                dve.wait_ge(dve_att, 2 * n + 3)
                nc.vector.tensor_tensor(heads_of(b, g), heads_of(b, g), o_n[:, :, :, :], ALU.add).then_inc(att_done, 1)

            dve.wait_ge(ctx_ps, 1)
            link(nc.vector.tensor_copy(ctx_t[:, :, :, 0:CTX], ps[:, 6, 0:B * KC * (CTX + 1)].rearrange(
                "p (b k t) -> p b k t", b=B, k=KC)[:, :, :, 0:CTX]))
            nc.vector.tensor_reduce(ctx_t[:, :, :, CTX:CTX + 1], ctx_t[:, :, :, 0:CTX], AX.X, ALU.add).then_inc(ctx_ready, 1)
            dve.wait_ge(work_zero, 1)
            nc.vector.tensor_copy(v2_sb[:, :, :, DH], counts[:, 0:1].unsqueeze(2).to_broadcast([CTX + 1, B, H]))
            link(nc.vector.tensor_scalar(hide[:, :, 0:CTX], mask_sb, 0.0, NEG, ALU.is_equal, ALU.mult))
            link(nc.vector.tensor_reduce(hide_max[:, :], hide[:, :, 0:CTX], AX.X, ALU.max))
            nc.vector.tensor_scalar(hide[:, :, CTX], hide_max[:, :], -1.0, NEG, ALU.mult, ALU.add).then_inc(hide_ready, 1)
            dve.wait_ge(kv2_ps, 1)
            nc.vector.tensor_reduce(k2_size[:, :], ps[:, 6, 0:KC * B * CTX].rearrange("p (m n) -> p m n", m=KC),
                                    AX.X, ALU.max, apply_absolute_value=True)
            for m in range(KC):
                for j in range(H // KC):
                    last = nc.vector.tensor_scalar(k2_pad[:, :, H // KC * m + j, 0:CTX],
                                                   ps[:, 6, B * CTX * m:B * CTX * (m + 1)].rearrange("p (b t) -> p b t", b=B),
                                                   head_rows[:, j:j + 1], None, ALU.mult)
            last.then_inc(kv2_ready, 1)
            dve.wait_ge(kv2_ps, 2)
            nc.vector.tensor_copy(v2_sb[:, :, :, 0:DH], ps[0:CTX + 1, 6, :].rearrange("p (b h d) -> p b h d", b=B, h=H))\
                .then_inc(kv2_ready, 1)
            for i in range(2):
                dve.wait_ge(hide_ps, i + 1)
                nc.vector.tensor_copy(hide_t[0:CTX + 1, S * i:S * (i + 1)], ps[0:CTX + 1, 6, :].bitcast(BF16)).then_inc(hide_out, 1)

            for g in range(NG):
                nv = VARYING[g]
                dve.wait_ge(bias_ps, g + 1)
                if nv:
                    nc.vector.tensor_copy(bias_t[:, 0:P * nv], ps[:, 6, 0:P * nv])
                nc.vector.tensor_copy(bias_t[:, P * nv:P * (nv + 1)], ps[:, 7, 0:1].to_broadcast([P, P])).then_inc(bias_out, 1)
                dve.wait_ge(bias_tr, g + 1)
                for b in range(B):
                    if nv:
                        nc.vector.tensor_copy(heads_of(b, g)[:, 0:nv],
                                              ps[:, 6, 0:P * nv].rearrange("p (c h b d) -> p c h b d", c=nv, h=HG, b=B)[:, :, :, b, :])
                    const = ps[:, 7, 0:P].rearrange("p (h b d) -> p h b d", h=HG, b=B)[:, :, b, :]
                    last = nc.vector.tensor_copy(heads_of(b, g)[:, nv:CP], const.unsqueeze(1).to_broadcast([P, CP - nv, HG, DH]))
                last.then_inc(bias_read, 1)
                group_outputs(0, g)

            with dve.Fori(0, NG) as g:
                n = [0]

                def link_pair(ins):
                    n[0] += 1
                    ins.then_inc(dve_pair, 1)
                    dve.wait_ge(dve_pair, PAIR_LINKS * g + n[0])

                def tile(t, j):
                    return t[:, bass.ds(2 * g + j, 1), :].squeeze(1)

                def moments(src, eps):
                    nc.vector.memset(root_s[:, 0:2], 0.0)
                    for j in range(2):
                        last = nc.vector.bn_stats(pair_stats[:, j, :], tile(src, j))
                    link_pair(last)
                    nc.vector.memset(root_s[:, 0:2], 0.0)
                    for j in range(2):
                        last = nc.vector.bn_aggr(pair_mv[:, j, :], pair_stats[:, j, :])
                    link_pair(last)
                    inverse_root(pair_r[:, 0:2], pair_mv[:, :, 1], eps, 2, link_pair)

                dve.wait_ge(att_done, g + NG)
                dve.wait_ge(x_shifted, 1)
                moments(xh, 1e-3)
                for j in range(2):
                    last = nc.vector.scalar_tensor_tensor(out=tile(xh, j), in0=tile(xh, j), scalar=pair_mv[:, j, 0:1],
                                                          in1=attn_g_sb, op0=ALU.subtract, op1=ALU.mult)
                link_pair(last)
                for j in range(2):
                    last = nc.vector.scalar_tensor_tensor(out=tile(x_sb, j), in0=tile(xh, j), scalar=pair_r[:, j:j + 1],
                                                          in1=tile(x_sb, j), op0=ALU.mult, op1=ALU.add)
                link_pair(last)
                moments(x_sb, 1e-5)
                for j in range(2):
                    nc.vector.tensor_scalar(pair_rows[:, j, :], tile(x_sb, j), pair_mv[:, j, 0:1], pair_r[:, j:j + 1],
                                            ALU.subtract, ALU.mult).then_inc(xh_ready, 1)
                assert n[0] == PAIR_LINKS
                dve.wait_ge(x2_ps, g + 1)
                nc.vector.tensor_copy(x2_t[:, :, 0:256], ps[:, 6, :].rearrange("p (k n) -> p k n", k=KC)).then_inc(x2_ready, 1)
                dve.wait_ge(q2_ps, g + 1)
                pair_q = ps[:, 7, :].rearrange("p (m n) -> p m n", m=KC)
                nc.vector.tensor_reduce(sizes[:, :, 0, bass.ds(g, 1)], pair_q, AX.X, ALU.max, apply_absolute_value=True)
                nc.vector.tensor_copy(q2_t[0][:, :, bass.ds(256 * g, 256)], pair_q).then_inc(q2_ready, 1)
                group_outputs(1, g)

            def cross_bound(b, n):
                link(nc.vector.tensor_reduce(size[:, :, 0], sizes[:, :, 0, 0:n], AX.X, ALU.max))
                link(nc.vector.tensor_copy(size[:, :, 1], k2_size[:, :]))
                bound(float(DH) ** -0.5, 1 + b, link)
                with needed(nc.vector, dve, 1 + b):
                    linked = link_on(dve_max2[b])
                    for t in range(CP):
                        dve.wait_ge(max2_ps[b], t + 1)
                        ins = nc.vector.tensor_tensor(hidden_s.rearrange("p (g h) t -> p g h t", g=NG),
                                                      ps[:, 0:NG, 0:HG * CTX].rearrange("p g (h t) -> p g h t", h=HG),
                                                      hide[:, CP * b + t, 0:CTX].unsqueeze(1).unsqueeze(1).to_broadcast([P, NG, HG, CTX]),
                                                      ALU.add)
                        linked(ins)
                        dve.sem_inc(max2_read[b], 1)
                        linked(nc.vector.tensor_reduce(row_max2[:, t, :], hidden_s, AX.X, ALU.max))
                    nc.vector.tensor_scalar(row_max2, row_max2, -float(2 ** 90), None, ALU.max).then_inc(max2_done[b], 1)
                    dve.wait_ge(max2_tr[b], 1)
                    negated_parts(neg_max2, 2, neg_parts2, linked, max2_split[b])

            second = range(CP, NT)

            def second_batch(stage):
                if stage in (0, 2):
                    src = (xh, x_sb)[stage // 2]
                    if stage == 0:
                        dve.wait_ge(att_done, B * NG)
                    for t in second:
                        last = nc.vector.bn_stats(stats[:, t, :], src[:, t, :])
                    link(last)
                    for t in second:
                        last = nc.vector.bn_aggr(mv[:, t, :], stats[:, t, :])
                    link(last)
                    inverse_root(rstd[:, CP:NT], mv[:, CP:NT, 1], (1e-3, 1e-5)[stage // 2], CP, link)
                elif stage == 1:
                    for t in second:
                        last = nc.vector.scalar_tensor_tensor(out=xh[:, t, :], in0=xh[:, t, :], scalar=mv[:, t, 0:1],
                                                              in1=attn_g_sb, op0=ALU.subtract, op1=ALU.mult)
                    link(last)
                    for t in second:
                        last = nc.vector.scalar_tensor_tensor(out=x_sb[:, t, :], in0=xh[:, t, :], scalar=rstd[:, t:t + 1],
                                                              in1=x_sb[:, t, :], op0=ALU.mult, op1=ALU.add)
                    link(last)
                else:
                    for t in second:
                        nc.vector.tensor_scalar(xh[:, t, :], x_sb[:, t, :], mv[:, t, 0:1], rstd[:, t:t + 1],
                                                ALU.subtract, ALU.mult).then_inc(xh_ready, 1)

            def second_columns(i):
                for p in range(2):
                    dve.wait_ge(x2_ps, NG + 2 * i + p + 1)
                    nc.vector.tensor_copy(x2_t[:, :, 256 * p:256 * (p + 1)],
                                          ps[:, 6 + p, :].rearrange("p (k n) -> p k n", k=KC)).then_inc(x2_ready, 1)
                dve.wait_ge(q2_ready, NG + KC * (i + 1))
                link(nc.vector.tensor_reduce(sizes[:, :, 0, i:i + 1], q2_t[1][:, :, 512 * i:512 * (i + 1)], AX.X, ALU.max,
                                             apply_absolute_value=True))

            def leave(n):
                if n >= 2:
                    dve.wait_ge(o2_tr_done, n - 1)
                dve.wait_ge(pv2_done, n + 1)
                nc.vector.tensor_copy(o2_tr[:, n % 2, :], ps[:, 4, :]).then_inc(o2_out, 1)

            def divide(n):
                hg = n % NG
                dve.wait_ge(o2_tr_done, n + 1)
                turned2 = ps[:, 5, :].rearrange("p (t h e) -> p t h e", t=CHUNK, h=HG)
                link(nc.vector.reciprocal(rden2, turned2[:, :, :, DH]))
                nc.vector.tensor_tensor(o2[:, :, 64 * hg:64 * (hg + 1)].rearrange("p t (h d) -> p t h d", h=HG),
                                        turned2[:, :, :, 0:DH],
                                        rden2.unsqueeze(3).to_broadcast([P, CHUNK, HG, DH]), ALU.mult).then_inc(o2_div, 1)

            def add_cross(ch):
                dve.wait_ge(x_shifted, 2 + ch // 2)
                for p in range(2):
                    dve.wait_ge(u_ps, 2 * ch + p + 1)
                    xs = x_sb[:, CHUNK * ch + 2 * p:CHUNK * ch + 2 * p + 2, :]
                    nc.vector.tensor_tensor(xs, ps[:, 6 + p, :].rearrange("p (t f) -> p t f", t=2), xs, ALU.add).then_inc(x2_added, 1)
                dve.wait_ge(x2_added, 2 * ch + 2)
                tiles = range(CHUNK * ch, CHUNK * (ch + 1))
                for t in tiles:
                    last = nc.vector.bn_stats(stats[:, t, :], x_sb[:, t, :])
                link(last)
                for t in tiles:
                    last = nc.vector.bn_aggr(mv[:, t, :], stats[:, t, :])
                link(last)
                rows = slice(CHUNK * ch, CHUNK * (ch + 1))
                inverse_root(rstd[:, rows], mv[:, rows, 1], 1e-5, CHUNK, link)

            def normalise3(ch):
                for t in range(CHUNK * ch, CHUNK * (ch + 1)):
                    nc.vector.tensor_scalar(xh[:, t, :], x_sb[:, t, :], mv[:, t, 0:1], rstd[:, t:t + 1],
                                            ALU.subtract, ALU.mult).then_inc(xh_ready, 1)

            e_names = [P, CHUNK, EXPERTS]
            at = [EXPERTS * NT, EXPERTS, EXPERTS * EXPERTS, EXPERTS]
            at = [0] + [sum(at[:n + 1]) for n in range(4)]
            thresholds, rev, tri, region, tiles_c = (route_c[:, a:b] for a, b in zip(at, at[1:] + [at[-1] + SLOT_TILES * EXPERTS]))
            thresholds = thresholds.rearrange("p (e j) -> p e j", e=EXPERTS)
            tri = tri.rearrange("p (e f) -> p e f", e=EXPERTS)
            tiles_c = tiles_c.rearrange("p (j e) -> p j e", e=EXPERTS)

            def first_largest(values, top, picked):
                link(nc.vector.tensor_reduce(top, values, AX.X, ALU.max))
                link(nc.vector.tensor_tensor(hit, values, top.unsqueeze(2).to_broadcast(e_names), ALU.is_equal))
                link(nc.vector.tensor_tensor(cand, hit, rev.unsqueeze(1).to_broadcast(e_names), ALU.mult))
                link(nc.vector.tensor_reduce(best, cand, AX.X, ALU.max))
                link(nc.vector.tensor_tensor(picked, cand, best.unsqueeze(2).to_broadcast(e_names), ALU.is_equal))

            def choose(ch):
                dve.wait_ge(gate_ps, ch + 1)
                link(nc.vector.tensor_copy(logits, ps[:, 6, 0:CHUNK * EXPERTS].rearrange("p (t e) -> p t e", t=CHUNK)))
                dve.sem_inc(gate_read, 1)
                pick1, pick2 = (picks[:, k, CHUNK * ch:CHUNK * (ch + 1), :] for k in range(2))
                first_largest(logits, top1, pick1)
                link(nc.vector.scalar_tensor_tensor(out=lg2, in0=pick1, scalar=NEG, in1=logits, op0=ALU.mult, op1=ALU.add))
                first_largest(lg2, top2, pick2)
                nc.vector.tensor_tensor(over[:, CHUNK * ch:CHUNK * (ch + 1)], top2, top1, ALU.subtract)
                nc.vector.tensor_tensor(both, pick1, pick2, ALU.add).then_inc(both_ready, 1)

            def place(ch):
                dve.wait_ge(rank_ps, ch + 1)
                link(nc.vector.tensor_tensor(pos, ps[:, 7, 0:CHUNK * EXPERTS].rearrange("p (t e) -> p t e", e=EXPERTS),
                                             region.unsqueeze(1).to_broadcast(e_names), ALU.add))
                dve.sem_inc(rank_read, 1)
                rows = slice(CHUNK * ch, CHUNK * (ch + 1))
                for k in range(2):
                    link(nc.vector.tensor_tensor(hit, picks[:, k, rows, :], pos, ALU.mult))
                    link(nc.vector.tensor_reduce(place_f[:, k, rows], hit, AX.X, ALU.add))
                nc.vector.tensor_copy(slot[:, :, rows], place_f[:, :, rows]).then_inc(slot_ready, 1)
                link(nc.vector.tensor_reduce(both_n, both.rearrange("p t e -> p e t"), AX.X, ALU.add))
                link(nc.vector.tensor_tensor(seen[:, :], seen[:, :], both_n, ALU.add))
                nc.vector.tensor_copy(seen_bf[:, :], seen[:, :]).then_inc(seen_ready, 1)

            dve.wait_ge(seen_ready, 1)
            cross_bound(0, NG)
            for ch in range(NT // CHUNK):
                b, i = divmod(ch, 2)
                n = NG * ch
                if ch == 2:
                    cross_bound(1, 2)
                if ch == 0:
                    second_batch(0)
                    leave(n)
                    second_batch(1)
                    divide(n)
                    leave(n + 1)
                    second_batch(2)
                    divide(n + 1)
                    leave(n + 2)
                    second_batch(3)
                else:
                    add_cross(ch - 1)
                    leave(n)
                    normalise3(ch - 1)
                    divide(n)
                    leave(n + 1)
                    divide(n + 1)
                    choose(ch - 1)
                    leave(n + 2)
                divide(n + 2)
                if ch >= 1:
                    place(ch - 1)
                leave(n + 3)
                divide(n + 3)
                if b == 0:
                    second_columns(i)
            add_cross(3)
            normalise3(3)
            choose(3)
            place(3)
            dve.wait_ge(count_ps, 1)
            link(nc.vector.tensor_tensor(full, thresholds, ps[:, 6, 0:EXPERTS].unsqueeze(2).to_broadcast([P, EXPERTS, NT]), ALU.is_lt))
            link(nc.vector.tensor_reduce(tiles_of, full, AX.X, ALU.add))
            link(nc.vector.tensor_tensor(full[:, :, 0:EXPERTS], tri, tiles_of.unsqueeze(1).to_broadcast([P, EXPERTS, EXPERTS]),
                                         ALU.mult))
            link(nc.vector.tensor_reduce(base, full[:, :, 0:EXPERTS], AX.X, ALU.add))
            link(nc.vector.tensor_tensor(ends, base, tiles_of, ALU.add))
            by_tile = [P, SLOT_TILES, EXPERTS]
            link(nc.vector.tensor_tensor(ended, ends.unsqueeze(1).to_broadcast(by_tile), tiles_c, ALU.is_le))
            nc.vector.tensor_reduce(ended_n, ended, AX.X, ALU.add)
            link(nc.vector.tensor_tensor(ended_x, ended, tiles_of.unsqueeze(1).to_broadcast(by_tile), ALU.mult))
            link(nc.vector.tensor_reduce(ended_w, ended_x, AX.X, ALU.add))
            link(nc.vector.tensor_tensor(rowf, tiles_c[:, :, 0], ended_w, ALU.subtract))
            nc.vector.tensor_scalar(tile_expert[:, :], ended_n, EXPERTS - 1.0, None, ALU.min)
            nc.vector.scalar_tensor_tensor(out=tile_row[:, :], in0=ended_n, scalar=float(REGION_TILES), in1=rowf,
                                           op0=ALU.mult, op1=ALU.add).then_inc(route_done, 1)
            link(nc.vector.scalar_tensor_tensor(out=delta, in0=base, scalar=float(P), in1=region, op0=ALU.mult, op1=ALU.subtract))
            link(nc.vector.tensor_tensor(moved, picks[:, :, :, :].rearrange("p k t e -> p (k t) e"),
                                         delta.unsqueeze(1).to_broadcast([P, 2 * NT, EXPERTS]), ALU.mult))
            link(nc.vector.tensor_reduce(move, moved, AX.X, ALU.add))
            nc.vector.tensor_tensor(slot_y[:, :, :].rearrange("p k t -> p (k t)"), move,
                                    place_f[:, :, :].rearrange("p k t -> p (k t)"), ALU.add).then_inc(moved_ready, 1)
            dve.wait_ge(pair_ready, 1)
            link(nc.vector.tensor_scalar(over_one[:, :], over[:, :], 1.0, None, ALU.add))
            link(nc.vector.reciprocal(weight[:, 0, :], over_one[:, :]))
            link(nc.vector.tensor_tensor(weight[:, 1, :], over[:, :], weight[:, 0, :], ALU.mult))

            def sum_hidden(buf, n, nb):
                dve.wait_ge(h_ps, n)
                dve.wait_ge(b1_landed[buf], nb)
                nc.vector.tensor_tensor(hid, ps[:, 0:2, :].rearrange("p a n -> p (a n)"), b1_row[:, buf, :],
                                        ALU.add).then_inc(h_sum, 1)

            def turned_hidden(n):
                dve.wait_ge(ht_ps, n)
                nc.vector.tensor_copy(hid_t, ps[:, 4:6, :].rearrange("p a (k n) -> p (a k) n", n=P)).then_inc(ht_ready, 1)

            def result(buf, n, landed, stored=None):
                dve.wait_ge(y_ps, n)
                dve.wait_ge(b2_landed[buf], landed)
                if stored is not None:
                    dve.wait_ge(y_stored[buf], stored)
                nc.vector.tensor_tensor(y_sb[:, buf, :], ps[:, 6, 0:D], b2_row[:, buf, :], ALU.add).then_inc(y_ready, 1)

            sum_hidden(0, 1, 16)
            turned_hidden(1)
            sum_hidden(1, 2, 16)
            result(0, 1, 16)
            turned_hidden(2)
            sum_hidden(0, 3, 32)
            result(1, 2, 16)
            with dve.Fori(1, (SLOT_TILES - 1) // 2 - 1) as i:
                for o in range(2):
                    turned_hidden(2 * i + (o + 1))
                    sum_hidden(1 - o, 2 * i + (o + 2), 16 * i + 16 * (1 + o))
                    result(o, 2 * i + (o + 1), 16 * i + 16, 16 * i)
            for j in range(SLOT_TILES - 2, SLOT_TILES + 1):
                turned_hidden(j)
                if j < SLOT_TILES:
                    sum_hidden(j % 2, j + 1, 16 * (j // 2 + 1))
                result((j - 1) % 2, j, 16 * ((j - 1) // 2 + 1), 16 * ((j - 1) // 2))
            dve.wait_ge(halved, 1)
            for t in range(NT):
                dve.wait_ge(y_landed[t % 2], 32 * (t // 2 + 1))
                link(nc.vector.scalar_tensor_tensor(out=acc[:, t, :], in0=y_in[:, t % 2, 0, :], scalar=weight[:, 0, t:t + 1],
                                                    in1=acc[:, t, :], op0=ALU.mult, op1=ALU.add))
                ins = nc.vector.scalar_tensor_tensor(out=acc[:, t, :], in0=y_in[:, t % 2, 1, :], scalar=weight[:, 1, t:t + 1],
                                                     in1=acc[:, t, :], op0=ALU.mult, op1=ALU.add)
                ins.then_inc(y_used, 1)
            dve.wait_ge(y_used, NT)
            dve.wait_ge(x_shifted, 2 + B)
            for b in range(B):
                normalise(acc, acc, b, 1e-5)
                dve.wait_ge(xh_ready, NT * 3 + CP * (b + 1))
                rows = slice(CP * b, CP * (b + 1))
                link(nc.vector.tensor_tensor(acc[:, rows, :], acc[:, rows, :], ffn_g_sb.unsqueeze(1).to_broadcast([P, CP, D]), ALU.mult))
                nc.vector.tensor_tensor(x_sb[:, rows, :], x_sb[:, rows, :], acc[:, rows, :], ALU.add).then_inc(out_ready, 1)

        @block.tensor
        def _(pe):
            pe.wait_ge(w_in, 16 * 12)
            for pair in range(NT // 2):
                pe.wait_ge(xh_ready, 2 * pair + 2)
                if pair >= 2:
                    pe.wait_ge(xt_ready, pair - 1)
                for k in range(KC):
                    for j in range(2):
                        last = nc.tensor.transpose(ps[:, 6 + pair % 2, 256 * k + P * j:256 * k + P * (j + 1)],
                                                   xh[:, 2 * pair + j, P * k:P * (k + 1)], ident[:, :])
                last.then_inc(xt_ps, 1)

            for c, (kind, m, n) in enumerate(proj):
                if c >= PB:
                    if proj[c - PB][0] == "v":
                        pe.wait_ge(v_ready, v_at.index(c - PB) + 1)
                    else:
                        pe.wait_ge(rest1, qk_at.index(c - PB) + 1)
                if c == 0:
                    pe.wait_ge(nat_ready, 4 * B)
                bank = ps[:, c % PB, :]
                if kind == "v":
                    for j in range(2):
                        t = S * m + P * (2 * n + j)
                        for k in range(KC):
                            last = nc.tensor.matmul(bank[:, D * j:D * (j + 1)], xt_nat[:, k, t:t + P], wv_sb[:, k, :],
                                                    start=(k == 0), stop=(k == KC - 1))
                else:
                    w, src = (wq_sb, xt_tile) if kind == "q" else (wk_sb, xt_nat)
                    for k in range(KC):
                        last = nc.tensor.matmul(bank, w[:, k, P * m:P * (m + 1)], src[:, k, 512 * n:512 * (n + 1)],
                                                start=(k == 0), stop=(k == KC - 1))
                last.then_inc(proj_ps, 1)
            pe.wait_ge(table_in, 16 * 8)
            pe.wait_ge(rest1, len(qk_at))
            pe.wait_ge(v_ready, len(v_at))

            def head_bounds(which):
                pe.wait_ge(bound_in, which + 1)
                for m in range(KC):
                    last = nc.tensor.matmul(ps[0:1, 7, 8 * m:8 * m + 8], size_prod[:, m:m + 1], head_rows,
                                            start=True, stop=True)
                last.then_inc(bound_ps, 1)

            def turn_maxima(maxima, tiles, into):
                for t in range(tiles):
                    last = nc.tensor.transpose(ps[0:H, 4 + t // 4, P * (t % 4):P * (t % 4 + 1)], maxima[:, t, :], ident[:, :])
                last.then_inc(into, 1)

            pe.wait_ge(late_in, 16 * LATE_DMAS)
            head_bounds(0)
            with needed(nc.tensor, pe, 0):
                with pe.Fori(0, NG) as g:
                    for b in range(B):
                        pe.wait_ge(max_in[b], 16 * (NSTK - 1) * g + 16 * (NSTK - 1))
                        for h in range(HG):
                            for t in range(CP):
                                u = CP * (HG * b + h) + t
                                pe.wait_ge(max_read, B * HG * CP * g + (u + 1))
                                for half in range(2):
                                    last = nc.tensor.matmul(ps[:, 2 * (u % 2) + half, :], q_stk[b][0:96, h, P * t:P * (t + 1)],
                                                            k_stk[b][0:96, h, 512 * half:512 * (half + 1)], start=True, stop=True)
                                last.then_inc(max_ps, 1)
                pe.wait_ge(max_read, B * HG * CP * NG + 2)
                turn_maxima(row_max, NT, max_tr)

            def context(part):
                if part == 0:
                    for b in range(B):
                        for k in range(KC):
                            at = (CTX + 1) * (KC * b + k)
                            last = nc.tensor.transpose(ps[:, 6, at:at + CTX], ctx_sb[:, b, P * k:P * (k + 1)], ident[0:CTX, 0:CTX])
                    last.then_inc(ctx_ps, 1)
                elif part == 1:
                    pe.wait_ge(ctx_ready, 1)
                    for m in range(KC):
                        for k in range(KC):
                            last = nc.tensor.matmul(ps[:, 6, B * CTX * m:B * CTX * (m + 1)], xwk_sb[:, k, P * m:P * (m + 1)],
                                                    ctx_t[:, :, k, 0:CTX], start=(k == 0), stop=(k == KC - 1))
                    last.then_inc(kv2_ps, 1)
                elif part == 2:
                    pe.wait_ge(kv2_ready, 1)
                    for b in range(B):
                        for k in range(KC):
                            last = nc.tensor.matmul(ps[0:CTX + 1, 6, D * b:D * (b + 1)], ctx_t[:, b, k, :], xwv_sb[:, k, :],
                                                    start=(k == 0), stop=(k == KC - 1))
                    last.then_inc(kv2_ps, 1)
                elif part == 3:
                    pe.wait_ge(kv2_ready, 2)
                    pe.wait_ge(hide_ready, 1)
                if part in (3, 4):
                    if part == 4:
                        pe.wait_ge(hide_out, 1)
                    bank = ps[0:CTX + 1, 6, :].bitcast(BF16)
                    for t in range(CP):
                        last = nc.tensor.transpose(bank[:, P * t:P * (t + 1)], hide[:, CP * (part - 3) + t, :], ident_bf[:, :])
                    last.then_inc(hide_ps, 1)

            def turn_group(n):
                pe.wait_ge(o_out, n + 1)
                for c in range(CP):
                    last = nc.tensor.transpose(ps[:, 6 + c // 4, P * (c % 4):P * (c % 4 + 1)],
                                               o_t[:, P * c:P * (c + 1)], ident[:, :])
                last.then_inc(o_tr, 1)

            pe.sem_inc(p_free, 2)

            def attention(b, g, buf):
                n = NG * b + g

                def scores(st, pair):
                    if st == 0 and pair == 0:
                        pe.wait_ge(stk_in[buf], 8 * NSTK * n + (16 - 8 * buf) * NSTK)
                    for h in range(2 * pair, 2 * pair + 2):
                        u = HG * st + h
                        pe.wait_ge(s_free, NKT * HG * n + (u + 1))
                        for half in range(2):
                            last = nc.tensor.matmul(ps[:, 2 * (u % 2) + half, :], k_stk[buf][:, h, P * st:P * (st + 1)],
                                                    q_stk[buf][:, h, 512 * half:512 * (half + 1)], start=True, stop=True)
                        last.then_inc(s_ready, 1)

                def bias(jt):
                    nv = VARYING[g]
                    if jt == 0:
                        pe.wait_ge(dve_att, 2 * n + 1)
                        pe.wait_ge(vb_ready, g + 1)
                    if nv:
                        for h in range(HG):
                            start = 440 + 64 * h - 8 * jt
                            row = dims(t_grp[:, start:start + 1], [-P, nv], [1, P])
                            nc.tensor.matmul(ps[32 * h:32 * h + 32, 6, 0:P * nv], v_bias[:, jt, h, :, :].rearrange("p b d -> p (b d)"),
                                             row, start=(jt == 0), stop=(jt == NKT - 1), tile_position=(0, 32 * h))
                    for h in range(HG):
                        last = nc.tensor.matmul(ps[32 * h:32 * h + 32, 7, 0:2], v_bias[:, jt, h, :, :].rearrange("p b d -> p (b d)"),
                                                table[:, 0:2], start=(jt == 0), stop=(jt == NKT - 1), tile_position=(0, 32 * h))
                    if jt == NKT - 1:
                        last.then_inc(bias_ps, 1)

                def values(st, half):
                    if st == 0 and half == 0:
                        pe.wait_ge(vg_ready, n + 1)
                        pe.wait_ge(o_out, n + 1)
                    if half == 0:
                        pe.wait_ge(s_free, NKT * HG * n + (HG * (st + 1) + 2))
                    for h in range(HG):
                        last = nc.tensor.matmul(ps[32 * h:32 * h + 32, 4 + half, :], v_grp[buf][:, st, h, :],
                                                probs[:, st % 2, h, 512 * half:512 * (half + 1)],
                                                start=(st == 0), stop=(st == NKT - 1), tile_position=(0, 32 * h))
                    if half == 1:
                        last.then_inc(p_free, 1)

                for st in range(NKT):
                    for half in range(2):
                        scores(st, half)
                        if st >= 1:
                            values(st - 1, half)
                    if b == 0:
                        if st == 0 and g >= 1:
                            pe.wait_ge(bias_read, g)
                            turn_group(n)
                        if g == 0 and 1 <= st <= 5:
                            context(st - 1)
                        for jt in ([], [0, 1], [2, 3], [4, 5], [6], [7], [], [])[st]:
                            bias(jt)
                        if st == 6:
                            pe.wait_ge(bias_out, g + 1)
                            if g == 0:
                                pe.wait_ge(hide_out, 2)
                            nv = VARYING[g]
                            for c in range(nv + 1):
                                last = nc.tensor.transpose(ps[:, 6 + c // nv if nv else 7, P * (c % nv if nv else 0):P * (c % nv if nv else 0) + P],
                                                           bias_t[:, P * c:P * (c + 1)], ident[:, :])
                            last.then_inc(bias_tr, 1)
                    else:
                        if st == 0:
                            turn_group(n)
                        if st == 4:
                            pe.wait_ge(xh_ready, 2 * g + (NT + 2))
                            pe.wait_ge(dve_att, 2 * n + 1)
                            for k in range(KC):
                                for j in range(2):
                                    last = nc.tensor.transpose(ps[:, 6, 256 * k + P * j:256 * k + P * (j + 1)],
                                                               pair_rows[:, j, P * k:P * (k + 1)], ident[:, :])
                            last.then_inc(x2_ps, 1)
                        if st == 6:
                            pe.wait_ge(x2_ready, g + 1)
                            for m in range(KC):
                                for k in range(KC):
                                    last = nc.tensor.matmul(ps[:, 7, 256 * m:256 * (m + 1)], xwq_sb[:, k, P * m:P * (m + 1)],
                                                            x2_t[:, k, 0:256], start=(k == 0), stop=(k == KC - 1))
                            last.then_inc(q2_ps, 1)
                for half in range(2):
                    values(NKT - 1, half)
                if b == 1:
                    pe.wait_ge(q2_ready, g + 1)

            for g in range(NG):
                attention(0, g, g % 2)
            with pe.Fori(0, NG // 2) as i:
                for o in range(2):
                    attention(1, 2 * i + o, o)
            turn_group(B * NG)

            def scores2(ch, hg, pr):
                b, i = divmod(ch, 2)
                u = 8 * ch + 2 * hg + pr
                if u >= 2:
                    pe.wait_ge(s2_free, u - 1)
                at = slice(512 * i, 512 * (i + 1))
                for hh in range(2):
                    h = HG * hg + 2 * pr + hh
                    bank = ps[0:CTX + 1, 2 * (u % 2) + hh, :]
                    nc.tensor.matmul(bank, k2_pad[:, b, h, :], q2_t[b][:, h // 8, at], start=True, stop=False)
                    last = nc.tensor.matmul(bank, pick[:, h, :], hide_t[0:CTX + 1 + 3 * H, 512 * ch:512 * (ch + 1)],
                                            start=False, stop=True)
                last.then_inc(s2_ready, 1)

            def values2(n):
                ch, hg = divmod(n, NG)
                if n >= 1:
                    pe.wait_ge(o2_out, n)
                pe.wait_ge(s2_free, 2 * n + 2)
                for h in range(HG):
                    last = nc.tensor.matmul(ps[32 * h:32 * h + 32, 4, :], v2_sb[:, ch // 2, HG * hg + h, :],
                                            probs2[:, hg % 2, h, :], start=True, stop=True, tile_position=(0, 32 * h))
                last.then_inc(pv2_done, 1)

            def turn2(n):
                pe.wait_ge(o2_out, n + 1)
                if n >= 1:
                    pe.wait_ge(o2_div, n)
                for t in range(CHUNK):
                    last = nc.tensor.transpose(ps[:, 5, P * t:P * (t + 1)], o2_tr[:, n % 2, P * t:P * (t + 1)], ident[:, :])
                last.then_inc(o2_tr_done, 1)

            def outputs(ch):
                pe.wait_ge(o2_div, NG * (ch + 1))
                if ch < 2:
                    pe.wait_ge(q2_ready, NG + KC * (ch + 1))
                else:
                    pe.wait_ge(sg_read, 2 * ch)
                    pe.wait_ge(rank_read, ch)
                for k in range(KC):
                    for t in range(CHUNK):
                        last = nc.tensor.transpose(ps[:, 6 + k, P * t:P * (t + 1)], o2[:, t, P * k:P * (k + 1)], ident[:, :])
                    last.then_inc(o2_ps, 1)

            def add_product(ch):
                pe.wait_ge(o2t_ready, KC * (ch + 1))
                for p in range(2):
                    for t in range(2):
                        for k in range(KC):
                            last = nc.tensor.matmul(ps[:, 6 + p, D * t:D * (t + 1)], o2_t[:, k, P * (2 * p + t):P * (2 * p + t + 1)],
                                                    xwu_sb[:, k, :], start=(k == 0), stop=(k == KC - 1))
                    last.then_inc(u_ps, 1)

            def turn_rows(first, bank_free, done):
                for p in range(2):
                    pe.wait_ge(*bank_free[p])
                    for k in range(KC):
                        for j in range(2):
                            last = nc.tensor.transpose(ps[:, 6 + p, 256 * k + P * j:256 * k + P * (j + 1)],
                                                       xh[:, first + 2 * p + j, P * k:P * (k + 1)], ident[:, :])
                    last.then_inc(done, 1)

            def rows3(ch):
                ready = (xh_ready, 2 * NT + CHUNK * (ch + 1))
                turn_rows(CHUNK * ch, (ready, ready), x3_ps)

            def gates(ch):
                pe.wait_ge(x3_ready, 2 * (ch + 1))
                for t in range(CHUNK):
                    for k in range(KC):
                        last = nc.tensor.matmul(ps[:, 6, EXPERTS * t:EXPERTS * (t + 1)], x3_t[:, k, P * t:P * (t + 1)],
                                                sgw_sb[:, k, D:], start=(k == 0), stop=(k == KC - 1))
                last.then_inc(gate_ps, 1)

            def shared(ch, p):
                if p == 1:
                    pe.wait_ge(gate_read, ch + 1)
                for t in range(2):
                    for k in range(KC):
                        last = nc.tensor.matmul(ps[:, 7 - p, D * t:D * (t + 1)], x3_t[:, k, P * (2 * p + t):P * (2 * p + t + 1)],
                                                sgw_sb[:, k, 0:D], start=(k == 0), stop=(k == KC - 1))
                last.then_inc(sg_ps, 1)

            def ranks(ch):
                pe.wait_ge(both_ready, ch + 1)
                pe.wait_ge(seen_ready, ch + 1)
                pe.wait_ge(sg_read, 2 * ch + 1)
                n = CHUNK * EXPERTS
                flat = both.rearrange("p t e -> p (t e)")
                nc.tensor.matmul(ps[:, 7, 0:n], before[:, :], flat, start=True, stop=False)
                for t in range(1, CHUNK):
                    nc.tensor.matmul(ps[:, 7, EXPERTS * t:n], ones[:, :], flat[:, 0:n - EXPERTS * t], start=False, stop=False)
                nc.tensor.matmul(ps[:, 7, 0:n], ones[:, :], seen_bf[:, :].unsqueeze(1).to_broadcast([P, CHUNK, EXPERTS]),
                                 start=False, stop=True).then_inc(rank_ps, 1)

            def second_queries(i):
                pe.wait_ge(xh_ready, 2 * NT)
                free = ((sg_read, 2 * i), (rank_read, i)) if i else ((q2_ready, NG), (q2_ready, NG))
                turn_rows(CP + CHUNK * i, free, x2_ps)
                pe.wait_ge(x2_ready, NG + 2 * (i + 1))
                for m in range(KC):
                    for k in range(KC):
                        last = nc.tensor.matmul(ps[:, 6 + m, :], xwq_sb[:, k, P * m:P * (m + 1)], x2_t[:, k, :],
                                                start=(k == 0), stop=(k == KC - 1))
                    last.then_inc(q2_ps, 1)

            pe.wait_ge(sgw_in, 32)
            for ch in range(NT // CHUNK):
                b, i = divmod(ch, 2)
                n = NG * ch
                if i == 0:
                    if ch == 2:
                        pe.wait_ge(q2_ready, NG + 2 * KC)
                    head_bounds(1 + b)
                    with needed(nc.tensor, pe, 1 + b):
                        pe.wait_ge(dve_att, 2 * B * NG + 1)
                        if b == 1:
                            pe.wait_ge(o2_div, 2 * NG)
                        for t in range(CP):
                            if t >= 1:
                                pe.wait_ge(max2_read[b], t)
                            for hg in range(NG):
                                last = nc.tensor.matmul(ps[:, hg, 0:HG * CTX], q2_t[b][:, hg // 2, P * t:P * (t + 1)],
                                                        k2_pad[:, b, HG * hg:HG * (hg + 1), 0:CTX], start=True, stop=True)
                            last.then_inc(max2_ps[b], 1)
                        pe.wait_ge(max2_done[b], 1)
                        turn_maxima(row_max2, CP, max2_tr[b])
                        pe.wait_ge(shift2_out[b], 48)
                scores2(ch, 0, 0)
                if ch >= 1:
                    outputs(ch - 1)
                scores2(ch, 0, 1)
                scores2(ch, 1, 0)
                if ch >= 1:
                    add_product(ch - 1)
                scores2(ch, 1, 1)
                values2(n)
                scores2(ch, 2, 0)
                turn2(n)
                scores2(ch, 2, 1)
                if ch >= 1:
                    rows3(ch - 1)
                values2(n + 1)
                scores2(ch, 3, 0)
                if ch >= 1:
                    gates(ch - 1)
                turn2(n + 1)
                scores2(ch, 3, 1)
                if ch >= 1:
                    shared(ch - 1, 0)
                values2(n + 2)
                if ch >= 1:
                    shared(ch - 1, 1)
                turn2(n + 2)
                values2(n + 3)
                if ch >= 1:
                    ranks(ch - 1)
                turn2(n + 3)
                if b == 0:
                    second_queries(i)
            outputs(3)
            add_product(3)
            rows3(3)
            gates(3)
            shared(3, 0)
            shared(3, 1)
            ranks(3)
            pe.wait_ge(seen_ready, 5)
            pe.wait_ge(sg_read, 8)
            nc.tensor.matmul(ps[:, 6, 0:EXPERTS], ones[:, :], seen_bf[:, :], start=True, stop=True).then_inc(count_ps, 1)

            def turn_tile(buf, n, ready=None):
                pe.wait_ge(xs_landed[buf], n)
                if ready is not None:
                    pe.wait_ge(xs_ready, ready)
                for k in range(KC):
                    last = nc.tensor.transpose(ps[:, 7, P * k:P * (k + 1)], xs_in[:, buf, P * k:P * (k + 1)], ident[:, :])
                last.then_inc(xs_ps, 1)

            def layer1(j, buf, ready, summed=None):
                e = nc.tensor.value_load(tile_expert[0:1, bass.ds(j, 1)], min_val=0, max_val=EXPERTS - 1)
                pe.wait_ge(xs_ready, ready)
                if summed is not None:
                    pe.wait_ge(h_sum, summed)
                for half in range(2):
                    for k in range(KC):
                        last = nc.tensor.matmul(ps[:, half, :], xs_t[:, buf, k, :],
                                                w1_sb[:, bass.ds(e, 1), k, 512 * half:512 * (half + 1)].squeeze(1),
                                                start=(k == 0), stop=(k == KC - 1))
                last.then_inc(h_ps, 1)

            def turn_hidden(n):
                pe.wait_ge(h_act, n)
                for k in range(HID // P):
                    last = nc.tensor.transpose(ps[:, 4 + k // 4, P * (k % 4):P * (k % 4 + 1)], hid[:, P * k:P * (k + 1)], ident[:, :])
                last.then_inc(ht_ps, 1)

            def layer2(j, n, taken=None):
                e = nc.tensor.value_load(tile_expert[0:1, bass.ds(j, 1)], min_val=0, max_val=EXPERTS - 1)
                pe.wait_ge(ht_ready, n)
                if taken is not None:
                    pe.wait_ge(y_ready, taken)
                for k in range(HID // P):
                    last = nc.tensor.matmul(ps[:, 6, 0:D], hid_t[:, k, :], w2_sb[:, bass.ds(e, 1), k, :].squeeze(1),
                                            start=(k == 0), stop=(k == HID // P - 1))
                last.then_inc(y_ps, 1)

            pe.wait_ge(w1_in, 16 * EXPERTS)
            pe.wait_ge(w2_in, 16 * EXPERTS)
            turn_tile(0, 16)
            layer1(0, 0, 1)
            turn_tile(1, 16, 1)
            turn_hidden(1)
            layer1(1, 1, 2, 1)
            turn_tile(0, 32, 2)
            layer2(0, 1)
            with pe.Fori(0, (SLOT_TILES - 3) // 2) as i:
                for o in range(2):
                    turn_hidden(2 * i + (o + 2))
                    layer1(2 * i + (o + 2), o, 2 * i + (o + 3), 2 * i + (o + 2))
                    turn_tile(1 - o, 16 * i + (32 + 16 * o), 2 * i + (3 + o))
                    layer2(2 * i + (o + 1), 2 * i + (o + 2), 2 * i + (o + 1))
            turn_hidden(SLOT_TILES - 1)
            layer1(SLOT_TILES - 1, 0, SLOT_TILES, SLOT_TILES - 1)
            layer2(SLOT_TILES - 2, SLOT_TILES - 1, SLOT_TILES - 2)
            turn_hidden(SLOT_TILES)
            layer2(SLOT_TILES - 1, SLOT_TILES, SLOT_TILES - 1)


_INS = ["x", "ctx_1024", "mask_BxSxS2_ik1", "L0_attn_Wq", "L0_attn_Wk", "L0_attn_Wv", "L0_attn_rel_table",
        "L0_attn_gamma", "L0_attn_beta", "L0_xattn_Wq", "L0_xattn_Wk", "L0_xattn_Wv", "L0_xattn_Wu", "L0_xattn_bu",
        "L0_ffn_W1", "L0_ffn_b1", "L0_ffn_W2", "L0_ffn_b2", "L0_ffn_gate_W", "L0_ffn_shared_W", "L0_ffn_shared_b",
        "L0_ffn_gamma", "L0_ffn_beta"]


def constants():
    bf16 = mybir.dt.np(BF16)
    p = np.arange(P)
    e = np.arange(EXPERTS)
    c = {"ident": np.eye(P, dtype=np.float32), "ident_bf": np.eye(P).astype(bf16)}
    pick = np.zeros((CTX + 1 + 3 * H, H, CTX + 1))
    pick[:CTX + 1] = np.eye(CTX + 1)[:, None, :]
    for n in range(3):
        for h in range(H):
            pick[CTX + 1 + H * n + h, h, :CTX] = 1
    c["pick"] = pick.astype(bf16)
    c["head_rows"] = (p[:, None] // DH == np.arange(8)[None, :]).astype(np.float32)
    c["counts"] = np.r_[np.ones(CTX), CTX].astype(np.float32)[:, None].repeat(2, 1)
    c["before"] = (p[:, None] < p[None, :]).astype(bf16)
    c["ones"] = np.ones((P, P)).astype(bf16)
    thresholds = np.tile(P * np.arange(NT), (EXPERTS, 1))
    tiles = np.tile(np.arange(SLOT_TILES)[:, None], (1, EXPERTS))
    row = np.concatenate([thresholds.ravel(), EXPERTS - e, (e[None, :] < e[:, None]).ravel(), REGION_TILES * P * e, tiles.ravel()])
    c["route_c"] = np.tile(row.astype(np.float32), (P, 1))
    return c


def kernel(**inputs):
    import concourse.bacc as bacc
    from concourse.bass_utils import run_bass_kernel_spmd

    nc = bacc.Bacc("TRN2", target_bir_lowering=False, num_devices=1)
    arrays, args = {}, []

    def give(name, a):
        a = np.ascontiguousarray(a)
        arrays[name] = a
        return nc.dram_tensor(name, a.shape, mybir.dt.from_np(a.dtype), kind="ExternalInput").ap()

    for name in _INS:
        a = np.asarray(inputs[name])
        if name == "L0_attn_rel_table":
            a = a[::-1].T
        if name in ("L0_xattn_Wq", "L0_xattn_Wk", "L0_xattn_Wv"):
            a = a.transpose(1, 0, 2).reshape(D, D)
        args.append(give("in_" + name, a))
    consts = {k: give("const_" + k, v) for k, v in constants().items()}
    out = nc.dram_tensor("out_0_dram", (B, S, D), F32, kind="ExternalOutput").ap()
    decoder_layer(nc, *args, consts, out)
    r = run_bass_kernel_spmd(nc, [arrays], core_ids=[0])
    return r.results[0]["out_0_dram"]
```

```python
from contextlib import ExitStack

import numpy as np

import concourse.bass as bass
from concourse import mybir

F32 = mybir.dt.float32
BF16 = mybir.dt.bfloat16
I32 = mybir.dt.int32
U32 = mybir.dt.uint32
ALU = mybir.AluOpType
ACT = mybir.ActivationFunctionType
AX = mybir.AxisListType

P = 128
B, S, D, H = 2, 1024, 256, 16
DH = D // H
NT = B * S // P
CP = S // P
KC = D // P
HG = 4
NG = H // HG
NKT = S // P
RELS = 511
TW = 2 * S - 8
TG = 8 * (NKT - 1) + P * 3 + 64 * (HG - 1) + P
T0 = TW - RELS
STK = 6 * DH + 3
NSTK = 13
CTX = 77
BOUND = 64.0
NEG = -float(2 ** 100)
EXPERTS, HID = 8, 1024
SLOT_TILES = 2 * NT + EXPERTS - 1


REGION_TILES = 2 * 1024 // P
ROW_TILES = EXPERTS * REGION_TILES + SLOT_TILES - 2 * NT
NEWTON = 3
PAIR_LINKS = 6 + 2 * (3 + 3 * NEWTON)
VARYING = (0, 0, 2, 4)
ROUNDS = ((0, 2), (2, 5), (5, 8), (8, 11), (11, 14), (14, 16))
SURE = (2 * NT - 2) // 2
PAIRS = (SLOT_TILES - 3) // 2
CHUNK = 4
ARENA = 651 * 64
LATE_DMAS = 4 + 1 + 2 * B + 6 + 6
W2_AT, SGW_AT, X_AT, ACC_AT = (n * 256 for n in (256, 520, 529, 587))


def dims(ap, *free):
    return bass.AP(ap.tensor, ap.offset, [list(ap.ap[0])] + [list(f) for f in free])


def decoder_layer(nc, x, ctx_in, mask, wq, wk, wv, rel_rows, attn_g, attn_b, xwq, xwk, xwv, xwu, xbu,
                  w1, b1, w2, b2, gate_w, shared_w, shared_b, ffn_g, ffn_b, consts, out):
    scope = ExitStack()

    def sb(name, shape, dt=F32):
        return scope.enter_context(nc.sbuf_tensor(name, shape, dt))

    def sem(name):
        return scope.enter_context(nc.semaphore(name))

    with scope:
        qs_dram = nc.dram_tensor("q_parts", [B, 3, D, S], BF16).ap()
        ks_dram = nc.dram_tensor("k_parts", [B, 3, D, S], BF16).ap()
        xs_dram = nc.dram_tensor("rows_by_expert", [ROW_TILES * P, D], F32).ap()
        ys_dram = nc.dram_tensor("results_by_expert", [SLOT_TILES * P, D], F32).ap()
        shift_dram = nc.dram_tensor("shift_parts", [B, 3, H, S], BF16).ap()

        x_sb = sb("x_sb", [P, NT, D])
        xh = sb("xh", [P, NT, D])
        ident = sb("ident", [P, P])
        stats = sb("stats", [P, NT, 6])
        mv = sb("mv", [P, NT, 2])
        rstd = sb("rstd", [P, NT])
        shift = sb("shift", [P, NT])
        root_s, root_t = sb("root_s", [P, CP]), sb("root_t", [P, CP])

        rows_sb = sb("rows_sb", [P, 6, D])
        attn_g_sb, attn_b_sb, xbu_sb, shared_b_sb, ffn_g_sb, ffn_b_sb = (rows_sb[:, i, :] for i in range(6))
        slot = sb("slot", [P, 2, NT], U32)
        slot_y = sb("slot_y", [P, 2, NT], U32)
        weight = sb("weight", [P, 2, NT])
        route_c = sb("route_c", [P, EXPERTS * (NT + 1 + EXPERTS + 1 + SLOT_TILES)])
        before = sb("before", [P, P], BF16)
        ones = sb("ones", [P, P], BF16)
        tile_expert = sb("tile_expert", [P, SLOT_TILES], I32)
        tile_row = sb("tile_row", [P, SLOT_TILES], I32)
        run = sb("run", [P, PAIRS - SURE], I32)[:, :]
        last_tile = sb("last_tile", [P, 1], I32)[:, :]
        seen = sb("seen", [P, EXPERTS])
        seen_bf = sb("seen_bf", [P, EXPERTS], BF16)
        over = sb("over", [P, NT])
        ident_bf = sb("ident_bf", [P, P], BF16)
        sizes = sb("sizes", [P, KC, 2, 4])[:, :, :, :]
        size = sb("size", [P, KC, 2])[:, :, :]
        size_prod = sb("size_prod", [P, KC])[:, :]
        head_bound = sb("head_bound", [1, H])[:, :]
        most = sb("most", [1, 2])[:, :]
        flags = sb("flags", [1, 1 + B], I32)[:, :]
        small = [P, CHUNK, EXPERTS]
        picks = sb("picks", [P, 2, NT, EXPERTS])
        place_f = sb("place_f", [P, 2, NT])
        delta = sb("delta", [P, EXPERTS])[:, :]
        both = sb("both", small, BF16)[:, :, :]
        top1, top2, best = (sb(n, [P, CHUNK])[:, :] for n in ("top1", "top2", "best"))
        both_n = sb("both_n", [P, EXPERTS])[:, :]
        tiles_of, base, ends = (sb(n, [P, EXPERTS])[:, :] for n in ("tiles_of", "base", "ends"))
        over_one = sb("over_one", [P, NT])
        head_rows = sb("head_rows", [P, 8])[:, :]
        counts = sb("counts", [CTX + 1, 2])[:, :]
        hide_max = sb("hide_max", [P, NT])
        k2_size = sb("k2_size", [P, KC])
        pair_stats, pair_mv, pair_r = sb("pair_stats", [P, 2, 6]), sb("pair_mv", [P, 2, 2]), sb("pair_r", [P, 2])
        arena = sb("arena", [P, ARENA])
        ended = arena[:, SGW_AT // 4:SGW_AT // 4 + SLOT_TILES * EXPERTS].rearrange("p (j e) -> p j e", e=EXPERTS)
        moved = arena[:, SGW_AT // 4:SGW_AT // 4 + 2 * NT * EXPERTS].rearrange("p (t e) -> p t e", e=EXPERTS)
        run_f = arena[:, X_AT // 4 + 960:X_AT // 4 + 960 + PAIRS - SURE]
        last_f = arena[:, X_AT // 4 + 970:X_AT // 4 + 971]
        move = arena[:, SGW_AT // 4 + 2 * NT * EXPERTS:SGW_AT // 4 + 2 * NT * (EXPERTS + 1)]
        ended_x = arena[:, X_AT // 4:X_AT // 4 + SLOT_TILES * EXPERTS].rearrange("p (j e) -> p j e", e=EXPERTS)
        full = arena[:, X_AT // 4 + 512:X_AT // 4 + 512 + EXPERTS * NT].rearrange("p (e j) -> p e j", e=EXPERTS)
        ended_n, ended_w, rowf = (arena[:, X_AT // 4 + 768 + 64 * n:X_AT // 4 + 768 + 64 * n + SLOT_TILES] for n in range(3))

        class Region:

            def __init__(self, at):
                self.at = at // 4

            def take(self, shape, dt=F32):
                n = int(np.prod(shape[1:])) * mybir.dt.size(dt) // 4
                ap = arena[0:shape[0], self.at:self.at + n]
                self.at += n
                assert self.at <= ARENA, self.at
                ap = ap if dt == F32 else ap.bitcast(dt)
                names = "abcde"[:len(shape) - 1]
                sizes = dict(zip(names, shape[1:]))
                return ap.rearrange(f"p ({' '.join(names)}) -> p {' '.join(names)}", **sizes)

        r = Region(0)
        wq_sb, wk_sb, wv_sb = (r.take([P, KC, D]) for _ in range(3))
        table = r.take([P, TW])
        t_grp = r.take([P, TG])
        table_end = 4 * r.at
        last_row = r.take([P, 2])
        v_sb = r.take([P, B, NKT, D])
        v_grp = [r.take([P, NKT, HG, 32]) for _ in range(B)]
        v_bias = r.take([P, NKT, HG, B, DH])
        q_stk = [None, r.take([P, HG, S], BF16)[0:STK]]
        rest = r.take([P, 4, 512])
        rest_end = r.at
        r.at -= 4 * 512
        o_t, bias_t = r.take([P, S]), r.take([P, 512 + P])
        rden = r.take([P, CP, HG])
        o_n = r.take([P, CP, HG, DH])
        assert 4 * max(r.at, rest_end) <= W2_AT
        r = Region(W2_AT)
        probs = r.take([P, 2, HG, S])
        xt = probs.rearrange("p a h s -> p (a h s)")
        xt_tile = xt[:, 0:KC * B * S].rearrange("p (k n) -> p k n", k=KC)
        xt_nat = xt[:, KC * B * S:2 * KC * B * S].rearrange("p (k n) -> p k n", k=KC)
        k_stk = [None, r.take([P, HG, S], BF16)[0:STK]]
        q_stk[0], k_stk[0] = (r.take([P, HG, S], BF16)[0:STK] for _ in range(2))
        parts_at = 4 * r.at
        parts = r.take([P, 4, 3, 512], BF16)
        assert 4 * r.at <= X_AT

        row_max = xt[:, 0:NT * H].rearrange("p (t h) -> p t h", h=H)
        neg_max = rest.rearrange("p a n -> p (a n)")[0:H]
        neg_parts = parts.rearrange("p a c n -> p (a c n)").rearrange("p (c n) -> p c n", c=3)[0:H]

        r = Region(X_AT)
        xwq_sb, xwu_sb = (r.take([P, KC, D]) for _ in range(2))
        pick = r.take([P, H, CTX + 1], BF16)[0:CTX + 1 + 3 * H]
        hide_t = r.take([P, B * S], BF16)
        v2_sb = r.take([P, B, H, 32])[0:CTX + 1]
        assert 4 * r.at <= ACC_AT
        r = Region(ACC_AT)
        xwk_sb, xwv_sb = (r.take([P, KC, D]) for _ in range(2))
        ctx_sb = r.take([P, B, D])[0:CTX]
        mask_sb = r.take([P, NT, CTX], I32)
        zeros = r.take([P, D])
        ctx_t = r.take([P, B, KC, CTX + 1])
        hide = r.take([P, NT, CTX + 1], BF16)
        assert 4 * ACC_AT // 4 + 12 * 1024 <= 4 * r.at <= ACC_AT + 16384
        k2_pad = Region(parts_at).take([P, B, H, CTX + 1])

        r = Region(W2_AT)
        probs2 = r.take([P, 2, HG, 512])[0:CTX + 1]
        q2_t = [None, r.take([P, KC, S])]
        o2_tr = r.take([P, 2, 512])
        o2 = r.take([P, CHUNK, D])
        o2_t = r.take([P, KC, 512])
        rden2 = r.take([P, CHUNK, HG])
        r = Region(parts_at - 16384)
        x3_t = r.take([P, KC, 512])
        logits, hit, cand, lg2, pos = (r.take([P, CHUNK, EXPERTS]) for _ in range(5))
        r = Region(0)
        q2_t[0] = r.take([P, KC, S])
        x2_t = r.take([P, KC, 512])
        pair_rows = r.take([P, 2, D])
        assert 4 * r.at <= table_end
        r = Region(W2_AT)
        hidden_s = r.take([P, H, CTX])
        row_max2 = r.take([P, CP, H])
        neg_max2 = r.take([P, S])[0:H]
        neg_parts2 = r.take([P, 3, S], BF16)[0:H]
        assert 4 * r.at <= W2_AT + 16384

        w1_sb = Region(0).take([P, EXPERTS, KC, HID])
        w2_sb = Region(W2_AT).take([P, EXPERTS, HID // P, D])
        acc = Region(ACC_AT).take([P, NT, D])
        sgw_sb = Region(SGW_AT).take([P, KC, D + EXPERTS])
        r = Region(X_AT)
        xs_in = r.take([P, 2, D])
        xs_t = r.take([P, 2, KC, P])
        y_sb = r.take([P, 2, D])
        b2_row = r.take([P, 2, D])
        y_in = Region(0).take([P, NT, 2, D])
        assert 4 * r.at <= ACC_AT
        xh_flat = xh[:, :, :].rearrange("p t f -> p (t f)")
        b1_row = xh_flat[:, 0:2 * HID].rearrange("p (a n) -> p a n", a=2)
        hid = xh_flat[:, 2 * HID:3 * HID]
        hid_t = xh_flat[:, 3 * HID:4 * HID].rearrange("p (k n) -> p k n", k=HID // P)

        ps = scope.enter_context(nc.psum_tensor("ps", [P, 8, 512], F32))

        x_in = [sem(f"x_in{b}") for b in range(B)]
        w_in, table_fill, table_in = sem("w_in"), sem("table_fill"), sem("table_in")
        ln_var, ln_std, dve_link = sem("ln_var"), sem("ln_std"), sem("dve_link")
        xh_ready, xt_ps, xt_ready, nat_ready = sem("xh_ready"), sem("xt_ps"), [sem(f"xt_ready{b}") for b in range(B)], sem("nat_ready")
        proj_ps, part0, rest1, part1, part2 = (sem(n) for n in ("proj_ps", "part0", "rest1", "part1", "part2"))
        v_ready = sem("v_ready")
        parts_out = [sem(f"parts_out{i}") for i in range(4)]
        zero_out = sem("zero_out")
        stk_in = [sem(f"stk_in{b}") for b in range(B)]
        ones_set, stk_again = sem("ones_set"), sem("stk_again")
        vg_ready, vb_ready, t_ready = sem("vg_ready"), sem("vb_ready"), sem("t_ready")
        s_ready, s_free, p_free = sem("s_ready"), sem("s_free"), sem("p_free")
        bias_ps, bias_out, bias_tr = sem("bias_ps"), sem("bias_out"), sem("bias_tr")
        half_in, o_half, o_out, o_tr, bias_read, dve_att = sem("half_in"), sem("o_half"), sem("o_out"), sem("o_tr"), sem("bias_read"), sem("dve_att")
        att_done = sem("att_done")
        bound_in, bound_ps, flag_set = sem("bound_in"), sem("bound_ps"), sem("flag_set")
        max_in = [sem(f"max_in{b}") for b in range(B)]
        max_ps, max_read, max_tr, max_split, shift_out, dve_max = (sem(n) for n in (
            "max_ps", "max_read", "max_tr", "max_split", "shift_out", "dve_max"))
        max2_ps, max2_read, max2_done, max2_tr, max2_split, shift2_out, dve_max2 = ([sem(f"{n}{b}") for b in range(B)] for n in (
            "max2_ps", "max2_read", "max2_done", "max2_tr", "max2_split", "shift2_out", "dve_max2"))
        late_in, ys_zero, zeros_set, xs_zero = sem("late_in"), sem("ys_zero"), sem("zeros_set"), sem("xs_zero")
        x_shifted = sem("x_shifted")
        x2_ps, x2_ready, q2_ps, q2_ready = sem("x2_ps"), sem("x2_ready"), sem("q2_ps"), sem("q2_ready")
        ctx_ps, ctx_ready, kv2_ps, kv2_ready = sem("ctx_ps"), sem("ctx_ready"), sem("kv2_ps"), sem("kv2_ready")
        hide_ready, hide_ps, hide_out = sem("hide_ready"), sem("hide_ps"), sem("hide_out")
        s2_ready, s2_free, pv2_done, o2_out = sem("s2_ready"), sem("s2_free"), sem("pv2_done"), sem("o2_out")
        o2_tr_done, o2_div, dve_pair, work_zero, pool_link = sem("o2_tr_done"), sem("o2_div"), sem("dve_pair"), sem("work_zero"), sem("pool_link")
        gate_ps, gate_read, seen_ready, slot_ready, count_ps, sh_added, moved_ready = (sem(n) for n in (
            "gate_ps", "gate_read", "seen_ready", "slot_ready", "count_ps", "sh_added", "moved_ready"))
        o2_ps, o2t_ready, u_ps, x2_added = sem("o2_ps"), sem("o2t_ready"), sem("u_ps"), sem("x2_added")
        w1_in, w2_in, sgw_in = sem("w1_in"), sem("w2_in"), sem("sgw_in")
        x3_ps, x3_ready, sg_ps, sg_read, sg_act, halved = (sem(n) for n in (
            "x3_ps", "x3_ready", "sg_ps", "sg_read", "sg_act", "halved"))
        pair_ready, both_ready, rank_ps, rank_read = (sem(n) for n in ("pair_ready", "both_ready", "rank_ps", "rank_read"))
        route_done, scattered = sem("route_done"), sem("scattered")
        xs_landed = [sem(f"xs_landed{i}") for i in range(2)]
        b1_landed = [sem(f"b1_landed{i}") for i in range(2)]
        b2_landed = [sem(f"b2_landed{i}") for i in range(2)]
        xs_ps, xs_ready, h_ps, h_sum, h_act, ht_ps, ht_ready, y_ps, y_ready = (sem(n) for n in (
            "xs_ps", "xs_ready", "h_ps", "h_sum", "h_act", "ht_ps", "ht_ready", "y_ps", "y_ready"))
        y_stored = [sem(f"y_stored{i}") for i in range(2)]
        y_landed = [sem(f"y_landed{i}") for i in range(len(ROUNDS))]
        second_shift, second_ready = sem("second_shift"), sem("second_ready")
        weights_set, y_weighted, out_moments, out_normed = (sem(n) for n in ("weights_set", "y_weighted", "out_moments", "out_normed"))
        out_ready, out_done = sem("out_ready"), sem("out_done")

        proj = ([(kind, m, n) for m in range(KC) for kind in "qk" for n in range(4)]
                + [("v", b, n) for b in range(B) for n in range(4)])
        qk_at = [c for c, (kind, _, _) in enumerate(proj) if kind != "v"]
        v_at = [c for c, (kind, _, _) in enumerate(proj) if kind == "v"]
        PB = 6

        block = scope.enter_context(nc.Block())

        def may_run(on, eng, i, body, counts):
            flag = on.alloc_register(f"run_{i}_{on.engine.name}")
            on.reg_load(flag, run[0:1, i - SURE:i - SURE + 1])
            with eng.If_ne(flag, 0):
                body(i)
            with eng.If_eq(flag, 0):
                for s, before_round, step in counts(i):
                    eng.wait_ge(s, before_round)
                    eng.sem_inc(s, step)

        def needed(on, eng, which):
            eng.wait_ge(flag_set, which + 1)
            flag = on.alloc_register(f"flag_{which}_{on.engine.name}")
            on.reg_load(flag, flags[0:1, which:which + 1])
            return eng.If_ne(flag, 0)

        @block.sync
        def _(sp):
            for b in range(B):
                rows = x[b].rearrange("(a c o) f -> o a c f", c=CP, o=2)
                for o in range(2):
                    sp.dma_start(x_sb[64 * (1 - o):64 * (2 - o), CP * b:CP * (b + 1), :], rows[o]).then_inc(x_in[b], 16)
            sp.dma_start(ident[:, :], consts["ident"]).then_inc(w_in, 16)
            sp.dma_start(head_rows, consts["head_rows"]).then_inc(w_in, 16)
            for dst, src in ((wk_sb, wk), (wq_sb, wq), (wv_sb, wv)):
                sp.dma_start(dst[:, :, :], src.rearrange("(k p) n -> p k n", p=P)).then_inc(w_in, 16)
            for r in range(8):
                sp.dma_start(last_row[16 * r:16 * r + 16, 0:1], rel_rows[:, 0:1],
                             allow_slow_non_contiguous=True).then_inc(w_in, 16)
            sp.wait_ge(table_fill, 1)
            for r in range(8):
                sp.dma_start(table[16 * r:16 * r + 16, T0 + r:TW], rel_rows[:, 0:RELS - r]).then_inc(table_in, 16)
            for dst, src in ((xwq_sb, xwq), (xwk_sb, xwk), (xwv_sb, xwv), (xwu_sb, xwu)):
                sp.dma_start(dst, src.rearrange("(k p) n -> p k n", p=P)).then_inc(late_in, 16)
            sp.dma_start(ctx_sb, ctx_in.rearrange("b t d -> t b d")).then_inc(late_in, 16)
            for b in range(B):
                rows = mask[b].rearrange("(a c o) t -> o a c t", c=CP, o=2)
                for o in range(2):
                    sp.dma_start(mask_sb[64 * (1 - o):64 * (2 - o), CP * b:CP * (b + 1), :], rows[o]).then_inc(late_in, 16)
            for i, row in enumerate((attn_g, attn_b, xbu, shared_b, ffn_g, ffn_b)):
                sp.dma_start(rows_sb[:, i, :], row.partition_broadcast(P)).then_inc(late_in, 16)
            for dst, name in ((pick, "pick"), (counts, "counts"), (ident_bf[:, :], "ident_bf"),
                              (before[:, :], "before"), (ones[:, :], "ones"), (route_c[:, :], "route_c")):
                sp.dma_start(dst, consts[name]).then_inc(late_in, 16)
            sp.wait_ge(zeros_set, 1)
            for b in range(B):
                sp.dma_start(shift_dram[b].rearrange("c h (a s) -> (c h) a s", a=2),
                             zeros[0:3 * H, :].bitcast(BF16).unsqueeze(1).to_broadcast([3 * H, 2, 512])).then_inc(zero_out, 16)
            def load_block(g, b, landed, buf, blk):
                for stk, src, part in ((k_stk[buf], ks_dram, (0, 1, 2, 0, 1, 0)[blk]),
                                       (q_stk[buf], qs_dram, (0, 0, 0, 1, 1, 2)[blk])):
                    rows = src[b, part, bass.ds(64 * g, 64), :].rearrange("(h d) s -> d h s", h=HG)
                    sp.dma_start(stk[16 * blk:16 * blk + 16, :, :], rows).then_inc(landed, 16)

            def load_parts(g, b, landed, buf):
                for blk in range(6):
                    load_block(g, b, landed, buf, blk)

            for q, c in enumerate(qk_at):
                kind, m, n = proj[c]
                dst = (qs_dram if kind == "q" else ks_dram)[n // 2, :, P * m:P * (m + 1), 512 * (n % 2):512 * (n % 2 + 1)]
                sp.wait_ge(part2, q + 1)
                sp.dma_start(dst.rearrange("c p n -> p c n"), parts[:, q % 4, :, :]).then_inc(parts_out[q % 4], 16)
                first = len(qk_at) // 2 + 1
                if q == first:
                    for i in range(4):
                        sp.wait_ge(parts_out[i], 16 * (len(qk_at) // 8))
                if first <= q < first + 6:
                    load_block(0, 0, stk_in[0], 0, q - first)
            sp.wait_ge(zero_out, 32)
            sp.wait_ge(ones_set, 1)

            def all_parts_out():
                for i in range(4):
                    sp.wait_ge(parts_out[i], 16 * (len(qk_at) // 4))

            with needed(nc.sync, sp, 0):
                sp.wait_ge(stk_in[0], 16 * (NSTK - 1))
                all_parts_out()
                with sp.Fori(0, NG) as g:
                    sp.wait_ge(max_read, B * HG * CP * g + 2)
                    for b in range(B):
                        load_parts(g, b, max_in[b], b)
                sp.wait_ge(max_read, B * HG * CP * NG + 2)
                sp.wait_ge(max_split, 1)
                for b in range(B):
                    sp.dma_start(shift_dram[b].rearrange("c h s -> h c s"), neg_parts[:, :, S * b:S * (b + 1)])\
                        .then_inc(shift_out, 16)
                sp.wait_ge(shift_out, 16 * B)
                load_parts(0, 0, stk_again, 0)
                sp.wait_ge(stk_again, 16 * (NSTK - 1))

            def load_group(b, g, buf, parts_too=True):
                if parts_too:
                    load_parts(g, b, stk_in[buf], buf)
                sp.dma_start(q_stk[buf][96:99, :, :], shift_dram[b, :, bass.ds(HG * g, HG), :]).then_inc(stk_in[buf], 16)

            sp.wait_ge(zeros_set, 1)
            for g in range(NG):
                if g >= 2:
                    sp.wait_ge(s_free, NKT * HG * (g - 1) + 2)
                load_group(0, g, g % 2, g >= 1)
                if g == 0:
                    all_parts_out()
                if g >= 1:
                    for part in range(3 * g - 3, 3 * g):
                        n = ROW_TILES // 9
                        rows = xs_dram[n * P * part:n * P * (part + 1), :].rearrange("(t p) f -> p t f", p=P)
                        sp.dma_start(rows, zeros.unsqueeze(1).to_broadcast([P, n, D])).then_inc(xs_zero, 16)
            n = SLOT_TILES - (2 * SURE + 3)
            sp.dma_start(ys_dram[(2 * SURE + 3) * P:, :].rearrange("(t p) f -> p t f", p=P),
                         zeros.unsqueeze(1).to_broadcast([P, n, D])).then_inc(ys_zero, 16)
            with sp.Fori(0, NG // 2) as i:
                for o in range(2):
                    g = sp.snap(2 * i + o, min_val=0, max_val=NG - 1)
                    sp.wait_ge(s_free, 2 * NKT * HG * i + (NKT * HG * (NG + o - 1) + 2))
                    load_group(1, g, o)

            def load_w1(e):
                sp.dma_start(w1_sb[:, e], w1[e].rearrange("(k p) n -> p k n", p=P)).then_inc(w1_in, 16)

            sp.wait_ge(att_done, B * NG)
            sp.dma_start(sgw_sb[:, :, 0:D], shared_w.rearrange("(k p) n -> p k n", p=P)).then_inc(sgw_in, 16)
            sp.dma_start(sgw_sb[:, :, D:D + EXPERTS], gate_w.rearrange("(k p) n -> p k n", p=P)).then_inc(sgw_in, 16)
            for e in range(2, EXPERTS):
                load_w1(e)
            for b in range(B):
                with needed(nc.sync, sp, 1 + b):
                    sp.wait_ge(max2_split[b], 1)
                    for c in range(3):
                        at = CTX + 1 + H * c
                        sp.dma_start(hide_t[at:at + H, S * b:S * (b + 1)], neg_parts2[:, c, :]).then_inc(shift2_out[b], 16)
            sp.wait_ge(s2_free, 16)
            for e in range(2):
                load_w1(e)

            def expert(j):
                return nc.sync.value_load(tile_expert[0:1, bass.ds(j, 1)], min_val=0, max_val=EXPERTS - 1)

            def slots_of(j):
                return bass.ds(nc.sync.value_load(tile_row[0:1, bass.ds(j, 1)], min_val=0, max_val=ROW_TILES - 1) * P, P)

            def load_rows(slots, buf):
                sp.dma_start(xs_in[:, buf, :], xs_dram[slots, :]).then_inc(xs_landed[buf], 16)

            def load_b1(e, buf):
                sp.dma_start(b1_row[:, buf, :], b1[bass.ds(e, 1), :].partition_broadcast(P)).then_inc(b1_landed[buf], 16)

            def load_b2(e, buf):
                sp.dma_start(b2_row[:, buf, :], b2[bass.ds(e, 1), :].partition_broadcast(P)).then_inc(b2_landed[buf], 16)

            def step(j, buf):
                slots, e = slots_of(j + 2), expert(j + 2)
                sp.wait_ge(xs_ps, j + 1)
                load_rows(slots, buf)
                sp.wait_ge(h_sum, j + 1)
                load_b1(e, buf)
                e = expert(j + 1)
                sp.wait_ge(y_ready, j)
                sp.dma_start(ys_dram[bass.ds((j - 1) * P, P), :], y_sb[:, 1 - buf, :]).then_inc(y_stored[1 - buf], 16)
                load_b2(e, 1 - buf)

            sp.wait_ge(ys_zero, 16)
            sp.wait_ge(scattered, 16 * 2 * NT)
            sp.wait_ge(route_done, 1)
            for j in range(2):
                load_rows(slots_of(j), j)
                load_b1(expert(j), j)
                load_b2(expert(j), j)
            sp.wait_ge(xs_ps, 1)
            load_rows(slots_of(2), 0)
            sp.wait_ge(h_sum, 1)
            load_b1(expert(2), 0)
            def round_sp(i):
                for o in range(2):
                    step(2 * i + (o + 1), 1 - o)

            with sp.Fori(0, SURE) as i:
                round_sp(i)
            for i in range(SURE, PAIRS):
                may_run(nc.sync, sp, i, round_sp, lambda i: (
                    (xs_landed[0], 16 * (i + 2), 16), (xs_landed[1], 16 * (i + 1), 16),
                    (b1_landed[0], 16 * (i + 2), 16), (b1_landed[1], 16 * (i + 1), 16),
                    (b2_landed[0], 16 * (i + 1), 16), (b2_landed[1], 16 * (i + 1), 16),
                    (y_stored[0], 16 * i, 16), (y_stored[1], 16 * i, 16)))
            final = nc.sync.value_load(last_tile[0:1, 0:1], min_val=2 * SURE + 2, max_val=SLOT_TILES - 1)
            for j in range(SLOT_TILES - 2, SLOT_TILES + 1):
                tile = final + (j - SLOT_TILES)
                if j + 1 < SLOT_TILES:
                    e = expert(final)
                rows = bass.ds(nc.sync.snap(tile * P, min_val=0, max_val=(SLOT_TILES - 1) * P), P)
                sp.wait_ge(y_ready, j)
                sp.dma_start(ys_dram[rows, :], y_sb[:, (j - 1) % 2, :]).then_inc(y_stored[(j - 1) % 2], 16)
                if j + 1 < SLOT_TILES:
                    load_b2(e, (j + 1) % 2)
            out_rows = out.rearrange("b (a c o) f -> b o a c f", c=CP, o=2)
            for n, (first, end) in enumerate(ROUNDS):
                sp.wait_ge(out_ready, n + 1)
                b = first // CP
                for o in range(2):
                    sp.dma_start(out_rows[b, o][:, first - CP * b:end - CP * b, :], x_sb[64 * (1 - o):64 * (2 - o), first:end, :])\
                        .then_inc(out_done, 16)
            sp.wait_ge(out_done, 16 * 2 * len(ROUNDS))

        @block.gpsimd
        def _(pool):
            nc.gpsimd.memset(zeros, 0.0).then_inc(zeros_set, 1)
            nc.gpsimd.memset(seen[:, :], 0.0)
            nc.gpsimd.memset(seen_bf[:, :], 0.0).then_inc(seen_ready, 1)
            for buf in range(2):
                nc.gpsimd.memset(v_grp[buf][:, :, :, DH:DH + 1], 1.0)
                nc.gpsimd.memset(v_grp[buf][:, :, :, DH + 1:32], 0.0).then_inc(pool_link, 1)
            pool.wait_ge(pool_link, 2)
            nc.gpsimd.memset(hide_t[64:P, :], 0.0).then_inc(pool_link, 1)
            pool.wait_ge(pool_link, 3)
            nc.gpsimd.memset(v2_sb, 0.0)
            pool.wait_ge(late_in, 16 * LATE_DMAS)
            pool.wait_ge(xh_ready, NT)
            nc.gpsimd.tensor_tensor(x_sb[:, :, :], x_sb[:, :, :], attn_b_sb.unsqueeze(1).to_broadcast([P, NT, D]),
                                    ALU.add).then_inc(x_shifted, 1)

            def values_of(b, g):
                return v_sb[:, b, :, 64 * g:64 * (g + 1)].rearrange("p t (h d) -> p t h d", h=HG)

            pool.wait_ge(v_ready, len(v_at))
            pool.wait_ge(table_in, 16 * 8)
            for b in range(B):
                for g in range(NG):
                    n = NG * b + g
                    if n >= 2:
                        pool.wait_ge(p_free, NKT * (n - 1) + 2)
                    nc.gpsimd.tensor_copy(v_grp[n % 2][:, :, :, 0:DH], values_of(b, g)).then_inc(vg_ready, 1)
                    if b == 0:
                        if g >= 1:
                            pool.wait_ge(bias_ps, g)
                        if g >= 2:
                            nc.gpsimd.tensor_copy(t_grp[:, :], table[:, 512 + 64 * HG * g:512 + 64 * HG * g + TG])
                        for c in range(B):
                            last = nc.gpsimd.tensor_copy(v_bias[:, :, :, c, :], values_of(c, g))
                        last.then_inc(vb_ready, 1)
                    if n == 0:
                        for i in range(2):
                            pool.wait_ge(stk_in[i], 16 * NSTK)
                        nc.gpsimd.memset(k2_pad, 0.0).then_inc(work_zero, 1)

            def shift_batch(b, row):
                rows = x_sb[:, CP * b:CP * (b + 1), :]
                return nc.gpsimd.tensor_tensor(rows, rows, row.unsqueeze(1).to_broadcast([P, CP, D]), ALU.add)

            for b in range(B):
                pool.wait_ge(*((xh_ready, NT + CP), (second_ready, CP))[b])
                shift_batch(b, xbu_sb).then_inc(x_shifted, 1)
            pool.wait_ge(xs_zero, 16 * 9)

            def load_w2(e):
                pool.dma_start(w2_sb[:, e], w2[e].rearrange("(k p) n -> p k n", p=P)).then_inc(w2_in, 16)

            for ch in range(NT // CHUNK):
                if ch == NT // CHUNK - 1:
                    pool.wait_ge(x2_added, NT // 2)
                    load_w2(0)
                pool.wait_ge(slot_ready, ch + 1)
                for t in range(CHUNK * ch, CHUNK * (ch + 1)):
                    for k in range(2):
                        nc.gpsimd.indirect_dma_start(
                            out=xs_dram, out_offset=bass.IndirectOffsetOnAxis(ap=slot[:, k, t:t + 1], axis=0),
                            in_=xh[:, t, :], in_offset=None).then_inc(scattered, 16)
                pool.wait_ge(sg_read, 2 * (ch + 1))
                rows = acc[:, CHUNK * ch:CHUNK * (ch + 1), :]
                nc.gpsimd.tensor_tensor(rows, rows, shared_b_sb.unsqueeze(1).to_broadcast([P, CHUNK, D]), ALU.add)\
                    .then_inc(sh_added, 1)
                if ch == NT // CHUNK - 1:
                    for e in range(1, EXPERTS):
                        pool.wait_ge(w2_in, 16 * e)
                        load_w2(e)
            pool.wait_ge(sg_act, NT // 4)
            nc.gpsimd.tensor_scalar(acc, acc, 0.5, None, ALU.mult).then_inc(halved, 1)
            nc.gpsimd.tensor_tensor(x_sb[:, :, :], x_sb[:, :, :], ffn_b_sb.unsqueeze(1).to_broadcast([P, NT, D]),
                                    ALU.add).then_inc(x_shifted, 1)
            pool.wait_ge(moved_ready, 1)
            for i in range(2):
                pool.wait_ge(y_stored[i], 16 * ((SLOT_TILES + 1 - i) // 2))
            for n, (first, end) in enumerate(ROUNDS):
                for t in range(first, end):
                    for k in range(2):
                        nc.gpsimd.indirect_dma_start(
                            out=y_in[:, t, k, :], out_offset=None, in_=ys_dram,
                            in_offset=bass.IndirectOffsetOnAxis(ap=slot_y[:, k, t:t + 1], axis=0)).then_inc(y_landed[n], 16)

        @block.scalar
        def _(act):
            n_sqrt = [0]

            def sqrt_of_var(first, end):
                n_sqrt[0] += 1
                act.wait_ge(ln_var, n_sqrt[0])
                r = rstd[:, first:end]
                nc.scalar.activation(r, r, ACT.Sqrt).then_inc(ln_std, 1)

            def natural(b):
                act.wait_ge(xt_ready[b], CP // 2)
                for k in range(KC):
                    for o in range(2):
                        src = xt_tile[:, k, S * b + 64 * (1 - o):S * b + 64 * (1 - o) + 1]
                        dst = xt_nat[:, k, S * b + o:S * b + o + 1]
                        nc.scalar.copy(dims(dst, [2, CP], [16, 64]), dims(src, [P, CP], [1, 64])).then_inc(nat_ready, 1)

            sqrt_of_var(0, CP)
            for pair in range(CP // 2):
                act.wait_ge(xt_ps, pair + 1)
                nc.scalar.copy(xt_tile[:, :, 2 * P * pair:2 * P * (pair + 1)],
                               ps[:, 6 + pair % 2, :].rearrange("p (k n) -> p k n", k=KC)).then_inc(xt_ready[0], 1)
            sqrt_of_var(CP, NT)
            for b in range(B):
                natural(b)

            def first_part(q):
                act.wait_ge(proj_ps, qk_at[q] + 1)
                if q >= 4:
                    act.wait_ge(parts_out[q % 4], 16 * (q // 4))
                nc.scalar.copy(parts[:, q % 4, 0, :], ps[:, qk_at[q] % PB, :]).then_inc(part0, 1)

            def second_part(q):
                act.wait_ge(rest1, q + 1)
                nc.scalar.copy(parts[:, q % 4, 1, :], rest[:, q % 4, :]).then_inc(part1, 1)

            for c, (kind, m, n) in enumerate(proj):
                if c == v_at[0]:
                    second_part(len(qk_at) - 1)
                if kind == "v":
                    act.wait_ge(proj_ps, c + 1)
                    nc.scalar.copy(v_sb[:, m, 2 * n:2 * n + 2, :],
                                   ps[:, c % PB, :].rearrange("p (t f) -> p t f", t=2)).then_inc(v_ready, 1)
                else:
                    q = qk_at.index(c)
                    first_part(q)
                    if q >= 1:
                        second_part(q - 1)

            act.sem_inc(s_free, 2)
            with act.Fori(0, B * NG) as g:
                for st in range(NKT):
                    for h in range(HG):
                        u = HG * st + h
                        if h == 0:
                            act.wait_ge(p_free, NKT * g + (st + 1))
                        act.wait_ge(s_ready, NKT * HG * g + (u + 1))
                        nc.scalar.activation(probs[:, st % 2, h, :],
                                             ps[:, 2 * (u % 2):2 * (u % 2) + 2, :].rearrange("p a n -> p (a n)"),
                                             ACT.Exp, scale=float(D) ** -0.5).then_inc(s_free, 1)

            def turned_outputs(ch):
                for k in range(KC):
                    act.wait_ge(o2_ps, KC * ch + k + 1)
                    nc.scalar.copy(o2_t[:, k, :], ps[:, 6 + k, :]).then_inc(o2t_ready, 1)

            def turned_rows3(ch):
                for p in range(2):
                    act.wait_ge(x3_ps, 2 * ch + p + 1)
                    nc.scalar.copy(x3_t[:, :, 256 * p:256 * (p + 1)],
                                   ps[:, 6 + p, :].rearrange("p (k n) -> p k n", k=KC)).then_inc(x3_ready, 1)

            def shared_results(ch):
                if ch == 0:
                    act.wait_ge(xs_zero, 16 * 9)
                for p in range(2):
                    act.wait_ge(sg_ps, 2 * ch + p + 1)
                    t = CHUNK * ch + 2 * p
                    nc.scalar.copy(acc[:, t:t + 2, :], ps[:, 7 - p, :].rearrange("p (t f) -> p t f", t=2)).then_inc(sg_read, 1)

            for ch in range(NT // CHUNK):
                b, i = divmod(ch, 2)
                if i == 0:
                    with needed(nc.scalar, act, 1 + b):
                        act.wait_ge(shift2_out[b], 48)
                for hg in range(NG):
                    for pr in range(2):
                        u = 8 * ch + 2 * hg + pr
                        act.wait_ge(s2_ready, u + 1)
                        if pr == 0 and NG * ch + hg >= 2:
                            act.wait_ge(pv2_done, NG * ch + hg - 1)
                        nc.scalar.activation(probs2[:, hg % 2, 2 * pr:2 * pr + 2, :], ps[0:CTX + 1, 2 * (u % 2):2 * (u % 2) + 2, :],
                                             ACT.Exp, scale=float(DH) ** -0.5).then_inc(s2_free, 1)
                        if ch == 0 and (hg, pr) == (3, 0):
                            act.wait_ge(second_shift, 1)
                            for t in range(CP, NT):
                                nc.scalar.activation(xh[:, t, :], x_sb[:, t, :], ACT.Identity, scale=rstd[:, t:t + 1],
                                                     bias=shift[:, t:t + 1]).then_inc(second_ready, 1)
                        if ch >= 1 and (hg, pr) == (0, 1):
                            turned_outputs(ch - 1)
                        if ch >= 1 and (hg, pr) == (3, 0):
                            turned_rows3(ch - 1)
                if ch >= 1:
                    shared_results(ch - 1)
                if b == 0:
                    for p in range(2):
                        act.wait_ge(x2_ps, NG + 2 * i + p + 1)
                        nc.scalar.copy(x2_t[:, :, 256 * p:256 * (p + 1)],
                                       ps[:, 6 + p, :].rearrange("p (k n) -> p k n", k=KC)).then_inc(x2_ready, 1)
                    for m in range(KC):
                        act.wait_ge(q2_ps, NG + KC * i + m + 1)
                        nc.scalar.copy(q2_t[1][:, m, 512 * i:512 * (i + 1)], ps[:, 6 + m, :]).then_inc(q2_ready, 1)
            turned_outputs(3)
            turned_rows3(3)
            shared_results(3)
            act.wait_ge(both_ready, NT // CHUNK)
            nc.scalar.activation(over[:, :], over[:, :], ACT.Exp).then_inc(pair_ready, 1)
            for q in range(NT // 4):
                act.wait_ge(sh_added, q + 1)
                nc.scalar.activation(acc[:, 4 * q:4 * q + 4, :], acc[:, 4 * q:4 * q + 4, :], ACT.Gelu).then_inc(sg_act, 1)
            def turned_rows(j, buf, n):
                act.wait_ge(xs_ps, n)
                nc.scalar.copy(xs_t[:, buf, :, :], ps[:, 7, 0:KC * P].rearrange("p (k n) -> p k n", k=KC)).then_inc(xs_ready, 1)

            def activate(n):
                act.wait_ge(h_sum, n)
                nc.scalar.activation(hid, hid, ACT.Gelu).then_inc(h_act, 1)

            turned_rows(0, 0, 1)
            turned_rows(1, 1, 2)
            activate(1)
            turned_rows(2, 0, 3)
            activate(2)

            def round_act(i):
                for o in range(2):
                    turned_rows(2 * i + (o + 3), 1 - o, 2 * i + (o + 4))
                    activate(2 * i + (o + 3))

            with act.Fori(0, SURE) as i:
                round_act(i)
            for i in range(SURE, PAIRS):
                may_run(nc.scalar, act, i, round_act, lambda i: ((xs_ready, 2 * i + 3, 2), (h_act, 2 * i + 2, 2)))
            activate(SLOT_TILES)
            def weight_results(n):
                first, end = ROUNDS[n]
                act.wait_ge(y_landed[n], 32 * (end - first))
                if n == 0:
                    act.wait_ge(weights_set, 1)
                for t in range(first, end):
                    last = nc.scalar.activation(y_in[:, t, 0, :], y_in[:, t, 0, :], ACT.Copy, scale=weight[:, 0, t:t + 1])
                last.then_inc(y_weighted, 1)

            weight_results(0)
            for n, (first, end) in enumerate(ROUNDS):
                sqrt_of_var(first, end)
                act.wait_ge(out_moments, n + 1)
                for t in range(first, end):
                    last = nc.scalar.activation(acc[:, t, :], acc[:, t, :], ACT.Identity, scale=rstd[:, t:t + 1], bias=shift[:, t:t + 1])
                last.then_inc(out_normed, 1)
                if n + 1 < len(ROUNDS):
                    weight_results(n + 1)

        @block.vector
        def _(dve):
            links = [0]

            def link(ins):
                links[0] += 1
                ins.then_inc(dve_link, 1)
                dve.wait_ge(dve_link, links[0])

            n_ln = [0]

            def inverse_root(r, v, eps, n, link):
                s, t = root_s[:, 0:n], root_t[:, 0:n]
                link(nc.vector.tensor_scalar(s, v, eps, None, ALU.add))
                link(nc.vector.tensor_scalar(t.bitcast(I32), s.bitcast(I32), 1, None, ALU.logical_shift_right))
                link(nc.vector.tensor_scalar(r.bitcast(I32), t.bitcast(I32), -1.0, float(0x5F3759DF), ALU.mult, ALU.add))
                for _ in range(NEWTON):
                    link(nc.vector.scalar_tensor_tensor(out=t, in0=r, scalar=-0.5, in1=s, op0=ALU.mult, op1=ALU.mult))
                    link(nc.vector.tensor_tensor(t, t, r, ALU.mult))
                    link(nc.vector.scalar_tensor_tensor(out=r, in0=t, scalar=1.5, in1=r, op0=ALU.add, op1=ALU.mult))

            def normalise(src, dst, b, eps):
                for t in range(CP * b, CP * (b + 1)):
                    last = nc.vector.bn_stats(stats[:, t, :], src[:, t, :])
                link(last)
                for t in range(CP * b, CP * (b + 1)):
                    last = nc.vector.bn_aggr(mv[:, t, :], stats[:, t, :])
                link(last)
                r = rstd[:, CP * b:CP * (b + 1)]
                nc.vector.tensor_scalar(r, mv[:, CP * b:CP * (b + 1), 1], eps, None, ALU.add).then_inc(ln_var, 1)
                n_ln[0] += 1
                dve.wait_ge(ln_std, n_ln[0])
                link(nc.vector.reciprocal(r, r))
                for t in range(CP * b, CP * (b + 1)):
                    last = nc.vector.tensor_scalar(dst[:, t, :], src[:, t, :], mv[:, t, 0:1], rstd[:, t:t + 1],
                                                   ALU.subtract, ALU.mult)
                    last.then_inc(xh_ready, 1)

            for b in range(B):
                dve.wait_ge(x_in[b], 32)
                normalise(x_sb, xh, b, 1e-5)
            dve.wait_ge(w_in, 16 * 13)
            nc.vector.tensor_copy(table[:, 0:T0 + 8], last_row[:, 0:1].to_broadcast([P, T0 + 8])).then_inc(table_fill, 1)
            for pair in range(CP // 2, NT // 2):
                dve.wait_ge(xt_ps, pair + 1)
                nc.vector.tensor_copy(xt_tile[:, :, 2 * P * pair:2 * P * (pair + 1)],
                                      ps[:, 6 + pair % 2, :].rearrange("p (k n) -> p k n", k=KC)).then_inc(xt_ready[1], 1)
            nc.vector.memset(k_stk[0][96:99, :, :], 1.0)
            nc.vector.memset(k_stk[1][96:99, :, :], 1.0).then_inc(ones_set, 1)

            def first_rest(q):
                dve.wait_ge(part0, q + 1)
                nc.vector.tensor_tensor(rest[:, q % 4, :], ps[:, qk_at[q] % PB, :], parts[:, q % 4, 0, :],
                                        ALU.subtract).then_inc(rest1, 1)

            def third_part(q):
                dve.wait_ge(part1, q + 1)
                nc.vector.tensor_tensor(parts[:, q % 4, 2, :], rest[:, q % 4, :], parts[:, q % 4, 1, :],
                                        ALU.subtract).then_inc(part2, 1)

            def largest(q):
                kind, m, n = proj[qk_at[q]]
                nc.vector.tensor_reduce(sizes[:, m, "qk".index(kind), n:n + 1], parts[:, q % 4, 0, :], AX.X, ALU.max, apply_absolute_value=True)

            for q in range(len(qk_at)):
                first_rest(q)
                largest(q)
                if q >= 1:
                    third_part(q - 1)
            third_part(len(qk_at) - 1)

            def bound(scale, which, linked):
                nc.vector.tensor_tensor(size_prod, size[:, :, 0], size[:, :, 1], ALU.mult).then_inc(bound_in, 1)
                dve.wait_ge(bound_ps, which + 1)
                linked(nc.vector.tensor_copy(head_bound, ps[0:1, 7, 0:H]))
                linked(nc.vector.tensor_reduce(most[:, 0:1], head_bound, AX.X, ALU.max))
                nc.vector.tensor_scalar(flags[:, which:which + 1], most[:, 0:1], BOUND / scale, None, ALU.is_gt)\
                    .then_inc(flag_set, 1)

            dve.wait_ge(part2, len(qk_at))
            link(nc.vector.tensor_reduce(size, sizes, AX.X, ALU.max))
            bound(float(D) ** -0.5, 0, link)

            def link_on(s):
                n = [0]

                def linked(ins):
                    n[0] += 1
                    ins.then_inc(s, 1)
                    dve.wait_ge(s, n[0])
                return linked

            def negated_parts(rows, banks, into, linked, done):
                linked(nc.vector.tensor_scalar(rows, ps[0:H, 4:4 + banks, :].rearrange("p a n -> p (a n)"), -1.0, None, ALU.mult))
                linked(nc.vector.tensor_copy(into[:, 0, :], rows))
                linked(nc.vector.tensor_tensor(rows, rows, into[:, 0, :], ALU.subtract))
                linked(nc.vector.tensor_copy(into[:, 1, :], rows))
                nc.vector.tensor_tensor(into[:, 2, :], rows, into[:, 1, :], ALU.subtract).then_inc(done, 1)

            with needed(nc.vector, dve, 0):
                dve.sem_inc(max_read, 2)
                with dve.Fori(0, NG) as g:
                    for b in range(B):
                        for h in range(HG):
                            for t in range(CP):
                                u = CP * (HG * b + h) + t
                                dve.wait_ge(max_ps, B * HG * CP * g + (u + 1))
                                nc.vector.tensor_reduce(row_max[:, CP * b + t, bass.ds(HG * g + h, 1)],
                                                        ps[:, 2 * (u % 2):2 * (u % 2) + 2, :].rearrange("p a n -> p (a n)"),
                                                        AX.X, ALU.max).then_inc(max_read, 1)
                dve.wait_ge(max_tr, 1)
                for i in range(4):
                    dve.wait_ge(parts_out[i], 16 * (len(qk_at) // 4))
                negated_parts(neg_max, 4, neg_parts, link_on(dve_max), max_split)

            dve.sem_inc(dve_att, 1)
            dve.sem_inc(o_half, 1)
            dve.sem_inc(o_out, 1)

            def heads_of(b, g):
                return xh[:, CP * b:CP * (b + 1), bass.ds(64 * g, 64)].rearrange("p t (h d) -> p t h d", h=HG)

            turned = ps[:, 6:8, :].rearrange("p a (c h e) -> p (a c) h e", c=4, h=HG)

            def group_outputs(b, g):
                n = NG * b + g
                dve.wait_ge(half_in, n + 1)
                nc.vector.tensor_copy(o_t[:, 0:512], ps[:, 4, :]).then_inc(o_half, 1)
                dve.wait_ge(p_free, NKT * n + (NKT + 2))
                nc.vector.tensor_copy(o_t[:, 512:1024], ps[:, 5, :]).then_inc(o_out, 1)
                dve.wait_ge(o_tr, n + 1)
                nc.vector.reciprocal(rden[:, :, :], turned[:, :, :, DH]).then_inc(dve_att, 1)
                dve.wait_ge(dve_att, 2 * n + 2)
                nc.vector.tensor_tensor(o_n[:, :, :, :], turned[:, :, :, 0:DH],
                                        rden[:, :, :].unsqueeze(3).to_broadcast([P, CP, HG, DH]), ALU.mult).then_inc(dve_att, 1)
                dve.wait_ge(dve_att, 2 * n + 3)
                nc.vector.tensor_tensor(heads_of(b, g), heads_of(b, g), o_n[:, :, :, :], ALU.add).then_inc(att_done, 1)

            dve.wait_ge(ctx_ps, 1)
            link(nc.vector.tensor_copy(ctx_t[:, :, :, 0:CTX], ps[:, 6, 0:B * KC * (CTX + 1)].rearrange(
                "p (b k t) -> p b k t", b=B, k=KC)[:, :, :, 0:CTX]))
            nc.vector.tensor_reduce(ctx_t[:, :, :, CTX:CTX + 1], ctx_t[:, :, :, 0:CTX], AX.X, ALU.add).then_inc(ctx_ready, 1)
            dve.wait_ge(work_zero, 1)
            nc.vector.tensor_copy(v2_sb[:, :, :, DH], counts[:, 0:1].unsqueeze(2).to_broadcast([CTX + 1, B, H]))
            link(nc.vector.tensor_scalar(hide[:, :, 0:CTX], mask_sb, 0.0, NEG, ALU.is_equal, ALU.mult))
            link(nc.vector.tensor_reduce(hide_max[:, :], hide[:, :, 0:CTX], AX.X, ALU.max))
            nc.vector.tensor_scalar(hide[:, :, CTX], hide_max[:, :], -1.0, NEG, ALU.mult, ALU.add).then_inc(hide_ready, 1)
            dve.wait_ge(kv2_ps, 1)
            nc.vector.tensor_reduce(k2_size[:, :], ps[:, 6, 0:KC * B * CTX].rearrange("p (m n) -> p m n", m=KC),
                                    AX.X, ALU.max, apply_absolute_value=True)
            for m in range(KC):
                for j in range(H // KC):
                    last = nc.vector.tensor_scalar(k2_pad[:, :, H // KC * m + j, 0:CTX],
                                                   ps[:, 6, B * CTX * m:B * CTX * (m + 1)].rearrange("p (b t) -> p b t", b=B),
                                                   head_rows[:, j:j + 1], None, ALU.mult)
            last.then_inc(kv2_ready, 1)
            dve.wait_ge(kv2_ps, 2)
            nc.vector.tensor_copy(v2_sb[:, :, :, 0:DH], ps[0:CTX + 1, 6, :].rearrange("p (b h d) -> p b h d", b=B, h=H))\
                .then_inc(kv2_ready, 1)
            for i in range(2):
                dve.wait_ge(hide_ps, i + 1)
                nc.vector.tensor_copy(hide_t[0:CTX + 1, S * i:S * (i + 1)], ps[0:CTX + 1, 6, :].bitcast(BF16)).then_inc(hide_out, 1)

            for g in range(NG):
                nv = VARYING[g]
                dve.wait_ge(bias_ps, g + 1)
                if nv:
                    nc.vector.tensor_copy(bias_t[:, 0:P * nv], ps[:, 6, 0:P * nv])
                nc.vector.tensor_copy(bias_t[:, P * nv:P * (nv + 1)], ps[:, 7, 0:1].to_broadcast([P, P])).then_inc(bias_out, 1)
                dve.wait_ge(bias_tr, g + 1)
                for b in range(B):
                    if nv:
                        nc.vector.tensor_copy(heads_of(b, g)[:, 0:nv],
                                              ps[:, 6, 0:P * nv].rearrange("p (c h b d) -> p c h b d", c=nv, h=HG, b=B)[:, :, :, b, :])
                    const = ps[:, 7, 0:P].rearrange("p (h b d) -> p h b d", h=HG, b=B)[:, :, b, :]
                    last = nc.vector.tensor_copy(heads_of(b, g)[:, nv:CP], const.unsqueeze(1).to_broadcast([P, CP - nv, HG, DH]))
                last.then_inc(bias_read, 1)
                group_outputs(0, g)

            with dve.Fori(0, NG) as g:
                n = [0]

                def link_pair(ins):
                    n[0] += 1
                    ins.then_inc(dve_pair, 1)
                    dve.wait_ge(dve_pair, PAIR_LINKS * g + n[0])

                def tile(t, j):
                    return t[:, bass.ds(2 * g + j, 1), :].squeeze(1)

                def moments(src, eps):
                    nc.vector.memset(root_s[:, 0:2], 0.0)
                    for j in range(2):
                        last = nc.vector.bn_stats(pair_stats[:, j, :], tile(src, j))
                    link_pair(last)
                    nc.vector.memset(root_s[:, 0:2], 0.0)
                    for j in range(2):
                        last = nc.vector.bn_aggr(pair_mv[:, j, :], pair_stats[:, j, :])
                    link_pair(last)
                    inverse_root(pair_r[:, 0:2], pair_mv[:, :, 1], eps, 2, link_pair)

                dve.wait_ge(att_done, g + NG)
                dve.wait_ge(x_shifted, 1)
                moments(xh, 1e-3)
                for j in range(2):
                    last = nc.vector.scalar_tensor_tensor(out=tile(xh, j), in0=tile(xh, j), scalar=pair_mv[:, j, 0:1],
                                                          in1=attn_g_sb, op0=ALU.subtract, op1=ALU.mult)
                link_pair(last)
                for j in range(2):
                    last = nc.vector.scalar_tensor_tensor(out=tile(x_sb, j), in0=tile(xh, j), scalar=pair_r[:, j:j + 1],
                                                          in1=tile(x_sb, j), op0=ALU.mult, op1=ALU.add)
                link_pair(last)
                moments(x_sb, 1e-5)
                for j in range(2):
                    nc.vector.tensor_scalar(pair_rows[:, j, :], tile(x_sb, j), pair_mv[:, j, 0:1], pair_r[:, j:j + 1],
                                            ALU.subtract, ALU.mult).then_inc(xh_ready, 1)
                assert n[0] == PAIR_LINKS
                dve.wait_ge(x2_ps, g + 1)
                nc.vector.tensor_copy(x2_t[:, :, 0:256], ps[:, 6, :].rearrange("p (k n) -> p k n", k=KC)).then_inc(x2_ready, 1)
                dve.wait_ge(q2_ps, g + 1)
                pair_q = ps[:, 7, :].rearrange("p (m n) -> p m n", m=KC)
                nc.vector.tensor_reduce(sizes[:, :, 0, bass.ds(g, 1)], pair_q, AX.X, ALU.max, apply_absolute_value=True)
                nc.vector.tensor_copy(q2_t[0][:, :, bass.ds(256 * g, 256)], pair_q).then_inc(q2_ready, 1)
                group_outputs(1, g)

            def cross_bound(b, n):
                link(nc.vector.tensor_reduce(size[:, :, 0], sizes[:, :, 0, 0:n], AX.X, ALU.max))
                link(nc.vector.tensor_copy(size[:, :, 1], k2_size[:, :]))
                bound(float(DH) ** -0.5, 1 + b, link)
                with needed(nc.vector, dve, 1 + b):
                    linked = link_on(dve_max2[b])
                    for t in range(CP):
                        dve.wait_ge(max2_ps[b], t + 1)
                        ins = nc.vector.tensor_tensor(hidden_s.rearrange("p (g h) t -> p g h t", g=NG),
                                                      ps[:, 0:NG, 0:HG * CTX].rearrange("p g (h t) -> p g h t", h=HG),
                                                      hide[:, CP * b + t, 0:CTX].unsqueeze(1).unsqueeze(1).to_broadcast([P, NG, HG, CTX]),
                                                      ALU.add)
                        linked(ins)
                        dve.sem_inc(max2_read[b], 1)
                        linked(nc.vector.tensor_reduce(row_max2[:, t, :], hidden_s, AX.X, ALU.max))
                    nc.vector.tensor_scalar(row_max2, row_max2, -float(2 ** 90), None, ALU.max).then_inc(max2_done[b], 1)
                    dve.wait_ge(max2_tr[b], 1)
                    negated_parts(neg_max2, 2, neg_parts2, linked, max2_split[b])

            second = range(CP, NT)

            def second_moments(src):
                for t in second:
                    last = nc.vector.bn_stats(stats[:, t, :], src[:, t, :])
                link(last)
                for t in second:
                    last = nc.vector.bn_aggr(mv[:, t, :], stats[:, t, :])
                link(last)

            def second_root(eps):
                inverse_root(rstd[:, CP:NT], mv[:, CP:NT, 1], eps, CP, link)

            def second_scaled():
                for t in second:
                    last = nc.vector.scalar_tensor_tensor(out=xh[:, t, :], in0=xh[:, t, :], scalar=mv[:, t, 0:1],
                                                          in1=attn_g_sb, op0=ALU.subtract, op1=ALU.mult)
                link(last)

            def second_added():
                for t in second:
                    last = nc.vector.scalar_tensor_tensor(out=x_sb[:, t, :], in0=xh[:, t, :], scalar=rstd[:, t:t + 1],
                                                          in1=x_sb[:, t, :], op0=ALU.mult, op1=ALU.add)
                link(last)

            def second_normalised():
                nc.vector.scalar_tensor_tensor(out=shift[:, CP:NT], in0=mv[:, CP:NT, 0], scalar=-1.0, in1=rstd[:, CP:NT],
                                               op0=ALU.mult, op1=ALU.mult).then_inc(second_shift, 1)

            def second_sizes():
                dve.wait_ge(q2_ready, NG + 2 * KC + 1)
                link(nc.vector.tensor_reduce(sizes[:, :, 0, 0:1], q2_t[1], AX.X, ALU.max, apply_absolute_value=True))

            def leave(n):
                if n >= 2:
                    dve.wait_ge(o2_tr_done, n - 1)
                dve.wait_ge(pv2_done, n + 1)
                nc.vector.tensor_copy(o2_tr[:, n % 2, :], ps[:, 4, :]).then_inc(o2_out, 1)

            def divide(n):
                hg = n % NG
                dve.wait_ge(o2_tr_done, n + 1)
                turned2 = ps[:, 5, :].rearrange("p (t h e) -> p t h e", t=CHUNK, h=HG)
                link(nc.vector.reciprocal(rden2, turned2[:, :, :, DH]))
                nc.vector.tensor_tensor(o2[:, :, 64 * hg:64 * (hg + 1)].rearrange("p t (h d) -> p t h d", h=HG),
                                        turned2[:, :, :, 0:DH],
                                        rden2.unsqueeze(3).to_broadcast([P, CHUNK, HG, DH]), ALU.mult).then_inc(o2_div, 1)

            def add_cross(ch):
                dve.wait_ge(x_shifted, 2 + ch // 2)
                for p in range(2):
                    dve.wait_ge(u_ps, 2 * ch + p + 1)
                    xs = x_sb[:, CHUNK * ch + 2 * p:CHUNK * ch + 2 * p + 2, :]
                    nc.vector.tensor_tensor(xs, ps[:, 6 + p, :].rearrange("p (t f) -> p t f", t=2), xs, ALU.add).then_inc(x2_added, 1)

            def moments3(ch):
                dve.wait_ge(x2_added, 2 * ch + 2)
                tiles = range(CHUNK * ch, CHUNK * (ch + 1))
                for t in tiles:
                    last = nc.vector.bn_stats(stats[:, t, :], x_sb[:, t, :])
                link(last)
                for t in tiles:
                    last = nc.vector.bn_aggr(mv[:, t, :], stats[:, t, :])
                link(last)

            def root3(ch):
                rows = slice(CHUNK * ch, CHUNK * (ch + 1))
                inverse_root(rstd[:, rows], mv[:, rows, 1], 1e-5, CHUNK, link)

            def normalise3(ch):
                for t in range(CHUNK * ch, CHUNK * (ch + 1)):
                    nc.vector.tensor_scalar(xh[:, t, :], x_sb[:, t, :], mv[:, t, 0:1], rstd[:, t:t + 1],
                                            ALU.subtract, ALU.mult).then_inc(xh_ready, 1)

            e_names = [P, CHUNK, EXPERTS]
            at = [EXPERTS * NT, EXPERTS, EXPERTS * EXPERTS, EXPERTS]
            at = [0] + [sum(at[:n + 1]) for n in range(4)]
            thresholds, rev, tri, region, tiles_c = (route_c[:, a:b] for a, b in zip(at, at[1:] + [at[-1] + SLOT_TILES * EXPERTS]))
            thresholds = thresholds.rearrange("p (e j) -> p e j", e=EXPERTS)
            tri = tri.rearrange("p (e f) -> p e f", e=EXPERTS)
            tiles_c = tiles_c.rearrange("p (j e) -> p j e", e=EXPERTS)

            def first_largest(values, top, picked):
                link(nc.vector.tensor_reduce(top, values, AX.X, ALU.max))
                link(nc.vector.tensor_tensor(hit, values, top.unsqueeze(2).to_broadcast(e_names), ALU.is_equal))
                link(nc.vector.tensor_tensor(cand, hit, rev.unsqueeze(1).to_broadcast(e_names), ALU.mult))
                link(nc.vector.tensor_reduce(best, cand, AX.X, ALU.max))
                link(nc.vector.tensor_tensor(picked, cand, best.unsqueeze(2).to_broadcast(e_names), ALU.is_equal))

            def choose(ch):
                dve.wait_ge(gate_ps, ch + 1)
                link(nc.vector.tensor_copy(logits, ps[:, 6, 0:CHUNK * EXPERTS].rearrange("p (t e) -> p t e", t=CHUNK)))
                dve.sem_inc(gate_read, 1)
                pick1, pick2 = (picks[:, k, CHUNK * ch:CHUNK * (ch + 1), :] for k in range(2))
                first_largest(logits, top1, pick1)
                link(nc.vector.scalar_tensor_tensor(out=lg2, in0=pick1, scalar=NEG, in1=logits, op0=ALU.mult, op1=ALU.add))
                first_largest(lg2, top2, pick2)
                nc.vector.tensor_tensor(over[:, CHUNK * ch:CHUNK * (ch + 1)], top2, top1, ALU.subtract)
                nc.vector.tensor_tensor(both, pick1, pick2, ALU.add).then_inc(both_ready, 1)

            def place(ch):
                dve.wait_ge(rank_ps, ch + 1)
                link(nc.vector.tensor_tensor(pos, ps[:, 7, 0:CHUNK * EXPERTS].rearrange("p (t e) -> p t e", e=EXPERTS),
                                             region.unsqueeze(1).to_broadcast(e_names), ALU.add))
                dve.sem_inc(rank_read, 1)
                rows = slice(CHUNK * ch, CHUNK * (ch + 1))
                for k in range(2):
                    link(nc.vector.tensor_tensor(hit, picks[:, k, rows, :], pos, ALU.mult))
                    link(nc.vector.tensor_reduce(place_f[:, k, rows], hit, AX.X, ALU.add))
                nc.vector.tensor_copy(slot[:, :, rows], place_f[:, :, rows]).then_inc(slot_ready, 1)
                if ch == NT // CHUNK - 1:
                    return
                link(nc.vector.tensor_reduce(both_n, both.rearrange("p t e -> p e t"), AX.X, ALU.add))
                link(nc.vector.tensor_tensor(seen[:, :], seen[:, :], both_n, ALU.add))
                nc.vector.tensor_copy(seen_bf[:, :], seen[:, :]).then_inc(seen_ready, 1)

            dve.wait_ge(seen_ready, 1)
            cross_bound(0, NG)
            for ch in range(NT // CHUNK):
                b, i = divmod(ch, 2)
                n = NG * ch
                if ch == 2:
                    second_sizes()
                    divide(n - 1)
                    cross_bound(1, 1)
                if ch == 0:
                    dve.wait_ge(att_done, B * NG)
                    second_moments(xh)
                    second_root(1e-3)
                    leave(n)
                    second_scaled()
                    divide(n)
                    leave(n + 1)
                    second_added()
                    second_moments(x_sb)
                    divide(n + 1)
                    leave(n + 2)
                    second_root(1e-5)
                    second_normalised()
                    divide(n + 2)
                else:
                    if ch != 2:
                        divide(n - 1)
                    if ch >= 2:
                        place(ch - 2)
                    add_cross(ch - 1)
                    moments3(ch - 1)
                    leave(n)
                    root3(ch - 1)
                    divide(n)
                    normalise3(ch - 1)
                    leave(n + 1)
                    divide(n + 1)
                    leave(n + 2)
                    choose(ch - 1)
                    divide(n + 2)
                leave(n + 3)
            divide(15)
            place(2)
            add_cross(3)
            moments3(3)
            root3(3)
            normalise3(3)
            choose(3)
            place(3)
            dve.wait_ge(count_ps, 1)
            link(nc.vector.tensor_tensor(full, thresholds, ps[:, 6, 0:EXPERTS].unsqueeze(2).to_broadcast([P, EXPERTS, NT]), ALU.is_lt))
            link(nc.vector.tensor_reduce(tiles_of, full, AX.X, ALU.add))
            link(nc.vector.tensor_tensor(full[:, :, 0:EXPERTS], tri, tiles_of.unsqueeze(1).to_broadcast([P, EXPERTS, EXPERTS]),
                                         ALU.mult))
            link(nc.vector.tensor_reduce(base, full[:, :, 0:EXPERTS], AX.X, ALU.add))
            link(nc.vector.tensor_tensor(ends, base, tiles_of, ALU.add))
            by_tile = [P, SLOT_TILES, EXPERTS]
            link(nc.vector.tensor_tensor(ended, ends.unsqueeze(1).to_broadcast(by_tile), tiles_c, ALU.is_le))
            nc.vector.tensor_reduce(ended_n, ended, AX.X, ALU.add)
            link(nc.vector.tensor_tensor(ended_x, ended, tiles_of.unsqueeze(1).to_broadcast(by_tile), ALU.mult))
            link(nc.vector.tensor_reduce(ended_w, ended_x, AX.X, ALU.add))
            link(nc.vector.tensor_tensor(rowf, tiles_c[:, :, 0], ended_w, ALU.subtract))
            nc.vector.tensor_scalar(tile_expert[:, :], ended_n, EXPERTS - 1.0, None, ALU.min)
            for i in range(SURE, PAIRS):
                last = nc.vector.tensor_scalar(run_f[:, i - SURE:i - SURE + 1], ends[:, EXPERTS - 1:EXPERTS], 2.0 * i + 3, None, ALU.is_gt)
            link(last)
            nc.vector.tensor_copy(run, run_f)
            link(nc.vector.tensor_reduce(last_f, run_f, AX.X, ALU.add))
            nc.vector.tensor_scalar(last_tile, last_f, 2.0, 2.0 * SURE + 2, ALU.mult, ALU.add)
            nc.vector.scalar_tensor_tensor(out=tile_row[:, :], in0=ended_n, scalar=float(REGION_TILES), in1=rowf,
                                           op0=ALU.mult, op1=ALU.add).then_inc(route_done, 1)
            link(nc.vector.scalar_tensor_tensor(out=delta, in0=base, scalar=float(P), in1=region, op0=ALU.mult, op1=ALU.subtract))
            link(nc.vector.tensor_tensor(moved, picks[:, :, :, :].rearrange("p k t e -> p (k t) e"),
                                         delta.unsqueeze(1).to_broadcast([P, 2 * NT, EXPERTS]), ALU.mult))
            link(nc.vector.tensor_reduce(move, moved, AX.X, ALU.add))
            nc.vector.tensor_tensor(slot_y[:, :, :].rearrange("p k t -> p (k t)"), move,
                                    place_f[:, :, :].rearrange("p k t -> p (k t)"), ALU.add).then_inc(moved_ready, 1)
            dve.wait_ge(pair_ready, 1)
            link(nc.vector.tensor_scalar(over_one[:, :], over[:, :], 1.0, None, ALU.add))
            link(nc.vector.reciprocal(weight[:, 0, :], over_one[:, :]))
            link(nc.vector.tensor_tensor(weight[:, 1, :], over[:, :], weight[:, 0, :], ALU.mult))
            dve.sem_inc(weights_set, 1)

            def sum_hidden(buf, n, nb):
                dve.wait_ge(h_ps, n)
                dve.wait_ge(b1_landed[buf], nb)
                nc.vector.tensor_tensor(hid, ps[:, 0:2, :].rearrange("p a n -> p (a n)"), b1_row[:, buf, :],
                                        ALU.add).then_inc(h_sum, 1)

            def turned_hidden(n):
                dve.wait_ge(ht_ps, n)
                nc.vector.tensor_copy(hid_t, ps[:, 4:6, :].rearrange("p a (k n) -> p (a k) n", n=P)).then_inc(ht_ready, 1)

            def result(buf, n, landed, stored=None):
                dve.wait_ge(y_ps, n)
                dve.wait_ge(b2_landed[buf], landed)
                if stored is not None:
                    dve.wait_ge(y_stored[buf], stored)
                nc.vector.tensor_tensor(y_sb[:, buf, :], ps[:, 6, 0:D], b2_row[:, buf, :], ALU.add).then_inc(y_ready, 1)

            sum_hidden(0, 1, 16)
            turned_hidden(1)
            sum_hidden(1, 2, 16)
            result(0, 1, 16)

            def round_dve(i, first=False):
                for o in range(2):
                    turned_hidden(2 * i + (o + 2))
                    sum_hidden(o, 2 * i + (o + 3), 16 * i + 32)
                    result(1 - o, 2 * i + (o + 2), 16 * i + 16 * (o + 1), None if first and o == 0 else 16 * i + 16 * o)

            round_dve(0, True)
            with dve.Fori(1, SURE) as i:
                round_dve(i)
            for i in range(SURE, PAIRS):
                may_run(nc.vector, dve, i, round_dve, lambda i: (
                    (h_sum, 2 * i + 2, 2), (ht_ready, 2 * i + 1, 2), (y_ready, 2 * i + 1, 2)))
            turned_hidden(SLOT_TILES - 1)
            sum_hidden(0, SLOT_TILES, 16 * (PAIRS + 2))
            result(1, SLOT_TILES - 1, 16 * (PAIRS + 1), 16 * PAIRS)
            turned_hidden(SLOT_TILES)
            result(0, SLOT_TILES, 16 * (PAIRS + 2), 16 * (PAIRS + 1))
            dve.wait_ge(halved, 1)
            dve.wait_ge(x_shifted, 2 + B)

            def finish(n):
                rows = slice(*ROUNDS[n])
                dve.wait_ge(out_normed, n + 1)
                tiles = ROUNDS[n][1] - ROUNDS[n][0]
                link(nc.vector.tensor_tensor(acc[:, rows, :], acc[:, rows, :], ffn_g_sb.unsqueeze(1).to_broadcast([P, tiles, D]), ALU.mult))
                nc.vector.tensor_tensor(x_sb[:, rows, :], x_sb[:, rows, :], acc[:, rows, :], ALU.add).then_inc(out_ready, 1)

            for n, (first, end) in enumerate(ROUNDS):
                tiles = range(first, end)
                dve.wait_ge(y_landed[n], 32 * (end - first))
                rows = slice(first, end)
                for t in tiles:
                    last = nc.vector.scalar_tensor_tensor(out=acc[:, t, :], in0=y_in[:, t, 1, :], scalar=weight[:, 1, t:t + 1],
                                                          in1=acc[:, t, :], op0=ALU.mult, op1=ALU.add)
                link(last)
                dve.wait_ge(y_weighted, n + 1)
                link(nc.vector.tensor_tensor(acc[:, rows, :], acc[:, rows, :], y_in[:, rows, 0, :], ALU.add))
                for t in tiles:
                    last = nc.vector.bn_stats(stats[:, t, :], acc[:, t, :])
                link(last)
                for t in tiles:
                    last = nc.vector.bn_aggr(mv[:, t, :], stats[:, t, :])
                link(last)
                r = rstd[:, first:end]
                nc.vector.tensor_scalar(r, mv[:, first:end, 1], 1e-5, None, ALU.add).then_inc(ln_var, 1)
                dve.wait_ge(ln_std, B + n + 1)
                link(nc.vector.reciprocal(r, r))
                nc.vector.scalar_tensor_tensor(out=shift[:, rows], in0=mv[:, rows, 0], scalar=-1.0, in1=r, op0=ALU.mult, op1=ALU.mult)\
                    .then_inc(out_moments, 1)
                if n >= 1:
                    finish(n - 1)
            finish(len(ROUNDS) - 1)

        @block.tensor
        def _(pe):
            pe.wait_ge(w_in, 16 * 13)
            def head_bounds(which):
                pe.wait_ge(bound_in, which + 1)
                for m in range(KC):
                    last = nc.tensor.matmul(ps[0:1, 7, 8 * m:8 * m + 8], size_prod[:, m:m + 1], head_rows,
                                            start=True, stop=True)
                last.then_inc(bound_ps, 1)

            def turn_pair(pair):
                pe.wait_ge(xh_ready, 2 * pair + 2)
                if pair >= 2:
                    b, n = divmod(pair - 2, CP // 2)
                    pe.wait_ge(xt_ready[b], n + 1)
                for k in range(KC):
                    for j in range(2):
                        last = nc.tensor.transpose(ps[:, 6 + pair % 2, 256 * k + P * j:256 * k + P * (j + 1)],
                                                   xh[:, 2 * pair + j, P * k:P * (k + 1)], ident[:, :])
                last.then_inc(xt_ps, 1)

            def project(c):
                kind, m, n = proj[c]
                if c >= PB:
                    if proj[c - PB][0] == "v":
                        pe.wait_ge(v_ready, v_at.index(c - PB) + 1)
                    else:
                        pe.wait_ge(rest1, qk_at.index(c - PB) + 1)
                if c == 0:
                    pe.wait_ge(xt_ready[0], CP // 2)
                if c == 2:
                    pe.wait_ge(xt_ready[1], CP // 2)
                if c == proj.index(("k", 0, 0)):
                    pe.wait_ge(nat_ready, 4 * B)
                bank = ps[:, c % PB, :]
                if kind == "v":
                    for j in range(2):
                        t = S * m + P * (2 * n + j)
                        for k in range(KC):
                            last = nc.tensor.matmul(bank[:, D * j:D * (j + 1)], xt_nat[:, k, t:t + P], wv_sb[:, k, :],
                                                    start=(k == 0), stop=(k == KC - 1))
                else:
                    w, src = (wq_sb, xt_tile) if kind == "q" else (wk_sb, xt_nat)
                    for k in range(KC):
                        last = nc.tensor.matmul(bank, w[:, k, P * m:P * (m + 1)], src[:, k, 512 * n:512 * (n + 1)],
                                                start=(k == 0), stop=(k == KC - 1))
                last.then_inc(proj_ps, 1)
            for pair in range(CP // 2):
                turn_pair(pair)
            for c in range(2):
                project(c)
            for pair in range(CP // 2, NT // 2):
                turn_pair(pair)
            for c in range(2, len(proj)):
                if c == len(proj) - 2:
                    head_bounds(0)
                project(c)
            pe.wait_ge(rest1, len(qk_at))
            pe.wait_ge(v_ready, len(v_at))

            def turn_maxima(maxima, tiles, into):
                for t in range(tiles):
                    last = nc.tensor.transpose(ps[0:H, 4 + t // 4, P * (t % 4):P * (t % 4 + 1)], maxima[:, t, :], ident[:, :])
                last.then_inc(into, 1)

            with needed(nc.tensor, pe, 0):
                with pe.Fori(0, NG) as g:
                    for b in range(B):
                        pe.wait_ge(max_in[b], 16 * (NSTK - 1) * g + 16 * (NSTK - 1))
                        for h in range(HG):
                            for t in range(CP):
                                u = CP * (HG * b + h) + t
                                pe.wait_ge(max_read, B * HG * CP * g + (u + 1))
                                for half in range(2):
                                    last = nc.tensor.matmul(ps[:, 2 * (u % 2) + half, :], q_stk[b][0:96, h, P * t:P * (t + 1)],
                                                            k_stk[b][0:96, h, 512 * half:512 * (half + 1)], start=True, stop=True)
                                last.then_inc(max_ps, 1)
                pe.wait_ge(max_read, B * HG * CP * NG + 2)
                turn_maxima(row_max, NT, max_tr)

            def context(part):
                if part == 0:
                    pe.wait_ge(late_in, 16 * LATE_DMAS)
                    pe.wait_ge(table_in, 16 * 8)
                    for b in range(B):
                        for k in range(KC):
                            at = (CTX + 1) * (KC * b + k)
                            last = nc.tensor.transpose(ps[:, 6, at:at + CTX], ctx_sb[:, b, P * k:P * (k + 1)], ident[0:CTX, 0:CTX])
                    last.then_inc(ctx_ps, 1)
                elif part == 1:
                    pe.wait_ge(ctx_ready, 1)
                    for m in range(KC):
                        for k in range(KC):
                            last = nc.tensor.matmul(ps[:, 6, B * CTX * m:B * CTX * (m + 1)], xwk_sb[:, k, P * m:P * (m + 1)],
                                                    ctx_t[:, :, k, 0:CTX], start=(k == 0), stop=(k == KC - 1))
                    last.then_inc(kv2_ps, 1)
                elif part == 2:
                    pe.wait_ge(kv2_ready, 1)
                    for b in range(B):
                        for k in range(KC):
                            last = nc.tensor.matmul(ps[0:CTX + 1, 6, D * b:D * (b + 1)], ctx_t[:, b, k, :], xwv_sb[:, k, :],
                                                    start=(k == 0), stop=(k == KC - 1))
                    last.then_inc(kv2_ps, 1)
                elif part == 3:
                    pe.wait_ge(kv2_ready, 2)
                    pe.wait_ge(hide_ready, 1)
                if part in (3, 4):
                    if part == 4:
                        pe.wait_ge(hide_out, 1)
                    bank = ps[0:CTX + 1, 6, :].bitcast(BF16)
                    for t in range(CP):
                        last = nc.tensor.transpose(bank[:, P * t:P * (t + 1)], hide[:, CP * (part - 3) + t, :], ident_bf[:, :])
                    last.then_inc(hide_ps, 1)

            def turn_group(n, half):
                if half == 0:
                    pe.wait_ge(o_out, n + 1)
                for c in range(4):
                    last = nc.tensor.transpose(ps[:, 6 + half, P * c:P * (c + 1)], o_t[:, 512 * half + P * c:512 * half + P * (c + 1)],
                                               ident[:, :])
                if half == 1:
                    last.then_inc(o_tr, 1)

            def values(n, buf, st, half):
                if st < 0:
                    buf = 1 - buf
                if half == 0:
                    pe.wait_ge(s_free, NKT * HG * n + (HG * (st + 1) + 2))
                    if st == 0:
                        pe.wait_ge(vg_ready, n + 1)
                if st == 0:
                    pe.wait_ge((o_half, o_out)[half], n + 1)
                kt = st % NKT
                for h in range(HG):
                    last = nc.tensor.matmul(ps[32 * h:32 * h + 32, 4 + half, :], v_grp[buf][:, kt, h, :],
                                            probs[:, kt % 2, h, 512 * half:512 * (half + 1)],
                                            start=(kt == 0), stop=(kt == NKT - 1), tile_position=(0, 32 * h))
                if half == 1:
                    last.then_inc(p_free, 1)
                elif kt == NKT - 1:
                    last.then_inc(half_in, 1)

            pe.sem_inc(p_free, 2)

            def attention(b, g, buf):
                n = NG * b + g

                def scores(st, h):
                    if st == 0 and h == 0:
                        pe.wait_ge(stk_in[buf], 8 * NSTK * n + (16 - 8 * buf) * NSTK)
                    u = HG * st + h
                    pe.wait_ge(s_free, NKT * HG * n + (u + 1))
                    for half in range(2):
                        last = nc.tensor.matmul(ps[:, 2 * (u % 2) + half, :], k_stk[buf][:, h, P * st:P * (st + 1)],
                                                q_stk[buf][:, h, 512 * half:512 * (half + 1)], start=True, stop=True)
                    last.then_inc(s_ready, 1)

                def bias(jt):
                    nv = VARYING[g]
                    if jt == 0:
                        pe.wait_ge(dve_att, 2 * n + 1)
                        pe.wait_ge(vb_ready, g + 1)
                    if nv:
                        for h in range(HG):
                            start = 440 + 64 * h - 8 * jt
                            row = dims(t_grp[:, start:start + 1], [-P, nv], [1, P])
                            nc.tensor.matmul(ps[32 * h:32 * h + 32, 6, 0:P * nv], v_bias[:, jt, h, :, :].rearrange("p b d -> p (b d)"),
                                             row, start=(jt == 0), stop=(jt == NKT - 1), tile_position=(0, 32 * h))
                    for h in range(HG):
                        last = nc.tensor.matmul(ps[32 * h:32 * h + 32, 7, 0:2], v_bias[:, jt, h, :, :].rearrange("p b d -> p (b d)"),
                                                table[:, 0:2], start=(jt == 0), stop=(jt == NKT - 1), tile_position=(0, 32 * h))
                    if jt == NKT - 1:
                        last.then_inc(bias_ps, 1)

                def beside(st, half):
                    if st == 2 and not (b == 0 and g == 0):
                        if half == 0 and b == 0:
                            pe.wait_ge(bias_read, g)
                        if half == 0 and b == 1:
                            pe.wait_ge(q2_ready, g + 1)
                        turn_group(n, half)
                    if b == 0:
                        if g == 0 and 1 <= st <= 5 and half == 1:
                            context(st - 1)
                        if 3 <= st <= 6:
                            bias(2 * (st - 3) + half)
                        if st == 7 and half == 1:
                            pe.wait_ge(bias_out, g + 1)
                            if g == 0:
                                pe.wait_ge(hide_out, 2)
                            nv = VARYING[g]
                            for c in range(nv):
                                nc.tensor.transpose(ps[:, 6, P * c:P * (c + 1)], bias_t[:, P * c:P * (c + 1)], ident[:, :])
                            nc.tensor.transpose(ps[:, 7, 0:P], bias_t[:, P * nv:P * (nv + 1)], ident[:, :]).then_inc(bias_tr, 1)
                    elif st == 7 and half == 0:
                        pe.wait_ge(xh_ready, 2 * g + (NT + 2))
                        pe.wait_ge(dve_att, 2 * n + 1)
                        for k in range(KC):
                            for j in range(2):
                                last = nc.tensor.transpose(ps[:, 6, 256 * k + P * j:256 * k + P * (j + 1)],
                                                           pair_rows[:, j, P * k:P * (k + 1)], ident[:, :])
                        last.then_inc(x2_ps, 1)
                    elif st == 7:
                        pe.wait_ge(x2_ready, g + 1)
                        for m in range(KC):
                            for k in range(KC):
                                last = nc.tensor.matmul(ps[:, 7, 256 * m:256 * (m + 1)], xwq_sb[:, k, P * m:P * (m + 1)],
                                                        x2_t[:, k, 0:256], start=(k == 0), stop=(k == KC - 1))
                        last.then_inc(q2_ps, 1)

                for st in range(NKT):
                    for h in range(HG):
                        scores(st, h)
                        if h % 2 == 1:
                            if not (b == 0 and g == 0 and st == 0):
                                values(n, buf, st - 1, h // 2)
                            beside(st, h // 2)

            pe.sem_inc(q2_ready, 1)
            for g in range(NG):
                attention(0, g, g % 2)
            with pe.Fori(0, NG // 2) as i:
                for o in range(2):
                    attention(1, 2 * i + o, o)
            for half in range(2):
                values(B * NG - 1, 1, NKT - 1, half)
            pe.wait_ge(q2_ready, NG + 1)
            for half in range(2):
                turn_group(B * NG, half)

            def scores2(ch, hg, pr):
                b, i = divmod(ch, 2)
                u = 8 * ch + 2 * hg + pr
                if u >= 2:
                    pe.wait_ge(s2_free, u - 1)
                at = slice(512 * i, 512 * (i + 1))
                for hh in range(2):
                    h = HG * hg + 2 * pr + hh
                    bank = ps[0:CTX + 1, 2 * (u % 2) + hh, :]
                    nc.tensor.matmul(bank, k2_pad[:, b, h, :], q2_t[b][:, h // 8, at], start=True, stop=False)
                    last = nc.tensor.matmul(bank, pick[:, h, :], hide_t[0:CTX + 1 + 3 * H, 512 * ch:512 * (ch + 1)],
                                            start=False, stop=True)
                last.then_inc(s2_ready, 1)

            def values2(n):
                ch, hg = divmod(n, NG)
                if n >= 1:
                    pe.wait_ge(o2_out, n)
                pe.wait_ge(s2_free, 2 * n + 2)
                for h in range(HG):
                    last = nc.tensor.matmul(ps[32 * h:32 * h + 32, 4, :], v2_sb[:, ch // 2, HG * hg + h, :],
                                            probs2[:, hg % 2, h, :], start=True, stop=True, tile_position=(0, 32 * h))
                last.then_inc(pv2_done, 1)

            def turn2(n):
                pe.wait_ge(o2_out, n + 1)
                if n >= 1:
                    pe.wait_ge(o2_div, n)
                for t in range(CHUNK):
                    last = nc.tensor.transpose(ps[:, 5, P * t:P * (t + 1)], o2_tr[:, n % 2, P * t:P * (t + 1)], ident[:, :])
                last.then_inc(o2_tr_done, 1)

            def outputs(ch):
                pe.wait_ge(o2_div, NG * (ch + 1))
                if ch < 2:
                    pe.wait_ge(q2_ready, NG + KC * (ch + 1) + 1)
                else:
                    pe.wait_ge(sg_read, 2 * ch)
                if ch >= 1:
                    pe.wait_ge(rank_read, ch)
                for k in range(KC):
                    for t in range(CHUNK):
                        last = nc.tensor.transpose(ps[:, 6 + k, P * t:P * (t + 1)], o2[:, t, P * k:P * (k + 1)], ident[:, :])
                    last.then_inc(o2_ps, 1)

            def add_product(ch):
                pe.wait_ge(o2t_ready, KC * (ch + 1))
                for p in range(2):
                    for t in range(2):
                        for k in range(KC):
                            last = nc.tensor.matmul(ps[:, 6 + p, D * t:D * (t + 1)], o2_t[:, k, P * (2 * p + t):P * (2 * p + t + 1)],
                                                    xwu_sb[:, k, :], start=(k == 0), stop=(k == KC - 1))
                    last.then_inc(u_ps, 1)

            def turn_rows(first, bank_free, done):
                for p in range(2):
                    pe.wait_ge(*bank_free[p])
                    for k in range(KC):
                        for j in range(2):
                            last = nc.tensor.transpose(ps[:, 6 + p, 256 * k + P * j:256 * k + P * (j + 1)],
                                                       xh[:, first + 2 * p + j, P * k:P * (k + 1)], ident[:, :])
                    last.then_inc(done, 1)

            def rows3(ch):
                ready = (xh_ready, NT + CP + CHUNK * (ch + 1))
                turn_rows(CHUNK * ch, (ready, ready), x3_ps)

            def gates(ch):
                if ch == 0:
                    pe.wait_ge(sgw_in, 32)
                pe.wait_ge(x3_ready, 2 * (ch + 1))
                for t in range(CHUNK):
                    for k in range(KC):
                        last = nc.tensor.matmul(ps[:, 6, EXPERTS * t:EXPERTS * (t + 1)], x3_t[:, k, P * t:P * (t + 1)],
                                                sgw_sb[:, k, D:], start=(k == 0), stop=(k == KC - 1))
                last.then_inc(gate_ps, 1)

            def shared(ch, p):
                if p == 1:
                    pe.wait_ge(gate_read, ch + 1)
                for t in range(2):
                    for k in range(KC):
                        last = nc.tensor.matmul(ps[:, 7 - p, D * t:D * (t + 1)], x3_t[:, k, P * (2 * p + t):P * (2 * p + t + 1)],
                                                sgw_sb[:, k, 0:D], start=(k == 0), stop=(k == KC - 1))
                last.then_inc(sg_ps, 1)

            def ranks(ch):
                pe.wait_ge(both_ready, ch + 1)
                pe.wait_ge(seen_ready, ch + 1)
                pe.wait_ge(sg_read, 2 * ch + 1)
                if ch == 0:
                    pe.wait_ge(q2_ready, NG + 2 * KC + 1)
                n = CHUNK * EXPERTS
                flat = both.rearrange("p t e -> p (t e)")
                nc.tensor.matmul(ps[:, 7, 0:n], before[:, :], flat, start=True, stop=False)
                for t in range(1, CHUNK):
                    nc.tensor.matmul(ps[:, 7, EXPERTS * t:n], ones[:, :], flat[:, 0:n - EXPERTS * t], start=False, stop=False)
                nc.tensor.matmul(ps[:, 7, 0:n], ones[:, :], seen_bf[:, :].unsqueeze(1).to_broadcast([P, CHUNK, EXPERTS]),
                                 start=False, stop=True).then_inc(rank_ps, 1)

            def second_columns(i):
                pe.wait_ge(second_ready, CHUNK * (i + 1))
                free = ((sg_read, 2 * i), (sg_read, 2 * i)) if i else ((q2_ready, NG + 1), (q2_ready, NG + 1))
                turn_rows(CP + CHUNK * i, free, x2_ps)

            def second_queries(i):
                pe.wait_ge(x2_ready, NG + 2 * (i + 1))
                for m in range(KC):
                    for k in range(KC):
                        last = nc.tensor.matmul(ps[:, 6 + m, :], xwq_sb[:, k, P * m:P * (m + 1)], x2_t[:, k, :],
                                                start=(k == 0), stop=(k == KC - 1))
                    last.then_inc(q2_ps, 1)

            for ch in range(NT // CHUNK):
                b, i = divmod(ch, 2)
                n = NG * ch
                if i == 0:
                    if ch == 2:
                        turn2(n - 1)
                        pe.wait_ge(q2_ready, NG + 2 * KC + 1)
                    head_bounds(1 + b)
                    with needed(nc.tensor, pe, 1 + b):
                        pe.wait_ge(dve_att, 2 * B * NG + 1)
                        if b == 1:
                            pe.wait_ge(o2_div, 2 * NG)
                        for t in range(CP):
                            if t >= 1:
                                pe.wait_ge(max2_read[b], t)
                            for hg in range(NG):
                                last = nc.tensor.matmul(ps[:, hg, 0:HG * CTX], q2_t[b][:, hg // 2, P * t:P * (t + 1)],
                                                        k2_pad[:, b, HG * hg:HG * (hg + 1), 0:CTX], start=True, stop=True)
                            last.then_inc(max2_ps[b], 1)
                        pe.wait_ge(max2_done[b], 1)
                        turn_maxima(row_max2, CP, max2_tr[b])
                        pe.wait_ge(shift2_out[b], 48)
                scores2(ch, 0, 0)
                if ch % 2 == 1:
                    turn2(n - 1)
                if ch >= 2:
                    ranks(ch - 2)
                scores2(ch, 0, 1)
                if ch >= 1:
                    outputs(ch - 1)
                scores2(ch, 1, 0)
                if ch >= 1:
                    add_product(ch - 1)
                scores2(ch, 1, 1)
                values2(n)
                scores2(ch, 2, 0)
                turn2(n)
                scores2(ch, 2, 1)
                values2(n + 1)
                scores2(ch, 3, 0)
                if ch >= 1:
                    rows3(ch - 1)
                turn2(n + 1)
                scores2(ch, 3, 1)
                if ch >= 1:
                    gates(ch - 1)
                values2(n + 2)
                if ch >= 1:
                    shared(ch - 1, 0)
                turn2(n + 2)
                if ch >= 1:
                    shared(ch - 1, 1)
                if b == 0:
                    second_columns(i)
                values2(n + 3)
                if b == 0:
                    second_queries(i)
            turn2(NG * 4 - 1)
            ranks(2)
            outputs(3)
            add_product(3)
            rows3(3)
            gates(3)
            shared(3, 0)
            shared(3, 1)
            ranks(3)
            pe.wait_ge(sg_read, 8)
            nc.tensor.matmul(ps[:, 6, 0:EXPERTS], ones[:, :], seen_bf[:, :], start=True, stop=False)
            for t in range(CHUNK):
                last = nc.tensor.matmul(ps[:, 6, 0:EXPERTS], ones[:, :], both[:, t, :], start=False, stop=(t == CHUNK - 1))
            last.then_inc(count_ps, 1)

            def turn_tile(buf, n, ready=None):
                pe.wait_ge(xs_landed[buf], n)
                if ready is not None:
                    pe.wait_ge(xs_ready, ready)
                for k in range(KC):
                    last = nc.tensor.transpose(ps[:, 7, P * k:P * (k + 1)], xs_in[:, buf, P * k:P * (k + 1)], ident[:, :])
                last.then_inc(xs_ps, 1)

            def layer1(j, buf, ready, summed=None):
                e = nc.tensor.value_load(tile_expert[0:1, bass.ds(j, 1)], min_val=0, max_val=EXPERTS - 1)
                pe.wait_ge(xs_ready, ready)
                if summed is not None:
                    pe.wait_ge(h_sum, summed)
                for half in range(2):
                    for k in range(KC):
                        last = nc.tensor.matmul(ps[:, half, :], xs_t[:, buf, k, :],
                                                w1_sb[:, bass.ds(e, 1), k, 512 * half:512 * (half + 1)].squeeze(1),
                                                start=(k == 0), stop=(k == KC - 1))
                last.then_inc(h_ps, 1)

            def turn_hidden(n):
                pe.wait_ge(h_act, n)
                for k in range(HID // P):
                    last = nc.tensor.transpose(ps[:, 4 + k // 4, P * (k % 4):P * (k % 4 + 1)], hid[:, P * k:P * (k + 1)], ident[:, :])
                last.then_inc(ht_ps, 1)

            def layer2(j, n, taken=None):
                e = nc.tensor.value_load(tile_expert[0:1, bass.ds(j, 1)], min_val=0, max_val=EXPERTS - 1)
                pe.wait_ge(w2_in, e * 16 + 16)
                pe.wait_ge(ht_ready, n)
                if taken is not None:
                    pe.wait_ge(y_ready, taken)
                for k in range(HID // P):
                    last = nc.tensor.matmul(ps[:, 6, 0:D], hid_t[:, k, :], w2_sb[:, bass.ds(e, 1), k, :].squeeze(1),
                                            start=(k == 0), stop=(k == HID // P - 1))
                last.then_inc(y_ps, 1)

            pe.wait_ge(w1_in, 16 * EXPERTS)
            turn_tile(0, 16)
            layer1(0, 0, 1)
            turn_tile(1, 16, 1)
            turn_hidden(1)
            layer1(1, 1, 2, 1)
            turn_tile(0, 32, 2)
            layer2(0, 1)
            def round_pe(i):
                for o in range(2):
                    turn_hidden(2 * i + (o + 2))
                    layer1(2 * i + (o + 2), o, 2 * i + (o + 3), 2 * i + (o + 2))
                    turn_tile(1 - o, 16 * i + (32 + 16 * o), 2 * i + (3 + o))
                    layer2(2 * i + (o + 1), 2 * i + (o + 2), 2 * i + (o + 1))

            with pe.Fori(0, SURE) as i:
                round_pe(i)
            for i in range(SURE, PAIRS):
                may_run(nc.tensor, pe, i, round_pe, lambda i: (
                    (xs_ps, 2 * i + 3, 2), (h_ps, 2 * i + 2, 2), (ht_ps, 2 * i + 1, 2), (y_ps, 2 * i + 1, 2)))
            final = nc.tensor.value_load(last_tile[0:1, 0:1], min_val=2 * SURE + 2, max_val=SLOT_TILES - 1)
            turn_hidden(SLOT_TILES - 1)
            layer1(final, 0, SLOT_TILES, SLOT_TILES - 1)
            layer2(final - 1, SLOT_TILES - 1, SLOT_TILES - 2)
            turn_hidden(SLOT_TILES)
            layer2(final, SLOT_TILES, SLOT_TILES - 1)


_INS = ["x", "ctx_1024", "mask_BxSxS2_ik1", "L0_attn_Wq", "L0_attn_Wk", "L0_attn_Wv", "L0_attn_rel_table",
        "L0_attn_gamma", "L0_attn_beta", "L0_xattn_Wq", "L0_xattn_Wk", "L0_xattn_Wv", "L0_xattn_Wu", "L0_xattn_bu",
        "L0_ffn_W1", "L0_ffn_b1", "L0_ffn_W2", "L0_ffn_b2", "L0_ffn_gate_W", "L0_ffn_shared_W", "L0_ffn_shared_b",
        "L0_ffn_gamma", "L0_ffn_beta"]


def constants():
    bf16 = mybir.dt.np(BF16)
    p = np.arange(P)
    e = np.arange(EXPERTS)
    c = {"ident": np.eye(P, dtype=np.float32), "ident_bf": np.eye(P).astype(bf16)}
    pick = np.zeros((CTX + 1 + 3 * H, H, CTX + 1))
    pick[:CTX + 1] = np.eye(CTX + 1)[:, None, :]
    for n in range(3):
        for h in range(H):
            pick[CTX + 1 + H * n + h, h, :CTX] = 1
    c["pick"] = pick.astype(bf16)
    c["head_rows"] = (p[:, None] // DH == np.arange(8)[None, :]).astype(np.float32)
    c["counts"] = np.r_[np.ones(CTX), CTX].astype(np.float32)[:, None].repeat(2, 1)
    c["before"] = (p[:, None] < p[None, :]).astype(bf16)
    c["ones"] = np.ones((P, P)).astype(bf16)
    thresholds = np.tile(P * np.arange(NT), (EXPERTS, 1))
    tiles = np.tile(np.arange(SLOT_TILES)[:, None], (1, EXPERTS))
    row = np.concatenate([thresholds.ravel(), EXPERTS - e, (e[None, :] < e[:, None]).ravel(), REGION_TILES * P * e, tiles.ravel()])
    c["route_c"] = np.tile(row.astype(np.float32), (P, 1))
    return c


def kernel(**inputs):
    import concourse.bacc as bacc
    from concourse.bass_utils import run_bass_kernel_spmd

    nc = bacc.Bacc("TRN2", target_bir_lowering=False, num_devices=1)
    arrays, args = {}, []

    def give(name, a):
        a = np.ascontiguousarray(a)
        arrays[name] = a
        return nc.dram_tensor(name, a.shape, mybir.dt.from_np(a.dtype), kind="ExternalInput").ap()

    for name in _INS:
        a = np.asarray(inputs[name])
        if name == "L0_attn_rel_table":
            a = a[::-1].T
        if name in ("L0_xattn_Wq", "L0_xattn_Wk", "L0_xattn_Wv"):
            a = a.transpose(1, 0, 2).reshape(D, D)
        args.append(give("in_" + name, a))
    consts = {k: give("const_" + k, v) for k, v in constants().items()}
    out = nc.dram_tensor("out_0_dram", (B, S, D), F32, kind="ExternalOutput").ap()
    decoder_layer(nc, *args, consts, out)
    r = run_bass_kernel_spmd(nc, [arrays], core_ids=[0])
    return r.results[0]["out_0_dram"]
```
